# Optimizing a Trainium2 kernel written in Bass

```python
import numpy as np
import jax
import jax.numpy as jnp

def _softmax(x, axis=-1):
    return jax.nn.softmax(x, axis=axis)

def _gelu(x):
    return jax.nn.gelu(x, approximate=True)

def _silu(x):
    return jax.nn.silu(x)

def _sigmoid(x):
    return jax.nn.sigmoid(x)

def _layernorm(x, axis=-1, eps=1e-05):
    m = jnp.mean(x, axis=axis, keepdims=True)
    v = jnp.var(x, axis=axis, keepdims=True)
    return (x - m) / jnp.sqrt(v + eps)

def _scatter_add(tgt, idx, src, axis=0):
    return tgt.at[idx].add(src)

def _segment_sum(src, seg, n):
    return jax.ops.segment_sum(src, seg, n)
kernel_name = 'mk_adaln_d2_jaxref_r8_55efad'

def setup_inputs(seed: int=0):
    np.random.seed(seed)
    _w = jnp.asarray

    def _L0_attn_setup():
        import jax, jax.numpy as jnp
        import numpy as np
        B, S, D, H = (2, 256, 128, 16)
        HD = D // H
        FF = 512
        NUM_ITERS = 8
        DT = 0.1
        LN_EPS = 1e-05

        def _ln(x, g, b):
            m = jnp.mean(x, axis=-1, keepdims=True)
            v = jnp.var(x, axis=-1, keepdims=True)
            return (x - m) * jax.lax.rsqrt(v + LN_EPS) * g + b

        def _forward(x, qkv_w, qkv_b, out_w, out_b, g_attn, b_attn, g1, b1, g2, b2, w_ctx, w_x, b_inl, ff_w1, ff_b1, ff_w2, ff_b2):
            b, s, d = x.shape
            xn = _ln(x, g_attn, b_attn)
            qkv = (xn @ qkv_w + qkv_b).reshape(b, s, 3, H, HD)
            qkv = jnp.transpose(qkv, (2, 0, 3, 1, 4))
            q, k, v = (qkv[0], qkv[1], qkv[2])
            scores = jnp.einsum('bhqd,bhkd->bhqk', q, k) / np.sqrt(HD).astype(np.float32)
            causal = jnp.triu(jnp.ones((s, s), dtype=bool), 1)
            scores = jnp.where(causal[None, None], -jnp.inf, scores)
            attn_w = jax.nn.softmax(scores, axis=-1)
            attn = jnp.einsum('bhqk,bhkd->bhqd', attn_w, v)
            attn = jnp.transpose(attn, (0, 2, 1, 3)).reshape(b, s, d)
            attn = attn @ out_w + out_b
            x = x + attn
            ctx = attn.reshape(b * s, d)
            xs = _ln(x, g1, b1).reshape(b * s, d)
            vs = jnp.zeros_like(xs)

            def step(carry, _):
                xs, vs = carry
                u = jnp.tanh(ctx @ w_ctx + xs @ w_x + b_inl)
                vn = vs + DT * (u - xs - vs)
                xn_ = xs + DT * vn
                return ((xn_, vn), None)
            (xs, vs), _ = jax.lax.scan(step, (xs, vs), None, length=NUM_ITERS)
            x = x + xs.reshape(b, s, d)
            h = _ln(x, g2, b2)
            h = jax.nn.gelu(h @ ff_w1 + ff_b1, approximate=False)
            x = x + (h @ ff_w2 + ff_b2)
            return x
        key = jax.random.key(seed)
        ks = jax.random.split(key, 16)

        def xav(k, shape):
            lim = np.sqrt(6.0 / (shape[0] + shape[1]))
            return jax.random.uniform(k, shape, minval=-lim, maxval=lim, dtype=jnp.float32)
        return {'x': jax.random.normal(ks[0], (B, S, D), dtype=jnp.float32), 'qkv_w': xav(ks[1], (D, 3 * D)), 'qkv_b': jnp.zeros((3 * D,), jnp.float32), 'out_w': xav(ks[2], (D, D)), 'out_b': jnp.zeros((D,), jnp.float32), 'g_attn': jnp.ones((D,), jnp.float32), 'b_attn': jnp.zeros((D,), jnp.float32), 'g1': jnp.ones((D,), jnp.float32), 'b1': jnp.zeros((D,), jnp.float32), 'g2': jnp.ones((D,), jnp.float32), 'b2': jnp.zeros((D,), jnp.float32), 'w_ctx': xav(ks[3], (D, D)), 'w_x': xav(ks[4], (D, D)), 'b_inl': jnp.zeros((D,), jnp.float32), 'ff_w1': xav(ks[5], (D, FF)), 'ff_b1': jnp.zeros((FF,), jnp.float32), 'ff_w2': xav(ks[6], (FF, D)), 'ff_b2': jnp.zeros((D,), jnp.float32)}
    _L0_attn_in = _L0_attn_setup()

    def _L0_ffn_setup():
        import jax, jax.numpy as jnp
        import numpy as np
        D = 128
        HD = 128
        EA = 8
        KA = 2
        EF = 16
        KF = 2
        FH = 64
        MAXP = 64
        B, S = (4, 128)
        EPS = 1e-05

        def _layer_norm(x, w, b):
            mu = x.mean(-1, keepdims=True)
            var = ((x - mu) ** 2).mean(-1, keepdims=True)
            return (x - mu) * jax.lax.rsqrt(var + EPS) * w + b

        def _topk_gates(logits, k):
            top_vals, top_idx = jax.lax.top_k(logits, k)
            g = jax.nn.softmax(top_vals, axis=-1)
            onehot = jax.nn.one_hot(top_idx, logits.shape[-1], dtype=logits.dtype)
            return jnp.einsum('...k,...ke->...e', g, onehot)

        def _moa(x, gate_w, q_w, q_b, k_w, k_b, v_w, v_b, o_w, o_b, rel_table):
            S_ = x.shape[1]
            gates = _topk_gates(x @ gate_w, KA)
            q = (jnp.einsum('bsd,edh->bseh', x, q_w) + q_b) * HD ** (-0.5)
            k = x @ k_w + k_b
            v = x @ v_w + v_b
            scores = jnp.einsum('bqeh,bkh->beqk', q, k)
            rel_s = jnp.einsum('bqeh,rh->beqr', q, rel_table)
            pos = jnp.arange(S_)
            rel_idx = jnp.clip(pos[None, :] - pos[:, None], -MAXP, MAXP) + MAXP
            scores = scores + jnp.take_along_axis(rel_s, rel_idx[None, None], axis=-1)
            p = jax.nn.softmax(scores, axis=-1)
            ctx = jnp.einsum('beqk,bkh->bqeh', p, v)
            out = jnp.einsum('bqeh,ehd,bqe->bqd', ctx, o_w, gates)
            return out + jnp.einsum('bqe,ed->bqd', gates, o_b)

        def _moe_ffn(x, gate_w, w1, b1, w2, b2):
            gates = _topk_gates(x @ gate_w, KF)
            h = jax.nn.relu(jnp.einsum('bsd,edh->bseh', x, w1) + b1)
            out = jnp.einsum('bseh,ehd,bse->bsd', h, w2, gates)
            return out + jnp.einsum('bse,ed->bsd', gates, b2)
        key = jax.random.key(seed)
        ks = jax.random.split(key, 12)
        r = lambda i, shape, scale=0.02: jax.random.normal(ks[i], shape, jnp.float32) * scale
        return {'src': jax.random.normal(ks[0], (B, S, D), jnp.float32), 'ln1_w': jnp.ones((D,), jnp.float32), 'ln1_b': jnp.zeros((D,), jnp.float32), 'ln2_w': jnp.ones((D,), jnp.float32), 'ln2_b': jnp.zeros((D,), jnp.float32), 'attn_gate_w': r(1, (D, EA)), 'q_w': r(2, (EA, D, HD)), 'q_b': jnp.zeros((EA, HD), jnp.float32), 'k_w': r(3, (D, HD)), 'k_b': jnp.zeros((HD,), jnp.float32), 'v_w': r(4, (D, HD)), 'v_b': jnp.zeros((HD,), jnp.float32), 'o_w': r(5, (EA, HD, D)), 'o_b': jnp.zeros((EA, D), jnp.float32), 'rel_table': r(6, (2 * MAXP + 1, HD)), 'ff_gate_w': r(7, (D, EF)), 'ff_w1': r(8, (EF, D, FH)), 'ff_b1': jnp.zeros((EF, FH), jnp.float32), 'ff_w2': r(9, (EF, FH, D)), 'ff_b2': jnp.zeros((EF, D), jnp.float32)}
    _L0_ffn_in = _L0_ffn_setup()
    _L0_c = _w((lambda *s: np.random.randn(*s).astype(np.float32) * 0.05)(1, 128))
    _L0_wmod = _w((lambda *s: np.random.randn(*s).astype(np.float32) * 0.05)(128, 6 * 128) * 128 ** (-0.5))

    def _L1_attn_setup():
        import jax, jax.numpy as jnp
        import numpy as np
        N_HEADS = 16

        def _alibi_causal_mask(T, n_heads, dtype):
            slopes = (1.0 / jnp.power(2.0, jnp.arange(1, n_heads + 1, dtype=dtype)))[:, None, None]
            idx = jnp.arange(T)
            rel = (idx[None, :] - idx[:, None]).astype(dtype)
            alibi = jnp.tril(rel)
            causal = jnp.where(idx[None, :] > idx[:, None], -jnp.inf, 0.0).astype(dtype)
            return (alibi + causal)[None, :, :] * slopes
        key = jax.random.key(seed)
        ks = jax.random.split(key, 5)
        B, T, C = (2, 256, 128)
        scale = 0.02
        return {'x': jax.random.normal(ks[0], (B, T, C), dtype=jnp.float32), 'W_attn': jax.random.normal(ks[1], (C, 3 * C), dtype=jnp.float32) * scale, 'b_attn': jax.random.normal(ks[2], (3 * C,), dtype=jnp.float32) * scale, 'W_proj': jax.random.normal(ks[3], (C, C), dtype=jnp.float32) * scale, 'b_proj': jax.random.normal(ks[4], (C,), dtype=jnp.float32) * scale}
    _L1_attn_in = _L1_attn_setup()

    def _L1_ffn_setup():
        import jax, jax.numpy as jnp
        import numpy as np
        E = 8
        TOPK = 2
        D = 128
        F = 512
        B, S = (2, 64)

        def _gmm(x, W, expert_onehot):
            return jnp.einsum('te,td,edf->tf', expert_onehot, x, W)
        key = jax.random.key(seed)
        k1, k2, k3, k4, k5 = jax.random.split(key, 5)
        scale_d = 1.0 / np.sqrt(D)
        scale_f = 1.0 / np.sqrt(F)
        return {'inputs': jax.random.normal(k1, (B, S, D), jnp.float32), 'gate_kernel': jax.random.normal(k2, (D, E), jnp.float32) * scale_d, 'w0': jax.random.normal(k3, (E, D, F), jnp.float32) * scale_d, 'w1': jax.random.normal(k4, (E, D, F), jnp.float32) * scale_d, 'wo': jax.random.normal(k5, (E, F, D), jnp.float32) * scale_f}
    _L1_ffn_in = _L1_ffn_setup()
    _L1_c = _w((lambda *s: np.random.randn(*s).astype(np.float32) * 0.05)(1, 128))
    _L1_wmod = _w((lambda *s: np.random.randn(*s).astype(np.float32) * 0.05)(128, 6 * 128) * 128 ** (-0.5))
    _d = {'L0_attn_x': _L0_attn_in['x'], 'L0_attn_qkv_w': _L0_attn_in['qkv_w'], 'L0_attn_qkv_b': _L0_attn_in['qkv_b'], 'L0_attn_out_w': _L0_attn_in['out_w'], 'L0_attn_out_b': _L0_attn_in['out_b'], 'L0_attn_g_attn': _L0_attn_in['g_attn'], 'L0_attn_b_attn': _L0_attn_in['b_attn'], 'L0_attn_g1': _L0_attn_in['g1'], 'L0_attn_b1': _L0_attn_in['b1'], 'L0_attn_g2': _L0_attn_in['g2'], 'L0_attn_b2': _L0_attn_in['b2'], 'L0_attn_w_ctx': _L0_attn_in['w_ctx'], 'L0_attn_w_x': _L0_attn_in['w_x'], 'L0_attn_b_inl': _L0_attn_in['b_inl'], 'L0_attn_ff_w1': _L0_attn_in['ff_w1'], 'L0_attn_ff_b1': _L0_attn_in['ff_b1'], 'L0_attn_ff_w2': _L0_attn_in['ff_w2'], 'L0_attn_ff_b2': _L0_attn_in['ff_b2'], 'L0_ffn_ln1_w': _L0_ffn_in['ln1_w'], 'L0_ffn_ln1_b': _L0_ffn_in['ln1_b'], 'L0_ffn_ln2_w': _L0_ffn_in['ln2_w'], 'L0_ffn_ln2_b': _L0_ffn_in['ln2_b'], 'L0_ffn_attn_gate_w': _L0_ffn_in['attn_gate_w'], 'L0_ffn_q_w': _L0_ffn_in['q_w'], 'L0_ffn_q_b': _L0_ffn_in['q_b'], 'L0_ffn_k_w': _L0_ffn_in['k_w'], 'L0_ffn_k_b': _L0_ffn_in['k_b'], 'L0_ffn_v_w': _L0_ffn_in['v_w'], 'L0_ffn_v_b': _L0_ffn_in['v_b'], 'L0_ffn_o_w': _L0_ffn_in['o_w'], 'L0_ffn_o_b': _L0_ffn_in['o_b'], 'L0_ffn_rel_table': _L0_ffn_in['rel_table'], 'L0_ffn_ff_gate_w': _L0_ffn_in['ff_gate_w'], 'L0_ffn_ff_w1': _L0_ffn_in['ff_w1'], 'L0_ffn_ff_b1': _L0_ffn_in['ff_b1'], 'L0_ffn_ff_w2': _L0_ffn_in['ff_w2'], 'L0_ffn_ff_b2': _L0_ffn_in['ff_b2'], 'L0_c': _L0_c, 'L0_wmod': _L0_wmod, 'L1_attn_W_attn': _L1_attn_in['W_attn'], 'L1_attn_b_attn': _L1_attn_in['b_attn'], 'L1_attn_W_proj': _L1_attn_in['W_proj'], 'L1_attn_b_proj': _L1_attn_in['b_proj'], 'L1_ffn_gate_kernel': _L1_ffn_in['gate_kernel'], 'L1_ffn_w0': _L1_ffn_in['w0'], 'L1_ffn_w1': _L1_ffn_in['w1'], 'L1_ffn_wo': _L1_ffn_in['wo'], 'L1_c': _L1_c, 'L1_wmod': _L1_wmod}
    _x0 = _d['L0_attn_x']
    _d['L0_attn_x'] = jax.random.normal(jax.random.fold_in(jax.random.key(seed), 1), (1, 2048, 128), dtype=_x0.dtype)
    del _x0
    return _d

def reference(L0_attn_x, L0_attn_qkv_w, L0_attn_qkv_b, L0_attn_out_w, L0_attn_out_b, L0_attn_g_attn, L0_attn_b_attn, L0_attn_g1, L0_attn_b1, L0_attn_g2, L0_attn_b2, L0_attn_w_ctx, L0_attn_w_x, L0_attn_b_inl, L0_attn_ff_w1, L0_attn_ff_b1, L0_attn_ff_w2, L0_attn_ff_b2, L0_ffn_ln1_w, L0_ffn_ln1_b, L0_ffn_ln2_w, L0_ffn_ln2_b, L0_ffn_attn_gate_w, L0_ffn_q_w, L0_ffn_q_b, L0_ffn_k_w, L0_ffn_k_b, L0_ffn_v_w, L0_ffn_v_b, L0_ffn_o_w, L0_ffn_o_b, L0_ffn_rel_table, L0_ffn_ff_gate_w, L0_ffn_ff_w1, L0_ffn_ff_b1, L0_ffn_ff_w2, L0_ffn_ff_b2, L0_c, L0_wmod, L1_attn_W_attn, L1_attn_b_attn, L1_attn_W_proj, L1_attn_b_proj, L1_ffn_gate_kernel, L1_ffn_w0, L1_ffn_w1, L1_ffn_wo, L1_c, L1_wmod):

    def _L0_attn_ref(x, qkv_w, qkv_b, out_w, out_b, g_attn, b_attn, g1, b1, g2, b2, w_ctx, w_x, b_inl, ff_w1, ff_b1, ff_w2, ff_b2):
        import jax, jax.numpy as jnp
        import numpy as np
        B, S, D, H = (2, 256, 128, 16)
        HD = D // H
        FF = 512
        NUM_ITERS = 8
        DT = 0.1
        LN_EPS = 1e-05

        def _ln(x, g, b):
            m = jnp.mean(x, axis=-1, keepdims=True)
            v = jnp.var(x, axis=-1, keepdims=True)
            return (x - m) * jax.lax.rsqrt(v + LN_EPS) * g + b

        def _forward(x, qkv_w, qkv_b, out_w, out_b, g_attn, b_attn, g1, b1, g2, b2, w_ctx, w_x, b_inl, ff_w1, ff_b1, ff_w2, ff_b2):
            b, s, d = x.shape
            xn = _ln(x, g_attn, b_attn)
            qkv = (xn @ qkv_w + qkv_b).reshape(b, s, 3, H, HD)
            qkv = jnp.transpose(qkv, (2, 0, 3, 1, 4))
            q, k, v = (qkv[0], qkv[1], qkv[2])
            scores = jnp.einsum('bhqd,bhkd->bhqk', q, k) / np.sqrt(HD).astype(np.float32)
            causal = jnp.triu(jnp.ones((s, s), dtype=bool), 1)
            scores = jnp.where(causal[None, None], -jnp.inf, scores)
            attn_w = jax.nn.softmax(scores, axis=-1)
            attn = jnp.einsum('bhqk,bhkd->bhqd', attn_w, v)
            attn = jnp.transpose(attn, (0, 2, 1, 3)).reshape(b, s, d)
            attn = attn @ out_w + out_b
            x = x + attn
            ctx = attn.reshape(b * s, d)
            xs = _ln(x, g1, b1).reshape(b * s, d)
            vs = jnp.zeros_like(xs)

            def step(carry, _):
                xs, vs = carry
                u = jnp.tanh(ctx @ w_ctx + xs @ w_x + b_inl)
                vn = vs + DT * (u - xs - vs)
                xn_ = xs + DT * vn
                return ((xn_, vn), None)
            (xs, vs), _ = jax.lax.scan(step, (xs, vs), None, length=NUM_ITERS)
            x = x + xs.reshape(b, s, d)
            h = _ln(x, g2, b2)
            h = jax.nn.gelu(h @ ff_w1 + ff_b1, approximate=False)
            x = x + (h @ ff_w2 + ff_b2)
            return x
        return _forward(x, qkv_w, qkv_b, out_w, out_b, g_attn, b_attn, g1, b1, g2, b2, w_ctx, w_x, b_inl, ff_w1, ff_b1, ff_w2, ff_b2)

    def _L0_ffn_ref(src, ln1_w, ln1_b, ln2_w, ln2_b, attn_gate_w, q_w, q_b, k_w, k_b, v_w, v_b, o_w, o_b, rel_table, ff_gate_w, ff_w1, ff_b1, ff_w2, ff_b2):
        import jax, jax.numpy as jnp
        import numpy as np
        D = 128
        HD = 128
        EA = 8
        KA = 2
        EF = 16
        KF = 2
        FH = 64
        MAXP = 64
        B, S = (4, 128)
        EPS = 1e-05

        def _layer_norm(x, w, b):
            mu = x.mean(-1, keepdims=True)
            var = ((x - mu) ** 2).mean(-1, keepdims=True)
            return (x - mu) * jax.lax.rsqrt(var + EPS) * w + b

        def _topk_gates(logits, k):
            top_vals, top_idx = jax.lax.top_k(logits, k)
            g = jax.nn.softmax(top_vals, axis=-1)
            onehot = jax.nn.one_hot(top_idx, logits.shape[-1], dtype=logits.dtype)
            return jnp.einsum('...k,...ke->...e', g, onehot)

        def _moa(x, gate_w, q_w, q_b, k_w, k_b, v_w, v_b, o_w, o_b, rel_table):
            S_ = x.shape[1]
            gates = _topk_gates(x @ gate_w, KA)
            q = (jnp.einsum('bsd,edh->bseh', x, q_w) + q_b) * HD ** (-0.5)
            k = x @ k_w + k_b
            v = x @ v_w + v_b
            scores = jnp.einsum('bqeh,bkh->beqk', q, k)
            rel_s = jnp.einsum('bqeh,rh->beqr', q, rel_table)
            pos = jnp.arange(S_)
            rel_idx = jnp.clip(pos[None, :] - pos[:, None], -MAXP, MAXP) + MAXP
            scores = scores + jnp.take_along_axis(rel_s, rel_idx[None, None], axis=-1)
            p = jax.nn.softmax(scores, axis=-1)
            ctx = jnp.einsum('beqk,bkh->bqeh', p, v)
            out = jnp.einsum('bqeh,ehd,bqe->bqd', ctx, o_w, gates)
            return out + jnp.einsum('bqe,ed->bqd', gates, o_b)

        def _moe_ffn(x, gate_w, w1, b1, w2, b2):
            gates = _topk_gates(x @ gate_w, KF)
            h = jax.nn.relu(jnp.einsum('bsd,edh->bseh', x, w1) + b1)
            out = jnp.einsum('bseh,ehd,bse->bsd', h, w2, gates)
            return out + jnp.einsum('bse,ed->bsd', gates, b2)
        res = src
        xn = _layer_norm(src, ln1_w, ln1_b)
        x = res + _moa(xn, attn_gate_w, q_w, q_b, k_w, k_b, v_w, v_b, o_w, o_b, rel_table)
        res = x
        xn = _layer_norm(x, ln2_w, ln2_b)
        return res + _moe_ffn(xn, ff_gate_w, ff_w1, ff_b1, ff_w2, ff_b2)

    def _L1_attn_ref(x, W_attn, b_attn, W_proj, b_proj):
        import jax, jax.numpy as jnp
        import numpy as np
        N_HEADS = 16

        def _alibi_causal_mask(T, n_heads, dtype):
            slopes = (1.0 / jnp.power(2.0, jnp.arange(1, n_heads + 1, dtype=dtype)))[:, None, None]
            idx = jnp.arange(T)
            rel = (idx[None, :] - idx[:, None]).astype(dtype)
            alibi = jnp.tril(rel)
            causal = jnp.where(idx[None, :] > idx[:, None], -jnp.inf, 0.0).astype(dtype)
            return (alibi + causal)[None, :, :] * slopes
        B, T, C = x.shape
        H = N_HEADS
        D = C // H
        qkv = x @ W_attn + b_attn
        q, k, v = jnp.split(qkv, 3, axis=-1)
        q = q.reshape(B, T, H, D).transpose(0, 2, 1, 3)
        k = k.reshape(B, T, H, D).transpose(0, 2, 1, 3)
        v = v.reshape(B, T, H, D).transpose(0, 2, 1, 3)
        att = jnp.einsum('bhtd,bhsd->bhts', q, k) / jnp.sqrt(jnp.asarray(D, x.dtype))
        att = att + _alibi_causal_mask(T, H, x.dtype)[None]
        att = jax.nn.softmax(att, axis=-1)
        y = jnp.einsum('bhts,bhsd->bhtd', att, v)
        y = y.transpose(0, 2, 1, 3).reshape(B, T, C)
        return y @ W_proj + b_proj

    def _L1_ffn_ref(inputs, gate_kernel, w0, w1, wo):
        import jax, jax.numpy as jnp
        import numpy as np
        E = 8
        TOPK = 2
        D = 128
        F = 512
        B, S = (2, 64)

        def _gmm(x, W, expert_onehot):
            return jnp.einsum('te,td,edf->tf', expert_onehot, x, W)
        dtype = inputs.dtype
        gate_logits = jnp.einsum('bsd,de->bse', inputs, gate_kernel)
        weights, selected_experts = jax.lax.top_k(gate_logits, TOPK)
        weights = jax.nn.softmax(weights.astype(jnp.float32), axis=-1).astype(dtype)
        inputs_2d = jnp.reshape(inputs, (-1, D))
        flat_sel = jnp.ravel(selected_experts)
        sort_idx = jnp.argsort(flat_sel)
        rep = jnp.repeat(inputs_2d, TOPK, axis=0)
        sorted_hidden = jnp.take(rep, sort_idx, axis=0)
        T = flat_sel.shape[0]
        group_sizes = jnp.zeros((E,), jnp.int32).at[flat_sel].add(1)
        expert_ids = jnp.repeat(jnp.arange(E), group_sizes, total_repeat_length=T)
        onehot = jax.nn.one_hot(expert_ids, E, dtype=dtype)
        layer_1 = _gmm(sorted_hidden, w0, onehot)
        layer_2 = _gmm(sorted_hidden, w1, onehot)
        intermediate = jax.nn.silu(layer_1) * layer_2
        layer_3 = _gmm(intermediate, wo, onehot)
        unsort = jnp.take(layer_3, jnp.argsort(sort_idx), axis=0)
        combined = unsort * jnp.ravel(weights)[:, None]
        out = jnp.sum(combined.reshape(-1, TOPK, D), axis=1)
        return out.reshape(inputs.shape).astype(dtype)
    x = L0_attn_x
    mod = (_silu(L0_c) @ L0_wmod).reshape(L0_c.shape[0], 6, 1, -1)
    sa, ca, ga, sb, cb, gb = (mod[:, 0], mod[:, 1], mod[:, 2], mod[:, 3], mod[:, 4], mod[:, 5])
    ga = (2 * (ga >= 0) - 1) * jnp.maximum(jnp.abs(ga), 0.25)
    gb = (2 * (gb >= 0) - 1) * jnp.maximum(jnp.abs(gb), 0.25)
    h = _layernorm(x, axis=-1) * (1 + ca) + sa
    x = x + ga * _L0_attn_ref(h, L0_attn_qkv_w, L0_attn_qkv_b, L0_attn_out_w, L0_attn_out_b, L0_attn_g_attn, L0_attn_b_attn, L0_attn_g1, L0_attn_b1, L0_attn_g2, L0_attn_b2, L0_attn_w_ctx, L0_attn_w_x, L0_attn_b_inl, L0_attn_ff_w1, L0_attn_ff_b1, L0_attn_ff_w2, L0_attn_ff_b2)
    h = _layernorm(x, axis=-1) * (1 + cb) + sb
    x = x + gb * _L0_ffn_ref(h, L0_ffn_ln1_w, L0_ffn_ln1_b, L0_ffn_ln2_w, L0_ffn_ln2_b, L0_ffn_attn_gate_w, L0_ffn_q_w, L0_ffn_q_b, L0_ffn_k_w, L0_ffn_k_b, L0_ffn_v_w, L0_ffn_v_b, L0_ffn_o_w, L0_ffn_o_b, L0_ffn_rel_table, L0_ffn_ff_gate_w, L0_ffn_ff_w1, L0_ffn_ff_b1, L0_ffn_ff_w2, L0_ffn_ff_b2)
    mod = (_silu(L1_c) @ L1_wmod).reshape(L1_c.shape[0], 6, 1, -1)
    sa, ca, ga, sb, cb, gb = (mod[:, 0], mod[:, 1], mod[:, 2], mod[:, 3], mod[:, 4], mod[:, 5])
    ga = (2 * (ga >= 0) - 1) * jnp.maximum(jnp.abs(ga), 0.25)
    gb = (2 * (gb >= 0) - 1) * jnp.maximum(jnp.abs(gb), 0.25)
    h = _layernorm(x, axis=-1) * (1 + ca) + sa
    x = x + ga * _L1_attn_ref(h, L1_attn_W_attn, L1_attn_b_attn, L1_attn_W_proj, L1_attn_b_proj)
    h = _layernorm(x, axis=-1) * (1 + cb) + sb
    x = x + gb * _L1_ffn_ref(h, L1_ffn_gate_kernel, L1_ffn_w0, L1_ffn_w1, L1_ffn_wo)
    return x

_drawn_inputs = setup_inputs


def setup_inputs(seed=0):
    import zlib

    import numpy as np

    out = dict(_drawn_inputs(seed))
    spreads = {'L0_attn_qkv_b': (0.0, 0.1),
     'L0_attn_out_b': (0.0, 0.1),
     'L0_attn_g_attn': (1.0, 0.6),
     'L0_attn_b_attn': (0.0, 0.1),
     'L0_attn_g1': (1.0, 0.2),
     'L0_attn_b1': (0.0, 0.375),
     'L0_attn_g2': (1.0, 0.565),
     'L0_attn_b2': (0.0, 0.55),
     'L0_attn_b_inl': (0.0, 0.8),
     'L0_attn_ff_b1': (0.0, 0.366),
     'L0_attn_ff_b2': (0.0, 0.344),
     'L0_ffn_ln1_w': (1.0, 0.6),
     'L0_ffn_ln1_b': (0.0, 0.8),
     'L0_ffn_ln2_w': (1.0, 0.6),
     'L0_ffn_ln2_b': (0.0, 0.8),
     'L0_ffn_q_b': (0.0, 0.8),
     'L0_ffn_k_b': (0.0, 0.8),
     'L0_ffn_v_b': (0.0, 0.8),
     'L0_ffn_o_b': (0.0, 0.415),
     'L0_ffn_ff_b1': (0.0, 0.8),
     'L0_ffn_ff_b2': (0.0, 0.419)}
    factors = {'L0_attn_w_ctx': 5.075,
     'L0_ffn_attn_gate_w': 3.251,
     'L0_ffn_q_w': 8.0,
     'L0_ffn_k_w': 8.0,
     'L0_ffn_v_w': 8.0,
     'L0_ffn_o_w': 8.0,
     'L0_ffn_rel_table': 8.0,
     'L0_ffn_ff_gate_w': 3.22,
     'L0_ffn_ff_w1': 8.0,
     'L0_ffn_ff_w2': 8.0,
     'L1_attn_W_attn': 8.0,
     'L1_attn_b_attn': 8.0,
     'L1_attn_W_proj': 8.0,
     'L1_attn_b_proj': 8.0}
    for name, (base, spread) in spreads.items():
        noise = np.random.default_rng([zlib.crc32(name.encode()), seed]).standard_normal(out[name].shape)
        drawn = base * np.exp(spread * noise) if base else spread * noise
        out[name] = jnp.asarray(drawn.astype(out[name].dtype))
    for name, factor in factors.items():
        out[name] = (out[name] * factor).astype(out[name].dtype)
    return out
```

```python
from contextlib import ExitStack

import numpy as np

import concourse.bass as bass
from concourse import mybir

F32 = mybir.dt.float32
BF16 = mybir.dt.bfloat16
U32 = mybir.dt.uint32
ALU = mybir.AluOpType
ACT = mybir.ActivationFunctionType
AX = mybir.AxisListType


def cleared_semaphores(nc, ctx, tag):
    taken = []

    def make(name):
        taken.append(nc.alloc_semaphore(name=tag + name))
        return taken[-1]

    ctx.callback(nc.all_engine_barrier)
    ctx.callback(nc.clear_and_free_semaphores, taken)
    return make

P=128; S=2048; H=16; HD=8; QB=512; NT=S//P
GROUPS_Q="hhmmhl"; GROUPS_K="hmhmlh"
NROW=48; CROWS=16; MROW=52
NEG=-3.0e38

def pieces():
    return [(i,k,min(QB,P*(i+1)-k)) for i in range(NT) for k in range(0,P*(i+1),QB)]
PIECES=pieces()
N_PIECE=len(PIECES)
A_TILES=12
A_LAST=sum(1 for i,_,_ in PIECES if i<A_TILES)
def slot_items(first):
    out=[]
    for n in range(N_PIECE):
        if n==6 and not first: out.append(("turn_b",None))
        if n==A_LAST+6: out.append(("turn_a",None))
        out.append(("piece",n))
    return out
N_ITEM=N_PIECE+2
P1_BANKS=3
def item_count(n,k):
    return k if isinstance(n,int) and n==0 else n*N_ITEM-1+k
def item_bank(first,k): return (k if first else k+N_ITEM-1)%P1_BANKS
def groups():
    out=[]
    for c in range(S//QB):
        for j in range(0,4*c+4,2):
            out.append((c,[(t,max(0,P*(t-4*c))) for t in (j,j+1)]))
    return out
GROUPS=groups(); N_GROUP=len(GROUPS)
N_PAIR=N_GROUP//2
PAIRS_DONE=[sum(c+1 for c in range(b+1)) for b in range(4)]
def group_cols(g):
    (_, ts)=GROUPS[g]
    w=[QB-f for _,f in ts]
    return [0,w[0]], w, sum(w)

def attention(nc, tag, q_rows, k_rows, q_const, k_const, v_all, ident, mask_q, mask_k, o_dram):
    with ExitStack() as ctx:
        sb=lambda n,s,d: ctx.enter_context(nc.sbuf_tensor(tag+n,s,d))
        sem=cleared_semaphores(nc, ctx, tag)
        ps=lambda n,s,d: ctx.enter_context(nc.psum_tensor(tag+n,s,d))
        qb=sb("qb",[P,3,S],BF16); kb=sb("kb",[P,3,S],BF16)
        vb=sb("vb",[P,3,NT,32],F32)
        probs=sb("probs",[P,4,2*QB],F32)
        o_sb=sb("o_sb",[P,3,S],F32)
        pmax=sb("pmax",[P,NT,4],F32)
        negmax=sb("negmax",[P,NT],F32)
        nothing=sb("nothing",[P,A_TILES],F32)
        split_a=sb("split_a",[P,2,A_TILES],BF16); split_b=sb("split_b",[P,2,NT-A_TILES],BF16)
        turned_a=sb("turned_a",[2*A_TILES,P],BF16); turned_b=sb("turned_b",[2*(NT-A_TILES),P],BF16)
        p1=ps("p1",[P,P1_BANKS,QB],F32)
        s2=ps("s2",[P,2,2*QB],F32)
        acc=ps("acc",[P,QB],F32)
        s_load=[sem(f"heads_loaded{i}") for i in range(3)]
        s_zero=sem("buffers_zeroed"); s_pmax=sem("pmax_set"); s_item=sem("p1_filled"); s_free=sem("p1_read")
        s_nm=sem("negmax_ready"); s_split=sem("negmax_split") 
        s_ma=sem("max_rows_a"); s_mb=sem("max_rows_b")
        s_scores=sem("scores_ready"); s_exp=sem("probs_ready"); s_pv=sem("pv_done"); s_evac=sem("out_copied")
        s_out=sem("out_stored"); s_v=sem("v_ready")
        block=ctx.enter_context(nc.Block())
        A=A_TILES; B=NT-A_TILES
        BIAS=2
        def turned(n,part):
            if part=="b": return item_count_next(n,6 if not (isinstance(n,int) and n==H-1) else 0)+1
            first=isinstance(n,int) and n==0
            return item_count(n,[k for k,_ in slot_items(first)].index("turn_a"))+1
        def item_count_next(n,k): return (n+1)*N_ITEM-1+k
        def last_pair(n): return BIAS+(n+1)*N_PAIR

        @block.sync
        def _(sp):
            def load(n,u):
                for dst,rows,const in ((kb,k_rows,k_const),(qb,q_rows,q_const)):
                    sp.dma_start(dst[0:NROW,u,:],rows[bass.ds(n,1)].rearrange("o r s -> (o r) s")).then_inc(s_load[u],16)
                    sp.dma_start(dst[NROW:NROW+CROWS,u,:],const(n)).then_inc(s_load[u],16)
            def max_rows(n,u,part):
                t0,t1,src,s_m=(0,A,turned_a,s_ma) if part=="a" else (A,NT,turned_b,s_mb)
                sp.wait_ge(s_free,turned(n,part))
                for j in range(2):
                    sp.dma_start(qb[MROW+j:MROW+j+1,u,t0*P:t1*P],
                                 src[j*(t1-t0):(j+1)*(t1-t0),:]).then_inc(s_m,16)
            def store(n,u):
                sp.wait_ge(s_evac,1+4*n+4)
                for g in range(4):
                    sp.dma_start(o_dram[bass.ds(n,1),g,:,:].rearrange("o r s -> (o r) s"),
                                 o_sb[32*g:32*g+9,u,:]).then_inc(s_out,16)
            def slot(n,u):
                max_rows(n-1,(u+2)%3,"b")
                store(n-2,(u+1)%3)
                sp.wait_ge(s_out,64*(n-1))
                load(n+1,(u+1)%3)
                max_rows(n,u,"a")
            load(0,0); load(1,1)
            sp.wait_ge(s_zero,5)
            max_rows(0,0,"a")
            load(2,2)
            max_rows(0,0,"b")
            max_rows(1,1,"a")
            slot(2,2)
            with sp.Fori(1,(H-1)//3) as it:
                for j in range(3): slot(it*3+j,j)
            max_rows(H-2,2,"b")
            store(H-3,1)
            max_rows(H-1,0,"a")
            max_rows(H-1,0,"b")
            store(H-2,2); store(H-1,0)
            sp.wait_ge(s_out,64*H)

        @block.gpsimd
        def _(pool):
            def split(n,part):
                t0,t1,dst,w=(0,A,split_a,2*n+1) if part=="a" else (A,NT,split_b,2*n+2)
                pool.wait_ge(s_nm,w)
                if not(isinstance(n,int) and n==0): pool.wait_ge(s_free,turned(n-1,part))
                pool.tensor_tensor(dst[:,0,:],negmax[:,t0:t1],nothing[:,0:t1-t0],ALU.add).then_inc(s_split,1)
                pool.wait_ge(s_split,2*w-1)
                pool.tensor_tensor(dst[:,1,:],negmax[:,t0:t1],dst[:,0,:],ALU.subtract).then_inc(s_split,1)
            def v_copy(n,u):
                pool.wait_ge(s_zero,5)
                if not(isinstance(n,int) and n<3): pool.wait_ge(s_pv,last_pair(n-3))
                pool.tensor_copy(vb[:,u,:,0:HD],v_all[:,:,bass.ds(n*HD,HD)]).then_inc(s_v,1)
            pool.memset(nothing[:],0.0).then_inc(s_zero,1)
            pool.wait_ge(s_zero,1)
            pool.memset(qb[64:128,:,:],0.0).then_inc(s_zero,1)
            pool.wait_ge(s_zero,2)
            pool.memset(kb[64:128,:,:],0.0).then_inc(s_zero,1)
            pool.wait_ge(s_zero,3)
            pool.memset(vb[:],0.0).then_inc(s_zero,1)
            pool.wait_ge(s_zero,4)
            pool.memset(vb[:,:,:,HD:HD+1],1.0).then_inc(s_zero,1)
            pool.wait_ge(s_zero,5)
            pool.memset(o_sb[:,:,0:QB],0.0).then_inc(s_zero,1)
            pool.wait_ge(s_zero,6)
            def slot(n,u):
                v_copy(n,u)
                split(n,"a"); split(n,"b")
            slot(0,0); slot(1,1); slot(2,2)
            with pool.Fori(1,(H-1)//3) as it:
                for j in range(3): slot(it*3+j,j)
            slot(H-1,0)

        @block.vector
        def _(dve):
            dve.memset(pmax[:],NEG).then_inc(s_pmax,1)
            dve.wait_ge(s_pmax,1)
            def items(n,first=False):
                for k,(kind,x) in enumerate(slot_items(first)):
                    at=item_count(n,k); bank=item_bank(first,k)
                    if kind=="piece":
                        i,k0,w=PIECES[x]
                        dve.wait_ge(s_item,at+1)
                        dve.tensor_reduce(pmax[:,i,k0//QB:k0//QB+1],p1[:,bank,0:w],AX.X,ALU.max).then_inc(s_free,1)
                        if x==A_LAST-1: negate(n,"a",at)
                        if x==N_PIECE-1: negate(n,"b",at)
                    elif kind=="turn_a": copy_turned(n,"a",bank,at)
                    else: copy_turned(n-1,"b",bank,at)
            def copy_turned(n,part,bank,at):
                dst,w=(turned_a,2*A) if part=="a" else (turned_b,2*B)
                dve.wait_ge(s_item,at+1)
                dve.tensor_copy(dst[:,:],p1[:,bank,:].bitcast(BF16)[0:w,0:P]).then_inc(s_free,1)
            def negate(n,part,at):
                t0,t1=(0,A) if part=="a" else (A,NT)
                dve.wait_ge(s_free,at+1)
                if not(isinstance(n,int) and n==0): dve.wait_ge(s_split,4*n)
                dve.tensor_reduce(negmax[:,t0:t1],pmax[:,t0:t1,:],AX.X,ALU.max,negate=True).then_inc(s_nm,1)
            items(0,True)
            with dve.Fori(0,(H-1)//3) as it:
                for j in range(3): items(it*3+(1+j))
            copy_turned(H-1,"b",item_bank(False,0),item_count(H,0))

        @block.scalar
        def _(act):
            act.sem_inc(s_exp,BIAS)
            act.sem_inc(s_evac,1)
            act.wait_ge(s_zero,6)
            def exp(m,g):
                _,_,w=group_cols(g)
                act.wait_ge(s_scores,m*N_GROUP+g+1)
                act.wait_ge(s_pv,BIAS+m*N_PAIR+g//2-1)
                act.activation(probs[:,g%4,0:w],s2[:,g%2,0:w],ACT.Exp).then_inc(s_exp,1)
            def evac(m,u,c):
                act.wait_ge(s_pv,BIAS+m*N_PAIR+PAIRS_DONE[c])
                r=32 if c==0 else P
                act.activation(o_sb[0:r,u,QB*c:QB*c+QB],acc[0:r,:],ACT.Copy).then_inc(s_evac,1)
            def body(m,u,more=True):
                for g in range(1,N_GROUP):
                    exp(m,g)
                    if g//2 in PAIRS_DONE and g%2==0: evac(m,u,PAIRS_DONE.index(g//2))
                if more: exp(m+1,0)
                evac(m,u,3)
            exp(0,0)
            with act.Fori(0,(H-1)//3) as it:
                for j in range(3): body(it*3+j,j)
            body(H-1,0,False)

        @block.tensor
        def _(pe):
            pe.sem_inc(s_pv,BIAS)
            def item(n,u,k,kind,x,first):
                at=item_count(n,k); bank=item_bank(first,k)
                if not(first and k<P1_BANKS): pe.wait_ge(s_free,at+1-P1_BANKS)
                if kind=="piece":
                    i,k0,w=PIECES[x]
                    diagonal=k0+w==P*(i+1)
                    mm=pe.matmul(p1[:,bank,0:w],qb[:,u,i*P:(i+1)*P],kb[:,u,k0:k0+w],start=True,stop=True)
                    if diagonal: mm=pe.matmul(p1[:,bank,w-P:w],ident[:,:],mask_q[:,:],start=False,stop=True,skip_group_check=True)
                    mm.then_inc(s_item,1)
                elif kind=="turn_a": turn(n,"a",bank)
                else: turn(n-1,"b",bank)
            def turn(n,part,bank):
                src,w,t=(split_a,2*A,4*n+2) if part=="a" else (split_b,2*B,4*n+4)
                pe.wait_ge(s_split,t)
                pe.transpose(p1[:,bank,:].bitcast(BF16)[0:w,0:P],src[:,:,:].rearrange("p a t -> p (a t)"),ident[:,:]).then_inc(s_item,1)
            def scores(m,u,g):
                c,ts=GROUPS[g]
                at,w,_=group_cols(g)
                if g==0: pe.wait_ge(s_ma,32*m+32)
                if c==3 and GROUPS[g-1][0]==2: pe.wait_ge(s_mb,32*m+32)
                pe.wait_ge(s_exp,BIAS+m*N_GROUP+g-1)
                for (t,f),a,n in zip(ts,at,w):
                    diagonal=t>=4*c
                    mm=pe.matmul(s2[:,g%2,a:a+n],kb[:,u,t*P:(t+1)*P],qb[:,u,c*QB+f:(c+1)*QB],start=True,stop=True)
                    if diagonal: mm=pe.matmul(s2[:,g%2,a:a+P],ident[:,:],mask_k[:,:],start=False,stop=True,skip_group_check=True)
                mm.then_inc(s_scores,1)
            def pv(m,u,p):
                c=GROUPS[2*p][0]
                first=p==0 or GROUPS[2*p-1][0]!=c
                if p==0: pe.wait_ge(s_v,m+1)
                pe.wait_ge(s_exp,BIAS+m*N_GROUP+2*p+2)
                if first: pe.wait_ge(s_evac,1+4*m+c)
                for g in (2*p,2*p+1):
                    at,w,_=group_cols(g)
                    for j,(t,f) in enumerate(GROUPS[g][1]):
                        strip=0 if c==0 else 32*(t%4)
                        st=(t==0 if c==0 else t<4); last=(t==3 if c==0 else t>=4*c)
                        mm=pe.matmul(acc[strip:strip+32,f:QB],vb[:,u,t,:],probs[:,g%4,at[j]:at[j]+w[j]],
                                     start=st,stop=last,skip_group_check=True)
                mm.then_inc(s_pv,1)
            def body(m,u,more=True,items=None):
                un=(u+1)%3
                todo=[]
                if more: todo=[(m+1,un,k,kind,x) for k,(kind,x) in enumerate(slot_items(False))]
                for s in range(2,N_GROUP+2):
                    if s<N_GROUP: scores(m,u,s)
                    elif more: scores(m+1,un,s-N_GROUP)
                    if s%2: pv(m,u,(s-3)//2)
                    if s==2 and not more: last_turn()
                    for _ in range(2 + (s<4) if s<N_GROUP+1 else len(todo)):
                        if todo: item(*todo.pop(0),False)
            def last_turn():
                k=item_count(H,0)
                pe.wait_ge(s_free,k+1-P1_BANKS)
                turn(H-1,"b",item_bank(False,0))
            for u in range(1): pe.wait_ge(s_load[u],64)
            pe.wait_ge(s_zero,5)
            for k,(kind,x) in enumerate(slot_items(True)): item(0,0,k,kind,x,True)
            scores(0,0,0); scores(0,0,1)
            with pe.Fori(0,(H-1)//3) as it:
                for j in range(3):
                    pe.wait_ge(s_load[(j+1)%3],it*64+64*((j+1)//3+1))
                    body(it*3+j,j)
            body(H-1,0,False)


NB = S // QB
D = P
EPS = 1e-5


def layer_norms(nc, tag, c, norms):
    with ExitStack() as ctx:
        sb = lambda n, s: ctx.enter_context(nc.sbuf_tensor(tag + n, s, F32))
        ps = lambda n, s: ctx.enter_context(nc.psum_tensor(tag + n, s, F32))
        sem = cleared_semaphores(nc, ctx, tag)
        centred = sb("centred", [P, 4, QB])
        squares = sb("squares", [P, 2, QB])
        deviation = sb("deviation", [P, 2, 4])
        rstd = sb("rstd", [P, 2, 4])
        diagonal = sb("diagonal", [P, 2, QB])
        scaled = sb("scaled", [P, 2, QB])
        mean_ps = ps("mean_ps", [P, 2, QB])
        var_ps = ps("var_ps", [P, 2, QB])
        bcast_ps = ps("bcast_ps", [P, 2, QB])
        s_mean = sem("mean_ready"); s_cent = sem("centred"); s_sq = sem("squared"); s_var = sem("var_ready")
        s_dev = sem("deviation_ready"); s_rstd = sem("rstd_ready"); s_diag = sem("diagonal_ready")
        s_bc = sem("rstd_broadcast"); s_mul = sem("scaled"); s_out = sem("normed")
        n_all = NB * len(norms)
        at = lambda i: (norms[i // NB], slice(i % NB * QB, (i % NB + 1) * QB))
        block = ctx.enter_context(nc.Block())

        @block.tensor
        def _(pe):
            for t in range(n_all + 2):
                if t < n_all:
                    i = t
                    (src, _, _, _), cols = at(i)
                    if i >= NB: pe.wait_ge(s_out, i - NB + 1)
                    if i >= 2: pe.wait_ge(s_cent, i - 1)
                    pe.matmul(mean_ps[:, i % 2, :], c.averages[:, :], src[:, cols], start=True, stop=True).then_inc(s_mean, 1)
                if 1 <= t <= n_all:
                    i = t - 1
                    pe.wait_ge(s_sq, i + 1)
                    if i >= 2: pe.wait_ge(s_dev, i - 1)
                    for k in range(4):
                        mm = pe.matmul(var_ps[:, i % 2, k:k + 1], squares[:, i % 2, k * P:(k + 1) * P],
                                       c.averages[:, 0:1], start=True, stop=True)
                    mm.then_inc(s_var, 1)
                if t >= 2:
                    i = t - 2
                    pe.wait_ge(s_diag, i + 1)
                    if i >= 2: pe.wait_ge(s_mul, i - 1)
                    pe.matmul(bcast_ps[:, i % 2, :], c.ones[:, :], diagonal[:, i % 2, :], start=True, stop=True).then_inc(s_bc, 1)

        @block.vector
        def _(dve):
            for t in range(n_all + 2):
                if t < n_all:
                    i = t
                    (src, _, _, _), cols = at(i)
                    dve.wait_ge(s_mean, i + 1)
                    if i >= 4: dve.wait_ge(s_sq, i - 3)
                    dve.tensor_tensor(centred[:, i % 4, :], src[:, cols], mean_ps[:, i % 2, :], ALU.subtract).then_inc(s_cent, 1)
                if 1 <= t <= n_all:
                    i = t - 1
                    dve.wait_ge(s_dev, i + 1)
                    dve.reciprocal(rstd[:, i % 2, :], deviation[:, i % 2, :]).then_inc(s_rstd, 1)
                    dve.wait_ge(s_rstd, i + 1)
                    if i >= 2: dve.wait_ge(s_bc, i - 1)
                    for k in range(4):
                        ins = dve.tensor_scalar(diagonal[:, i % 2, k * P:(k + 1) * P], c.ident[:, :],
                                                rstd[:, i % 2, k:k + 1], None, ALU.mult)
                    ins.then_inc(s_diag, 1)
                if t >= 2:
                    i = t - 2
                    dve.wait_ge(s_bc, i + 1)
                    if i >= 2: dve.wait_ge(s_out, i - 1)
                    dve.tensor_tensor(scaled[:, i % 2, :], centred[:, i % 4, :], bcast_ps[:, i % 2, :], ALU.mult).then_inc(s_mul, 1)

        @block.scalar
        def _(act):
            for t in range(n_all + 2):
                if t < n_all:
                    i = t
                    act.wait_ge(s_cent, i + 1)
                    if i >= 2: act.wait_ge(s_var, i - 1)
                    act.activation(squares[:, i % 2, :], centred[:, i % 4, :], ACT.Square).then_inc(s_sq, 1)
                if 1 <= t <= n_all:
                    i = t - 1
                    act.wait_ge(s_var, i + 1)
                    act.activation(deviation[:, i % 2, :], var_ps[:, i % 2, 0:4], ACT.Sqrt, bias=c.eps).then_inc(s_dev, 1)
                if t >= 2:
                    i = t - 2
                    (_, dst, scale, bias), cols = at(i)
                    act.wait_ge(s_mul, i + 1)
                    act.activation(dst[:, cols], scaled[:, i % 2, :], ACT.Identity, scale=scale, bias=bias).then_inc(s_out, 1)


def qkv(nc, tag, c, src, weights, q_bias, k_bias, v_all, q_rows, k_rows):
    with ExitStack() as ctx:
        sb = lambda n, s, d: ctx.enter_context(nc.sbuf_tensor(tag + n, s, d))
        sem = cleared_semaphores(nc, ctx, tag)
        full = sb("full", [P, 2, QB], F32)
        rest = sb("rest", [P, 2, QB], F32)
        parts = {k: sb("part_" + k, [P, 2, S], BF16) for k in "hml"}
        qk_ps = ctx.enter_context(nc.psum_tensor(tag + "qk_ps", [P, 2, QB], F32))
        v_ps = ctx.enter_context(nc.psum_tensor(tag + "v_ps", [P, 2, QB], F32))
        s_qk = sem("qk_ready"); s_full = sem("full_ready"); s_high = sem("high_ready"); s_rest = sem("rest_ready")
        s_mid = sem("mid_ready"); s_low = sem("low_ready"); s_v = sem("v_ready"); s_vcopy = sem("v_copied"); s_store = sem("rows_stored")
        units = [(w, b) for w in range(2) for b in range(NB)]
        block = ctx.enter_context(nc.Block())

        @block.tensor
        def _(pe):
            for i, (w, b) in enumerate(units):
                if i >= 2: pe.wait_ge(s_full, i - 1)
                pe.matmul(qk_ps[:, i % 2, :], weights[:, w * D:(w + 1) * D], src[:, b * QB:(b + 1) * QB],
                          start=True, stop=True).then_inc(s_qk, 1)
                if i % 2:
                    v = i // 2
                    if v >= 2: pe.wait_ge(s_vcopy, v - 1)
                    for k in range(4):
                        t = 4 * v + k
                        mm = pe.matmul(v_ps[:, v % 2, k * D:(k + 1) * D], src[:, t * P:(t + 1) * P],
                                       weights[:, 2 * D:3 * D], start=True, stop=True)
                    mm.then_inc(s_v, 1)

        @block.vector
        def _(dve):
            for i, (w, b) in enumerate(units):
                dve.wait_ge(s_qk, i + 1)
                if i >= 2: dve.wait_ge(s_rest, i - 1)
                dve.tensor_scalar(full[:, i % 2, :], qk_ps[:, i % 2, :], q_bias if w == 0 else k_bias,
                                  HD ** -0.5 if w == 0 else 1.0, ALU.add, ALU.mult).then_inc(s_full, 1)
                dve.wait_ge(s_high, i + 1)
                if i >= 2: dve.wait_ge(s_low, i - 1)
                dve.tensor_tensor(rest[:, i % 2, :], full[:, i % 2, :], parts["h"][:, w, b * QB:(b + 1) * QB],
                                  ALU.subtract).then_inc(s_rest, 1)

        @block.scalar
        def _(act):
            for i, (w, b) in enumerate(units):
                cols = slice(b * QB, (b + 1) * QB)
                act.wait_ge(s_full, i + 1)
                act.activation(parts["h"][:, w, cols], full[:, i % 2, :], ACT.Copy).then_inc(s_high, 1)
                if i % 2:
                    v = i // 2
                    act.wait_ge(s_v, v + 1)
                    act.activation(v_all[:, 4 * v:4 * v + 4, :], v_ps[:, v % 2, :].rearrange("p (t d) -> p t d", t=4),
                                   ACT.Copy).then_inc(s_vcopy, 1)
                act.wait_ge(s_rest, i + 1)
                act.activation(parts["m"][:, w, cols], rest[:, i % 2, :], ACT.Copy).then_inc(s_mid, 1)

        @block.gpsimd
        def _(pool):
            for i, (w, b) in enumerate(units):
                cols = slice(b * QB, (b + 1) * QB)
                pool.wait_ge(s_mid, i + 1)
                if i: pool.wait_ge(s_low, i)
                pool.tensor_tensor(parts["l"][:, w, cols], rest[:, i % 2, :], parts["m"][:, w, cols],
                                   ALU.subtract).then_inc(s_low, 1)

        @block.sync
        def _(sp):
            for w, (rows, groups) in enumerate(((q_rows, GROUPS_Q), (k_rows, GROUPS_K))):
                for kind, s in (("h", s_high), ("m", s_mid), ("l", s_low)):
                    sp.wait_ge(s, NB * (w + 1))
                    for g, part in enumerate(groups):
                        if part == kind:
                            sp.dma_start(rows[:, g * HD:(g + 1) * HD, :], parts[kind][:, w, :]).then_inc(s_store, 16)
            sp.wait_ge(s_store, 16 * 12)


def attention_out(nc, tag, c, o_dram, rden_dram, weights, v_bias, out_bias, ctx_out, gain, base, dst):
    with ExitStack() as ctx:
        sb = lambda n, s, d=F32: ctx.enter_context(nc.sbuf_tensor(tag + n, s, d))
        sem = cleared_semaphores(nc, ctx, tag)
        strips = sb("strips", [P, 4, S])
        sums = sb("sums", [P, 4, S // 8])
        total = sb("total", [P, S // 8])
        inverse = sb("inverse", [P, S // 8])
        inverse_rows = sb("inverse_rows", [H, S])
        bias = sb("bias", [P, 1])
        bcast_ps = ctx.enter_context(nc.psum_tensor(tag + "bcast_ps", [P, 2, QB], F32))
        out_ps = ctx.enter_context(nc.psum_tensor(tag + "out_ps", [P, 2, QB], F32))
        bias_ps = ctx.enter_context(nc.psum_tensor(tag + "bias_ps", [P, QB], F32))
        s_sums = sem("sums_loaded"); s_strips = [sem(f"strips_loaded{i}") for i in range(4)]
        s_step = sem("sums_step"); s_inv = sem("inverse_stored"); s_rows = sem("inverse_rows_loaded")
        s_half = sem("half_summed"); s_add = sem("strips_summed"); s_bc = sem("inverse_broadcast"); s_norm = sem("divided")
        s_bias_ps = sem("bias_product"); s_bias = sem("bias_ready"); s_out = sem("projected"); s_ctx = sem("ctx_written"); s_dst = sem("dst_written")
        block = ctx.enter_context(nc.Block())

        @block.sync
        def _(sp):
            for g in range(4):
                sp.dma_start(sums[:, g, :], o_dram[:, g, HD, :].rearrange("h (e s) -> h e s", e=8)).then_inc(s_sums, 16)
            for g in range(4):
                sp.dma_start(strips[:, g, :], o_dram[:, g, 0:HD, :]).then_inc(s_strips[g], 16)
            sp.wait_ge(s_step, 4)
            sp.dma_start(rden_dram.rearrange("h (e s) -> (h e) s", e=8), inverse[:, :]).then_inc(s_inv, 16)
            sp.wait_ge(s_inv, 16)
            sp.dma_start(inverse_rows[:, :], rden_dram).then_inc(s_rows, 16)

        @block.gpsimd
        def _(pool):
            pool.wait_ge(s_strips[2], 16)
            pool.wait_ge(s_strips[3], 16)
            pool.tensor_tensor(strips[:, 2, :], strips[:, 2, :], strips[:, 3, :], ALU.add).then_inc(s_half, 1)

        @block.vector
        def _(dve):
            dve.wait_ge(s_sums, 64)
            dve.tensor_tensor(total[:, :], sums[:, 0, :], sums[:, 1, :], ALU.add).then_inc(s_step, 1)
            for g in (2, 3):
                dve.wait_ge(s_step, g - 1)
                dve.tensor_tensor(total[:, :], total[:, :], sums[:, g, :], ALU.add).then_inc(s_step, 1)
            dve.wait_ge(s_step, 3)
            dve.reciprocal(inverse[:, :], total[:, :]).then_inc(s_step, 1)
            dve.wait_ge(s_bias_ps, 1)
            dve.tensor_tensor(bias[:, :], bias_ps[:, 0:1], out_bias, ALU.add).then_inc(s_bias, 1)
            dve.wait_ge(s_strips[0], 16)
            dve.wait_ge(s_strips[1], 16)
            dve.tensor_tensor(strips[:, 0, :], strips[:, 0, :], strips[:, 1, :], ALU.add).then_inc(s_add, 1)
            dve.wait_ge(s_add, 1)
            dve.wait_ge(s_half, 1)
            dve.tensor_tensor(strips[:, 0, :], strips[:, 0, :], strips[:, 2, :], ALU.add).then_inc(s_add, 1)
            dve.wait_ge(s_add, 2)
            for b in range(NB + 1):
                if b < NB:
                    cols = slice(b * QB, (b + 1) * QB)
                    dve.wait_ge(s_bc, b + 1)
                    dve.tensor_tensor(strips[:, 1, cols], strips[:, 0, cols], bcast_ps[:, b % 2, :], ALU.mult).then_inc(s_norm, 1)
                if b:
                    cols = slice((b - 1) * QB, b * QB)
                    dve.wait_ge(s_ctx, b)
                    dve.scalar_tensor_tensor(out=dst[:, cols], in0=ctx_out[:, cols], scalar=gain, in1=base[:, cols],
                                             op0=ALU.mult, op1=ALU.add).then_inc(s_dst, 1)

        @block.scalar
        def _(act):
            act.wait_ge(s_bias, 1)
            for b in range(NB):
                act.wait_ge(s_out, b + 1)
                act.activation(ctx_out[:, b * QB:(b + 1) * QB], out_ps[:, b % 2, :], ACT.Identity, bias=bias[:, 0:1]).then_inc(s_ctx, 1)

        @block.tensor
        def _(pe):
            pe.matmul(bias_ps[:, 0:1], weights[:, :], v_bias, start=True, stop=True).then_inc(s_bias_ps, 1)
            pe.wait_ge(s_rows, 16)
            for b in range(NB + 1):
                if b < NB:
                    if b >= 2: pe.wait_ge(s_norm, b - 1)
                    pe.matmul(bcast_ps[:, b % 2, :], c.spread_heads[0:H, :], inverse_rows[:, b * QB:(b + 1) * QB],
                              start=True, stop=True).then_inc(s_bc, 1)
                if b:
                    pe.wait_ge(s_norm, b)
                    if b >= 3: pe.wait_ge(s_ctx, b - 2)
                    pe.matmul(out_ps[:, (b - 1) % 2, :], weights[:, :], strips[:, 1, (b - 1) * QB:b * QB],
                              start=True, stop=True).then_inc(s_out, 1)


def liquid(nc, tag, c, ctx_in, w_ctx, w_x, bias, xs, x2, dst):
    STEPS = 8
    with ExitStack() as ctx:
        sb = lambda n, s: ctx.enter_context(nc.sbuf_tensor(tag + n, s, F32))
        sem = cleared_semaphores(nc, ctx, tag)
        drive = sb("drive", [P, S])
        change = sb("change", [P, 2, QB])
        u_ps = ctx.enter_context(nc.psum_tensor(tag + "u_ps", [P, NB, QB], F32))
        v_ps = ctx.enter_context(nc.psum_tensor(tag + "v_ps", [P, NB, QB], F32))
        s_drive_ps = sem("drive_product"); s_drive = sem("drive_ready"); s_zero = sem("v_zeroed")
        s_pre = sem("before_tanh"); s_u = sem("u_ready"); s_change = sem("change_ready"); s_v = sem("v_ready"); s_xs = sem("xs_ready")
        block = ctx.enter_context(nc.Block())

        @block.tensor
        def _(pe):
            for b in range(NB):
                mm = pe.matmul(u_ps[:, b, :], w_ctx[:, :], ctx_in[:, b * QB:(b + 1) * QB], start=True, stop=True)
                mm.then_inc(s_drive_ps, 1)
            with pe.Fori(0, STEPS) as n:
                for b in range(NB):
                    cols = slice(b * QB, (b + 1) * QB)
                    pe.wait_ge(s_xs, n * NB + b + 1)
                    pe.matmul(u_ps[:, b, :], c.ident[:, :], drive[:, cols], start=True, stop=False)
                    pe.matmul(u_ps[:, b, :], w_x[:, :], xs[:, cols], start=False, stop=True).then_inc(s_pre, 1)

        @block.scalar
        def _(act):
            for b in range(NB):
                act.wait_ge(s_drive_ps, b + 1)
                act.activation(drive[:, b * QB:(b + 1) * QB], u_ps[:, b, :], ACT.Identity, bias=bias).then_inc(s_xs, 1)
            with act.Fori(0, STEPS) as n:
                for b in range(NB):
                    act.wait_ge(s_pre, n * NB + b + 1)
                    act.activation(u_ps[:, b, :], u_ps[:, b, :], ACT.Tanh).then_inc(s_u, 1)

        @block.vector
        def _(dve):
            dve.memset(v_ps[:, :, :], 0.0).then_inc(s_zero, 1)
            dve.wait_ge(s_zero, 1)
            with dve.Fori(0, STEPS) as n:
                for b in range(NB):
                    cols = slice(b * QB, (b + 1) * QB)
                    dve.wait_ge(s_u, n * NB + b + 1)
                    dve.tensor_tensor(change[:, b % 2, :], u_ps[:, b, :], xs[:, cols], ALU.subtract).then_inc(s_change, 1)
                    dve.wait_ge(s_change, n * NB + b + 1)
                    dve.scalar_tensor_tensor(out=v_ps[:, b, :], in0=v_ps[:, b, :], scalar=0.9, in1=change[:, b % 2, :],
                                             op0=ALU.mult, op1=ALU.add).then_inc(s_v, 1)
                    dve.wait_ge(s_v, n * NB + b + 1)
                    dve.scalar_tensor_tensor(out=xs[:, cols], in0=v_ps[:, b, :], scalar=0.01, in1=xs[:, cols],
                                             op0=ALU.mult, op1=ALU.add).then_inc(s_xs, 1)
            dve.wait_ge(s_xs, (STEPS + 1) * NB)
            dve.tensor_tensor(dst[:, :], x2[:, :], xs[:, :], ALU.add).then_inc(s_zero, 1)


def gelu_ffn(nc, tag, c, src, w1, b1, w2, b2, base, gain, x):
    F = 4
    with ExitStack() as ctx:
        sb = lambda n, s: ctx.enter_context(nc.sbuf_tensor(tag + n, s, F32))
        sem = cleared_semaphores(nc, ctx, tag)
        hidden = sb("hidden", [P, 2 * F, QB])
        total = sb("total", [P, 2, QB])
        h_ps = ctx.enter_context(nc.psum_tensor(tag + "h_ps", [P, F, QB], F32))
        o_ps = ctx.enter_context(nc.psum_tensor(tag + "o_ps", [P, 2, QB], F32))
        s_h = sem("h_ready"); s_g = sem("gelu_ready"); s_o = sem("o_ready"); s_total = sem("total_ready"); s_x = sem("x_ready")
        block = ctx.enter_context(nc.Block())

        @block.tensor
        def _(pe):
            for b in range(NB + 1):
                if b < NB:
                    for f in range(F):
                        if b: pe.wait_ge(s_g, F * (b - 1) + f + 1)
                        pe.matmul(h_ps[:, f, :], w1[:, f * P:(f + 1) * P], src[:, b * QB:(b + 1) * QB],
                                  start=True, stop=True).then_inc(s_h, 1)
                if b:
                    n = b - 1
                    if n >= 2: pe.wait_ge(s_total, n - 1)
                    pe.wait_ge(s_g, F * b)
                    for f in range(F):
                        mm = pe.matmul(o_ps[:, n % 2, :], w2[:, f, :], hidden[:, n % 2 * F + f, :],
                                       start=(f == 0), stop=(f == F - 1))
                    mm.then_inc(s_o, 1)

        @block.scalar
        def _(act):
            for b in range(NB):
                if b >= 2: act.wait_ge(s_o, b - 1)
                for f in range(F):
                    act.wait_ge(s_h, F * b + f + 1)
                    act.activation(hidden[:, b % 2 * F + f, :], h_ps[:, f, :], ACT.Gelu, bias=b1(f)).then_inc(s_g, 1)

        @block.vector
        def _(dve):
            for b in range(NB):
                cols = slice(b * QB, (b + 1) * QB)
                dve.wait_ge(s_o, b + 1)
                dve.scalar_tensor_tensor(out=total[:, b % 2, :], in0=o_ps[:, b % 2, :], scalar=b2, in1=base[:, cols],
                                         op0=ALU.add, op1=ALU.add).then_inc(s_total, 1)
                dve.wait_ge(s_total, b + 1)
                dve.scalar_tensor_tensor(out=x[:, cols], in0=total[:, b % 2, :], scalar=gain, in1=x[:, cols],
                                         op0=ALU.mult, op1=ALU.add).then_inc(s_x, 1)


def top2_gates(nc, tag, c, src, gate_w, n_experts, rows, rows_bf=None):
    E = n_experts
    R = rows.shape[0]
    chosen = rows_bf is not None
    with ExitStack() as ctx:
        sb = lambda n, s, d=F32: ctx.enter_context(nc.sbuf_tensor(tag + n, s, d))
        sem = cleared_semaphores(nc, ctx, tag)
        logits = sb("logits", [P, NT, E])
        best = sb("best", [P, NT, 8])
        index = sb("index", [P, NT, 8], U32)
        index_f = sb("index_f", [P, NT, 2])
        gap = sb("gap", [P, NT]); ratio = sb("ratio", [P, NT]); whole = sb("whole", [P, NT])
        gate = sb("gate", [P, NT, 2])
        hot = sb("hot", [P, 2, NT, E])
        weighed = sb("weighed", [P, 2, NT, E])
        token = sb("token", [P, NT, R])
        logit_ps = ctx.enter_context(nc.psum_tensor(tag + "logit_ps", [P, NT, E], F32))
        turn_ps = ctx.enter_context(nc.psum_tensor(tag + "turn_ps", [P, 2, QB], F32))
        s_logit = sem("logits_ready"); s_step = sem("step"); s_gap = sem("gap_ready"); s_ratio = sem("ratio_ready")
        s_token = sem("token_rows_ready"); s_turn = sem("turned"); s_rows = sem("rows_ready")
        block = ctx.enter_context(nc.Block())

        @block.tensor
        def _(pe):
            for t in range(NT):
                mm = pe.matmul(logit_ps[:, t, :], src[:, t * P:(t + 1) * P], gate_w, start=True, stop=True)
            mm.then_inc(s_logit, 1)
            pe.wait_ge(s_token, 1)
            for b in range(NB):
                if b >= 2: pe.wait_ge(s_rows, b - 1)
                for k in range(4):
                    mm = pe.transpose(turn_ps[0:R, b % 2, k * P:(k + 1) * P], token[:, 4 * b + k, :], c.ident[:, :])
                mm.then_inc(s_turn, 1)

        @block.scalar
        def _(act):
            act.wait_ge(s_gap, 1)
            act.activation(ratio[:, :], gap[:, :], ACT.Exp).then_inc(s_ratio, 1)
            for b in range(NB):
                act.wait_ge(s_turn, b + 1)
                if chosen: act.activation(rows_bf[:, b * QB:(b + 1) * QB], turn_ps[0:R, b % 2, :], ACT.Copy)
                act.activation(rows[:, b * QB:(b + 1) * QB], turn_ps[0:R, b % 2, :], ACT.Copy).then_inc(s_rows, 1)

        @block.vector
        def _(dve):
            done = [0]

            def link(ins):
                done[0] += 1
                ins.then_inc(s_step, 1)
                dve.wait_ge(s_step, done[0])

            dve.wait_ge(s_logit, 1)
            if R > E + (2 * E + 2 if chosen else 0):
                dve.memset(token[:, :, :], 0.0).then_inc(s_step, 1)
                done[0] += 1
            link(dve.tensor_copy(logits[:, :, :], logit_ps[:, :, :]))
            for t in range(NT):
                ins = dve.max(best[:, t, :], logits[:, t, :])
            link(ins)
            for t in range(NT):
                ins = dve.max_index(index[:, t, :], best[:, t, :], logits[:, t, :])
            link(ins)
            dve.tensor_tensor(gap[:, :], best[:, :, 1], best[:, :, 0], ALU.subtract).then_inc(s_gap, 1)
            link(dve.tensor_copy(index_f[:, :, :], index[:, :, 0:2]))
            for k in range(2):
                ins = dve.tensor_tensor(hot[:, k, :, :], c.counting[:, 0:E].unsqueeze(1).to_broadcast([P, NT, E]),
                                        index_f[:, :, k].unsqueeze(2).to_broadcast([P, NT, E]), ALU.is_equal)
            link(ins)
            dve.wait_ge(s_ratio, 1)
            link(dve.tensor_scalar(whole[:, :], ratio[:, :], 1.0, None, ALU.add))
            link(dve.reciprocal(gate[:, :, 0], whole[:, :]))
            link(dve.tensor_tensor(gate[:, :, 1], ratio[:, :], gate[:, :, 0], ALU.mult))
            for k in range(2):
                ins = dve.tensor_tensor(weighed[:, k, :, :], hot[:, k, :, :],
                                        gate[:, :, k].unsqueeze(2).to_broadcast([P, NT, E]), ALU.mult)
            link(ins)
            if chosen:
                for k in range(2):
                    dve.tensor_copy(token[:, :, E * (1 + k):E * (2 + k)], hot[:, k, :, :])
                dve.tensor_copy(token[:, :, 3 * E:3 * E + 2], gate[:, :, :])
            dve.tensor_tensor(token[:, :, 0:E], weighed[:, 0, :, :], weighed[:, 1, :, :], ALU.add).then_inc(s_token, 1)


EA = 8


def moa_keys(nc, tag, c, src, k_w, k_bias, v_w, rel, keys, values):
    with ExitStack() as ctx:
        sem = cleared_semaphores(nc, ctx, tag)
        k_ps = ctx.enter_context(nc.psum_tensor(tag + "k_ps", [P, 2, QB], F32))
        v_ps = ctx.enter_context(nc.psum_tensor(tag + "v_ps", [P, 2, QB], F32))
        s_k = sem("k_ready"); s_copy = sem("k_copied"); s_v = sem("v_ready"); s_vcopy = sem("v_copied"); s_side = sem("sides_ready")
        block = ctx.enter_context(nc.Block())

        @block.tensor
        def _(pe):
            for b in range(NB):
                if b >= 2: pe.wait_ge(s_copy, b - 1)
                pe.matmul(k_ps[:, b % 2, :], k_w, src[:, b * QB:(b + 1) * QB], start=True, stop=True).then_inc(s_k, 1)
                if b >= 2: pe.wait_ge(s_vcopy, b - 1)
                for k in range(4):
                    t = 4 * b + k
                    mm = pe.matmul(v_ps[:, b % 2, k * D:(k + 1) * D], src[:, t * P:(t + 1) * P], v_w, start=True, stop=True)
                mm.then_inc(s_v, 1)

        @block.scalar
        def _(act):
            for b in range(NB):
                act.wait_ge(s_k, b + 1)
                act.activation(keys[:, 1, b * QB:(b + 1) * QB], k_ps[:, b % 2, :], ACT.Identity, bias=k_bias).then_inc(s_copy, 1)
                act.wait_ge(s_v, b + 1)
                act.activation(values[:, 4 * b:4 * b + 4, :], v_ps[:, b % 2, :].rearrange("p (t d) -> p t d", t=4),
                               ACT.Copy).then_inc(s_vcopy, 1)

        @block.vector
        def _(dve):
            for b in range(NB):
                cols = slice(b * QB, (b + 1) * QB)
                dve.wait_ge(s_copy, b + 1)
                dve.tensor_scalar(keys[:, 0, cols], keys[:, 1, cols], rel[:, 0:1], None, ALU.add)
                dve.tensor_scalar(keys[:, 2, cols], keys[:, 1, cols], rel[:, 2 * P - 1:2 * P], None, ALU.add).then_inc(s_side, 1)


def moa_queries(nc, tag, c, src, q_w, q_bias, rows_bf, queries):
    with ExitStack() as ctx:
        sb = lambda n, s: ctx.enter_context(nc.sbuf_tensor(tag + n, s, F32))
        sem = cleared_semaphores(nc, ctx, tag)
        all_q = sb("all_q", [P, 2, QB])
        q_ps = ctx.enter_context(nc.psum_tensor(tag + "q_ps", [P, 2, QB], F32))
        mask_ps = ctx.enter_context(nc.psum_tensor(tag + "mask_ps", [P, 4, QB], F32))
        s_q = sem("q_ready"); s_copy = sem("q_copied"); s_mask = sem("masks_ready"); s_pick = sem("picked")
        units = [(b, e) for b in range(NB) for e in range(EA)]
        block = ctx.enter_context(nc.Block())

        @block.tensor
        def _(pe):
            for i, (b, e) in enumerate(units):
                cols = slice(b * QB, (b + 1) * QB)
                if i >= 2: pe.wait_ge(s_copy, i - 1)
                pe.matmul(q_ps[:, i % 2, :], q_w[:, e, :], src[:, cols], start=True, stop=True).then_inc(s_q, 1)
                if i >= 2: pe.wait_ge(s_pick, 2 * (i - 1))
                for k in range(2):
                    mm = pe.matmul(mask_ps[:, i % 2 * 2 + k, :], c.pick_bf[0:32, EA * (1 + k) + e, :], rows_bf[:, cols], start=True, stop=True)
                mm.then_inc(s_mask, 1)

        @block.scalar
        def _(act):
            for i, (b, e) in enumerate(units):
                act.wait_ge(s_q, i + 1)
                if i >= 2: act.wait_ge(s_pick, 2 * (i - 1))
                act.activation(all_q[:, i % 2, :], q_ps[:, i % 2, :], ACT.Identity, scale=float(D) ** -0.5, bias=q_bias(e)).then_inc(s_copy, 1)

        @block.vector
        def _(dve):
            for i, (b, e) in enumerate(units):
                cols = slice(b * QB, (b + 1) * QB)
                dve.wait_ge(s_copy, i + 1)
                dve.wait_ge(s_mask, i + 1)
                for k in range(2):
                    if e == 0:
                        dve.tensor_tensor(queries[:, k, cols], all_q[:, i % 2, :], mask_ps[:, i % 2 * 2 + k, :], ALU.mult).then_inc(s_pick, 1)
                    else:
                        if k == 0: dve.wait_ge(s_pick, 2 * i)
                        dve.copy_predicated(queries[:, k, cols], mask_ps[:, i % 2 * 2 + k, :].bitcast(U32), all_q[:, i % 2, :]).then_inc(s_pick, 1)


NEAR = 64
WINDOW = P + 2 * NEAR


def moa_near_bias(nc, tag, c, rel, queries, slot, near, band_dram):
    W = 2 * P
    with ExitStack() as ctx:
        sb = lambda n, s: ctx.enter_context(nc.sbuf_tensor(tag + n, s, F32))
        sem = cleared_semaphores(nc, ctx, tag)
        band = sb("band", [P, 2, 4, W])
        far = sb("far", [P, NT, 2])
        band_ps = ctx.enter_context(nc.psum_tensor(tag + "band_ps", [P, 4, QB], F32))
        s_band = sem("band_ready"); s_copy = sem("band_copied"); s_far = sem("far_copied"); s_store = [sem(f"band_stored{b}") for b in range(NB)]
        s_near = [sem(f"near_loaded{b}") for b in range(NB)]; s_zero = sem("corners_zeroed"); s_out = sem("near_ready")
        block = ctx.enter_context(nc.Block())

        @block.tensor
        def _(pe):
            for t in range(NT):
                if t >= 4: pe.wait_ge(s_copy, t - 3)
                pe.matmul(band_ps[:, t % 4, 0:W], queries[:, slot, t * P:(t + 1) * P], rel, start=True, stop=True).then_inc(s_band, 1)

        @block.scalar
        def _(act):
            for t in range(NT):
                act.wait_ge(s_band, t + 1)
                if t % 4 == 0 and t >= 8:
                    act.wait_ge(s_store[t // 4 - 2], 16)
                    act.wait_ge(s_far, t - 4)
                act.activation(band[:, t // 4 % 2, t % 4, :], band_ps[:, t % 4, 0:W], ACT.Copy).then_inc(s_copy, 1)

        @block.sync
        def _(sp):
            def load(b):
                sp.wait_ge(s_store[b], 16)
                for half in range(2):
                    at = 4 * b * P * W + ((W - 1) * NEAR + P if half else P - NEAR)
                    src = bass.AP(band_dram.tensor, at, [[W - 1, NEAR], [P * W, 4], [1, P + NEAR]])
                    sp.dma_start(near[NEAR * half:NEAR * (half + 1), 4 * b:4 * b + 4, NEAR * half:NEAR * half + P + NEAR], src).then_inc(s_near[b], 16)
            for b in range(NB):
                sp.wait_ge(s_copy, 4 * (b + 1))
                sp.dma_start(band_dram[4 * b:4 * b + 4].rearrange("t p w -> p t w"), band[:, b % 2, :, :]).then_inc(s_store[b], 16)
                if b: load(b - 1)
            load(NB - 1)

        @block.gpsimd
        def _(pool):
            pool.memset(near[0:NEAR, :, P + NEAR:WINDOW], 0.0).then_inc(s_zero, 1)
            pool.wait_ge(s_zero, 1)
            pool.memset(near[NEAR:P, :, 0:NEAR], 0.0).then_inc(s_zero, 1)
            pool.wait_ge(s_zero, 2)

        def side(dve, b):
            dve.wait_ge(s_far, 4 * b + 4)
            dve.wait_ge(s_near[b], 32)
            for t in range(4 * b, 4 * b + 4):
                for rows, cols, k in ((slice(0, NEAR), slice(0, NEAR), 0), (slice(NEAR, P), slice(P + NEAR, WINDOW), 1)):
                    dve.tensor_scalar(near[rows, t, cols], near[rows, t, cols], far[rows, t, k:k + 1], None, ALU.subtract).then_inc(s_out, 1)

        @block.vector
        def _(dve):
            for t in range(NT):
                dve.wait_ge(s_copy, t + 1)
                dve.tensor_copy(far[:, t, :], band[:, t // 4 % 2, t % 4, 0:W:W - 1]).then_inc(s_far, 1)
                if t >= 8 and t % 4 == 3: side(dve, t // 4 - 2)
            side(dve, NB - 2)
            side(dve, NB - 1)



def moa_attention(nc, tag, c, keys, values, queries, slot, near, rows, v_bias, out):
    NEGMAX_ROWS = 2
    with ExitStack() as ctx:
        sb = lambda n, s, d=F32: ctx.enter_context(nc.sbuf_tensor(tag + n, s, d))
        sem = cleared_semaphores(nc, ctx, tag)
        ps = lambda n, s: ctx.enter_context(nc.psum_tensor(tag + n, s, F32))
        pmax = sb("pmax", [P, 2, 4, NB])
        negmax = sb("negmax", [P, 2, 4])
        split = sb("split", [P, 2, NEGMAX_ROWS, 4], BF16)
        turned = sb("turned", [NEGMAX_ROWS * 4, P], BF16)
        max_rows = sb("max_rows", [NEGMAX_ROWS, 2, QB], BF16)
        probs = sb("probs", [P, 4, 2 * QB])
        acc_sb = sb("acc_sb", [P, QB]); sum_sb = sb("sum_sb", [P, QB]); inverse = sb("inverse", [P, QB])
        p1 = ps("p1", [P, 2, QB]); s2 = ps("s2", [P, 2, 2 * QB]); acc = ps("acc", [P, QB]); sums = ps("sums", [P, QB])
        s_item = sem("p1_filled"); s_free = sem("p1_read"); s_nm = sem("negmax_ready"); s_split = sem("negmax_split")
        s_rows = sem("max_rows_ready"); s_scores = sem("scores_ready"); s_exp = sem("probs_ready"); s_pv = sem("pv_done")
        s_evac = sem("out_copied"); s_inv = sem("inverse_ready"); s_div = sem("divided"); s_out = sem("out_ready")
        PAIRS = NT // 2
        seq = []
        for slot_n in range(NB + 2):
            if slot_n < NB: seq += [(slot_n, ("piece", n)) for n in range(8)]
            if slot_n >= 2: seq += [(slot_n, ("sum", slot_n - 2)), (slot_n, ("gate", slot_n - 2))]
            if slot_n < NB: seq += [(slot_n, ("piece", n)) for n in range(8, 16)] + [(slot_n, ("turn", slot_n))]
        where = {(s, it): n for n, (s, it) in enumerate(seq)}
        block = ctx.enter_context(nc.Block())

        def kinds(t, k0, k1):
            cuts = [k0] + [x for x in (t * P, (t + 1) * P) if k0 < x < k1] + [k1]
            return [(0 if a < t * P else 1 if a < (t + 1) * P else 2, a, z) for a, z in zip(cuts, cuts[1:])]

        @block.tensor
        def _(pe):
            def item(n):
                sl, (kind, x) = seq[n]
                bank = n % 2
                if n >= 2: pe.wait_ge(s_free, n - 1)
                if kind == "piece":
                    t, k0 = 4 * sl + x // 4, x % 4 * QB
                    q = queries[:, slot, t * P:(t + 1) * P]
                    for which, a, z in kinds(t, k0, k0 + QB):
                        mm = pe.matmul(p1[:, bank, a - k0:z - k0], q, keys[:, which, a:z], start=(a == k0), stop=True,
                                       skip_group_check=True)
                    lo, hi = max(k0, t * P - NEAR), min(k0 + QB, t * P + P + NEAR)
                    if lo < hi:
                        w0 = lo - (t * P - NEAR)
                        mm = pe.matmul(p1[:, bank, lo - k0:hi - k0], c.ident[:, :], near[:, t, w0:w0 + hi - lo],
                                       start=False, stop=True, skip_group_check=True)
                    mm.then_inc(s_item, 1)
                elif kind == "turn":
                    pe.wait_ge(s_split, 2 * (x + 1))
                    pe.transpose(p1[:, bank, :].bitcast(BF16)[0:NEGMAX_ROWS * 4, 0:P],
                                 split[:, x % 2, :, :].rearrange("p a t -> p (a t)"), c.ident_bf[:, :]).then_inc(s_item, 1)
                elif kind == "sum":
                    pe.wait_ge(s_evac, 2 * (x + 1))
                    pe.matmul(p1[:, bank, :], c.strip_heads[:, :], sum_sb[:, :], start=True, stop=True).then_inc(s_item, 1)
                else:
                    pe.matmul(p1[:, bank, :], c.pick_gate[0:32, slot, :], rows[:, x * QB:(x + 1) * QB],
                              start=True, stop=True).then_inc(s_item, 1)

            def scores(b, g):
                G = b * PAIRS + g
                if g == 0: pe.wait_ge(s_rows, 32 * (b + 1))
                if G >= 2: pe.wait_ge(s_exp, G - 1)
                for h in range(2):
                    j = 2 * g + h
                    at = s2[:, G % 2, h * QB:(h + 1) * QB]
                    runs = []
                    for i in range(4):
                        which = 0 if j < 4 * b + i else 1 if j == 4 * b + i else 2
                        if runs and runs[-1][0] == which: runs[-1][2] = i + 1
                        else: runs.append([which, i, i + 1])
                    for which, i0, i1 in runs:
                        pe.matmul(at[:, i0 * P:i1 * P], keys[:, which, j * P:(j + 1) * P],
                                  queries[:, slot, (4 * b + i0) * P:(4 * b + i1) * P], start=(i0 == 0), stop=True,
                                  skip_group_check=True)
                    mm = pe.matmul(at, c.ones_bf[0:NEGMAX_ROWS, :], max_rows[:, b % 2, :], start=False, stop=True, skip_group_check=True)
                    for i in range(4):
                        t = 4 * b + i
                        if abs(j - t) > 1: continue
                        w0, p0, n = ((0, NEAR, NEAR), (NEAR, 0, P), (P + NEAR, 0, NEAR))[j - t + 1]
                        mm = pe.matmul(at[p0:p0 + n, i * P:(i + 1) * P], near[:, t, w0:w0 + n], c.ident[:, :],
                                       start=False, stop=True, skip_group_check=True)
                mm.then_inc(s_scores, 1)

            def pv(b, q):
                pe.wait_ge(s_exp, b * PAIRS + 2 * q + 2)
                if q == 0 and b: pe.wait_ge(s_evac, 2 * b)
                for k in range(4):
                    j = 4 * q + k
                    p = probs[:, (b * PAIRS + j // 2) % 4, j % 2 * QB:(j % 2 + 1) * QB]
                    pe.matmul(acc[:, :], values[:, j, :], p, start=(j == 0), stop=(j == NT - 1))
                for k in range(4):
                    j = 4 * q + k
                    p = probs[:, (b * PAIRS + j // 2) % 4, j % 2 * QB:(j % 2 + 1) * QB]
                    mm = pe.matmul(sums[32 * k:32 * k + 32, :], c.ones[:, 0:32], p, start=(q == 0), stop=(q == 3), skip_group_check=True)
                mm.then_inc(s_pv, 1)

            todo = list(range(len(seq)))
            while todo and seq[todo[0]][0] == 0: item(todo.pop(0))
            for b in range(NB):
                for g in range(PAIRS):
                    scores(b, g)
                    if g >= 2 and g % 2 == 0: pv(b, g // 2 - 1)
                    for _ in range(3):
                        if todo and seq[todo[0]][0] == b + 1: item(todo.pop(0))
                pv(b, 3)
                while todo and seq[todo[0]][0] == b + 1: item(todo.pop(0))
            for n in todo: item(n)

        @block.vector
        def _(dve):
            for n, (sl, (kind, x)) in enumerate(seq):
                bank = n % 2
                dve.wait_ge(s_item, n + 1)
                if kind == "piece":
                    dve.tensor_reduce(pmax[:, sl % 2, x // 4, x % 4:x % 4 + 1], p1[:, bank, :], AX.X, ALU.max).then_inc(s_free, 1)
                    if x == 15:
                        dve.wait_ge(s_free, n + 1)
                        if sl >= 2: dve.wait_ge(s_split, 2 * (sl - 1))
                        dve.tensor_reduce(negmax[:, sl % 2, :], pmax[:, sl % 2, :, :], AX.X, ALU.max, negate=True).then_inc(s_nm, 1)
                elif kind == "turn":
                    if x: dve.wait_ge(s_rows, 32 * x)
                    dve.tensor_copy(turned[:, :], p1[:, bank, :].bitcast(BF16)[0:NEGMAX_ROWS * 4, 0:P]).then_inc(s_free, 1)
                elif kind == "sum":
                    if x: dve.wait_ge(s_free, where[(sl - 1, ("gate", x - 1))] + 1)
                    dve.reciprocal(inverse[:, :], p1[:, bank, :]).then_inc(s_free, 1)
                    dve.wait_ge(s_free, n + 1)
                    dve.tensor_tensor(inverse[:, :], acc_sb[:, :], inverse[:, :], ALU.mult).then_inc(s_div, 1)
                else:
                    dve.wait_ge(s_div, x + 1)
                    dve.scalar_tensor_tensor(out=out[:, slot, x * QB:(x + 1) * QB], in0=inverse[:, :], scalar=v_bias,
                                             in1=p1[:, bank, :], op0=ALU.add, op1=ALU.mult).then_inc(s_free, 1)

        @block.gpsimd
        def _(pool):
            for b in range(NB):
                pool.wait_ge(s_nm, b + 1)
                if b >= 2: pool.wait_ge(s_free, where[(b - 2, ("turn", b - 2))] + 1)
                pool.tensor_copy(split[:, b % 2, 0, :], negmax[:, b % 2, :]).then_inc(s_split, 1)
                pool.wait_ge(s_split, 2 * b + 1)
                pool.tensor_tensor(split[:, b % 2, 1, :], negmax[:, b % 2, :], split[:, b % 2, 0, :], ALU.subtract).then_inc(s_split, 1)

        @block.sync
        def _(sp):
            for b in range(NB):
                sp.wait_ge(s_free, where[(b, ("turn", b))] + 1)
                if b >= 2: sp.wait_ge(s_scores, (b - 1) * PAIRS)
                for k in range(NEGMAX_ROWS):
                    sp.dma_start(max_rows[k:k + 1, b % 2, :], turned[4 * k:4 * k + 4, :]).then_inc(s_rows, 16)

        @block.scalar
        def _(act):
            for b in range(NB):
                for g in range(PAIRS):
                    G = b * PAIRS + g
                    act.wait_ge(s_scores, G + 1)
                    if G >= 4: act.wait_ge(s_pv, G // 2 - 1)
                    act.activation(probs[:, G % 4, :], s2[:, G % 2, :], ACT.Exp).then_inc(s_exp, 1)
                act.wait_ge(s_pv, 4 * (b + 1))
                if b: act.wait_ge(s_div, b)
                act.activation(acc_sb[:, :], acc[:, :], ACT.Copy).then_inc(s_evac, 1)
                act.activation(sum_sb[:, :], sums[:, :], ACT.Copy).then_inc(s_evac, 1)


def moa_out(nc, tag, c, heads, rows, rows_bf, o_w, o_bias_rows, base, dst):
    with ExitStack() as ctx:
        sb = lambda n, s: ctx.enter_context(nc.sbuf_tensor(tag + n, s, F32))
        sem = cleared_semaphores(nc, ctx, tag)
        routed = sb("routed", [P, 2, QB])
        mask_ps = ctx.enter_context(nc.psum_tensor(tag + "mask_ps", [P, 4, QB], F32))
        o_ps = ctx.enter_context(nc.psum_tensor(tag + "o_ps", [P, 2, QB], F32))
        s_mask = sem("masks_ready"); s_first = sem("first_routed"); s_routed = sem("routed"); s_o = sem("o_ready"); s_used = sem("routed_used"); s_dst = sem("dst_ready")
        units = [(b, e) for b in range(NB) for e in range(EA)]
        block = ctx.enter_context(nc.Block())

        @block.tensor
        def _(pe):
            for i in range(len(units) + 1):
                if i < len(units):
                    b, e = units[i]
                    cols = slice(b * QB, (b + 1) * QB)
                    if i >= 2: pe.wait_ge(s_routed, i - 1)
                    for k in range(2):
                        mm = pe.matmul(mask_ps[:, i % 2 * 2 + k, :], c.pick_bf[0:32, EA * (1 + k) + e, :], rows_bf[:, cols], start=True, stop=True)
                    mm.then_inc(s_mask, 1)
                if i:
                    b, e = units[i - 1]
                    cols = slice(b * QB, (b + 1) * QB)
                    if e == 0:
                        if b >= 2: pe.wait_ge(s_dst, b - 1)
                        pe.matmul(o_ps[:, b % 2, :], o_bias_rows[:, :], rows[:, cols], start=True, stop=False)
                    pe.wait_ge(s_routed, i)
                    pe.matmul(o_ps[:, b % 2, :], o_w[:, e, :], routed[:, (i - 1) % 2, :], start=False, stop=(e == EA - 1)).then_inc(s_used, 1)

        def finish(dve, b):
            dve.wait_ge(s_used, EA * (b + 1))
            dve.tensor_tensor(dst[:, b * QB:(b + 1) * QB], base[:, b * QB:(b + 1) * QB], o_ps[:, b % 2, :], ALU.add).then_inc(s_dst, 1)

        @block.vector
        def _(dve):
            for i, (b, e) in enumerate(units):
                cols = slice(b * QB, (b + 1) * QB)
                dve.wait_ge(s_mask, i + 1)
                if i >= 2: dve.wait_ge(s_used, i - 1)
                dve.tensor_tensor(routed[:, i % 2, :], heads[:, 0, cols], mask_ps[:, i % 2 * 2, :], ALU.mult).then_inc(s_first, 1)
                dve.wait_ge(s_first, i + 1)
                dve.copy_predicated(routed[:, i % 2, :], mask_ps[:, i % 2 * 2 + 1, :].bitcast(U32), heads[:, 1, cols]).then_inc(s_routed, 1)
                if e == 1 and b: finish(dve, b - 1)
            finish(dve, NB - 1)



def moe_ffn(nc, tag, c, src, rows, w1, b1, w2, b2_rows, base, gain, x):
    PAIRS = 8
    with ExitStack() as ctx:
        sb = lambda n, s: ctx.enter_context(nc.sbuf_tensor(tag + n, s, F32))
        sem = cleared_semaphores(nc, ctx, tag)
        hidden = sb("hidden", [P, 2, QB]); gated = sb("gated", [P, 2, QB]); total = sb("total", [P, 2, QB])
        h_ps = ctx.enter_context(nc.psum_tensor(tag + "h_ps", [P, 2, QB], F32))
        g_ps = ctx.enter_context(nc.psum_tensor(tag + "g_ps", [P, 2, QB], F32))
        o_ps = ctx.enter_context(nc.psum_tensor(tag + "o_ps", [P, 2, QB], F32))
        s_h = sem("h_ready"); s_relu = sem("relu_ready"); s_g = sem("gates_ready"); s_gated = sem("gated"); s_used = sem("gated_used")
        s_total = sem("total_ready"); s_x = sem("x_ready")
        units = [(b, e) for b in range(NB) for e in range(PAIRS)]
        block = ctx.enter_context(nc.Block())

        @block.tensor
        def _(pe):
            for i in range(len(units) + 1):
                if i < len(units):
                    b, e = units[i]
                    cols = slice(b * QB, (b + 1) * QB)
                    if i >= 2: pe.wait_ge(s_relu, i - 1)
                    pe.matmul(h_ps[:, i % 2, :], w1[:, e, :], src[:, cols], start=True, stop=True).then_inc(s_h, 1)
                    if i >= 2: pe.wait_ge(s_gated, i - 1)
                    pe.matmul(g_ps[:, i % 2, :], c.pick_pair[0:16, e, :], rows[:, cols], start=True, stop=True).then_inc(s_g, 1)
                if i:
                    b, e = units[i - 1]
                    cols = slice(b * QB, (b + 1) * QB)
                    if e == 0:
                        if b >= 2: pe.wait_ge(s_total, b - 1)
                        pe.matmul(o_ps[:, b % 2, :], b2_rows[:, :], rows[:, cols], start=True, stop=False)
                    pe.wait_ge(s_gated, i)
                    pe.matmul(o_ps[:, b % 2, :], w2[:, e, :], gated[:, (i - 1) % 2, :], start=False, stop=(e == PAIRS - 1)).then_inc(s_used, 1)

        @block.scalar
        def _(act):
            for i, (b, e) in enumerate(units):
                act.wait_ge(s_h, i + 1)
                if i >= 2: act.wait_ge(s_gated, i - 1)
                act.activation(hidden[:, i % 2, :], h_ps[:, i % 2, :], ACT.Relu, bias=b1(e)).then_inc(s_relu, 1)

        def finish(dve, b):
            cols = slice(b * QB, (b + 1) * QB)
            dve.wait_ge(s_used, PAIRS * (b + 1))
            dve.tensor_tensor(total[:, b % 2, :], base[:, cols], o_ps[:, b % 2, :], ALU.add).then_inc(s_total, 1)
            dve.wait_ge(s_total, b + 1)
            dve.scalar_tensor_tensor(out=x[:, cols], in0=total[:, b % 2, :], scalar=gain, in1=x[:, cols],
                                     op0=ALU.mult, op1=ALU.add).then_inc(s_x, 1)

        @block.vector
        def _(dve):
            for i, (b, e) in enumerate(units):
                dve.wait_ge(s_relu, i + 1)
                dve.wait_ge(s_g, i + 1)
                if i >= 2: dve.wait_ge(s_used, i - 1)
                dve.tensor_tensor(gated[:, i % 2, :], hidden[:, i % 2, :], g_ps[:, i % 2, :], ALU.mult).then_inc(s_gated, 1)
                if e == 1 and b: finish(dve, b - 1)
            finish(dve, NB - 1)



def swiglu_experts(nc, tag, c, src, rows, rows_dram, w0, w1, wo, gain, x):
    E = 8
    F = 4
    with ExitStack() as ctx:
        sb = lambda n, s: ctx.enter_context(nc.sbuf_tensor(tag + n, s, F32))
        sem = cleared_semaphores(nc, ctx, tag)
        ps = lambda n, s: ctx.enter_context(nc.psum_tensor(tag + n, s, F32))
        w0_sb = sb("w0_sb", [P, 2, F * P]); w1_sb = sb("w1_sb", [P, 2, F * P]); wo_sb = sb("wo_sb", [P, 2, F, D])
        gates = sb("gates", [P, 2, S]); gated = sb("gated", [P, 2, QB])
        silu = sb("silu", [P, 4, QB]); hidden = sb("hidden", [P, 2 * F, QB]); zeros = sb("zeros", [P, QB])
        a_ps = ps("a_ps", [P, 2, QB]); b_ps = ps("b_ps", [P, 2, QB]); o_ps = ps("o_ps", [P, NB, QB])
        s_store = sem("gates_stored"); s_load = [sem(f"expert_loaded{i}") for i in range(2)]; s_zero = sem("zeroed")
        s_gated = sem("src_gated"); s_a = sem("a_ready"); s_b = sem("b_ready"); s_silu = sem("silu_ready"); s_hidden = sem("hidden_ready")
        s_o = sem("o_ready"); s_x = sem("x_ready")
        UNITS = NB * F
        AHEAD, AHEAD_B = 2, F + 2
        block = ctx.enter_context(nc.Block())

        @block.sync
        def _(sp):
            def load(e, u):
                one = lambda a: a[bass.ds(e, 1)]
                sp.dma_start(w0_sb[:, u, :], one(w0).rearrange("e d f -> (e d) f")).then_inc(s_load[u], 16)
                sp.dma_start(w1_sb[:, u, :], one(w1).rearrange("e d f -> (e d) f")).then_inc(s_load[u], 16)
                sp.dma_start(gates[:, u, :], one(rows_dram).rearrange("e s -> (e s)").partition_broadcast(P)).then_inc(s_load[u], 16)
                sp.dma_start(wo_sb[:, u, :, :], one(wo).rearrange("e (f p) d -> (e p) f d", p=P)).then_inc(s_load[u], 16)
            sp.dma_start(rows_dram, rows[0:E, :]).then_inc(s_store, 16)
            sp.wait_ge(s_store, 16)
            load(0, 0); load(1, 1)
            with sp.Fori(0, E // 2 - 1) as it:
                for u in range(2):
                    sp.wait_ge(s_o, it * 2 * NB + (u + 1) * NB)
                    load(it * 2 + (u + 2), u)

        @block.gpsimd
        def _(pool):
            pool.memset(zeros[:, :], 0.0).then_inc(s_zero, 1)
            with pool.Fori(0, E // 2) as it:
                for u in range(2):
                    for b in range(NB):
                        cols = slice(b * QB, (b + 1) * QB)
                        n = it * 2 * NB + (u * NB + b)
                        if b == 0: pool.wait_ge(s_load[u], it * 64 + 64)
                        pool.wait_ge(s_b, n * F + (AHEAD_B - F))
                        pool.tensor_tensor(gated[:, b % 2, :], src[:, cols], gates[:, u, cols], ALU.mult).then_inc(s_gated, 1)

        @block.tensor
        def _(pe):
            pe.wait_ge(s_zero, 1)
            for b in range(NB):
                pe.matmul(o_ps[:, b, :], zeros[:, 0:P], zeros[:, :], start=True, stop=True)
            pe.sem_inc(s_b, AHEAD_B)

            def hidden_products(it, u, b, f, U):
                cols = slice(b * QB, (b + 1) * QB)
                pe.wait_ge(s_silu, U + (AHEAD - 1))
                pe.matmul(a_ps[:, f % 2, :], w0_sb[:, u, f * P:(f + 1) * P], src[:, cols], start=True, stop=True).then_inc(s_a, 1)
                pe.wait_ge(s_hidden, U + (AHEAD - 1))
                pe.matmul(b_ps[:, f % 2, :], w1_sb[:, u, f * P:(f + 1) * P], gated[:, b % 2, :], start=True, stop=True).then_inc(s_b, 1)

            def out_products(u, b, n):
                pe.wait_ge(s_hidden, n * F + (F + AHEAD))
                for f in range(F):
                    mm = pe.matmul(o_ps[:, b, :], wo_sb[:, u, f, :], hidden[:, b % 2 * F + f, :], start=False, stop=True, skip_group_check=True)
                mm.then_inc(s_o, 1)

            with pe.Fori(0, E // 2) as it:
                for u in range(2):
                    pe.wait_ge(s_load[u], it * 64 + 64)
                    for b in range(NB):
                        n = it * 2 * NB + (u * NB + b)
                        pe.wait_ge(s_gated, n + 1)
                        for f in range(F): hidden_products(it, u, b, f, n * F + f)
                        if b: out_products(u, b - 1, n - 1)
                    out_products(u, NB - 1, n)

        @block.scalar
        def _(act):
            act.sem_inc(s_silu, AHEAD)
            with act.Fori(0, E // 2) as it:
                for k in range(2 * UNITS):
                    U = it * 2 * UNITS + k
                    act.wait_ge(s_a, U + 1)
                    act.activation(silu[:, k % 4, :], a_ps[:, k % 2, :], ACT.Silu).then_inc(s_silu, 1)

        @block.vector
        def _(dve):
            dve.sem_inc(s_hidden, AHEAD)
            with dve.Fori(0, E // 2) as it:
                for k in range(2 * UNITS):
                    U = it * 2 * UNITS + k
                    dve.wait_ge(s_silu, U + (1 + AHEAD))
                    dve.wait_ge(s_b, U + (1 + AHEAD_B))
                    dve.tensor_tensor(hidden[:, k // F % 2 * F + k % F, :], silu[:, k % 4, :], b_ps[:, k % 2, :], ALU.mult).then_inc(s_hidden, 1)
            dve.wait_ge(s_o, E * NB)
            for b in range(NB):
                cols = slice(b * QB, (b + 1) * QB)
                dve.scalar_tensor_tensor(out=x[:, cols], in0=o_ps[:, b, :], scalar=gain, in1=x[:, cols],
                                         op0=ALU.mult, op1=ALU.add).then_inc(s_x, 1)


VECTORS = ["L0_c", "L1_c", "qkv_b", "out_b", "g_attn", "b_attn", "g1", "b1", "g2", "b2", "b_inl", "ff_b1", "ff_b2",
           "ln1_w", "ln1_b", "ln2_w", "ln2_b", "q_b", "k_b", "v_b", "moe_b1", "L1_b_attn", "L1_b_proj"]
WIDTHS = {"qkv_b": 3, "ff_b1": 4, "q_b": 8, "moe_b1": 8, "L1_b_attn": 3}


def vector_columns():
    at, n = {}, 0
    for name in VECTORS:
        at[name] = n
        n += WIDTHS.get(name, 1)
    return at, n


CONST_F32 = [("ident", P), ("averages", P), ("ones", P), ("strip_heads", P), ("spread_heads", P), ("counting", 16),
             ("eps", 1), ("one", 1), ("pick_gate", 2 * P), ("pick_pair", 8 * P)]
CONST_BF16 = [("ident_bf", P), ("ones_bf", P), ("mask_q", P), ("mask_k", P), ("pick_bf", 24 * P)]


class Constants:

    def __init__(self, consts, consts_bf):
        cut = {}
        for names, tensor in ((CONST_F32, consts), (CONST_BF16, consts_bf)):
            n = 0
            for name, w in names:
                cut[name] = tensor[:, n:n + w]
                n += w
        self.ident, self.averages, self.ones = cut["ident"], cut["averages"], cut["ones"]
        self.strip_heads, self.spread_heads = cut["strip_heads"], cut["spread_heads"]
        self.counting, self.eps, self.one = cut["counting"], cut["eps"], cut["one"]
        self.pick_gate = cut["pick_gate"].rearrange("p (k m) -> p k m", m=P)
        self.pick_pair = cut["pick_pair"].rearrange("p (k m) -> p k m", m=P)
        self.ident_bf, self.ones_bf, self.mask_q, self.mask_k = cut["ident_bf"], cut["ones_bf"], cut["mask_q"], cut["mask_k"]
        self.pick_bf = cut["pick_bf"].rearrange("p (k m) -> p k m", m=P)


def modulation(nc, c, modulations, vectors, at, weights, loaded, s_wait):
    with ExitStack() as ctx:
        sem = cleared_semaphores(nc, ctx, "mod_")
        silu = ctx.enter_context(nc.sbuf_tensor("mod_silu", [P, 2], F32))
        sign = ctx.enter_context(nc.sbuf_tensor("mod_sign", [P, 2, 2], F32))
        size = ctx.enter_context(nc.sbuf_tensor("mod_size", [P, 2, 2], F32))
        mod_ps = ctx.enter_context(nc.psum_tensor("mod_ps", [P, 2, 6], F32))
        s_silu = sem("silu_ready"); s_mod = sem("product"); s_step = sem("step")
        block = ctx.enter_context(nc.Block())

        @block.scalar
        def _(act):
            act.wait_ge(loaded, s_wait)
            act.activation(silu[:, :], vectors[:, at["L0_c"]:at["L1_c"] + 1], ACT.Silu).then_inc(s_silu, 1)

        @block.tensor
        def _(pe):
            pe.wait_ge(loaded, s_wait)
            pe.wait_ge(s_silu, 1)
            for layer in range(2):
                for i in range(6):
                    mm = pe.matmul(mod_ps[:, layer, i:i + 1], weights[:, layer, i * P:(i + 1) * P], silu[:, layer:layer + 1],
                                   start=True, stop=True)
            mm.then_inc(s_mod, 1)

        @block.vector
        def _(dve):
            dve.wait_ge(s_mod, 1)
            dve.tensor_copy(modulations[:, :, :], mod_ps[:, :, :]).then_inc(s_step, 1)
            dve.wait_ge(s_step, 1)
            gates = modulations[:, :, 2:6:3]
            dve.tensor_scalar(modulations[:, :, 1:5:3], mod_ps[:, :, 1:5:3], 1.0, None, ALU.add)
            dve.tensor_scalar(sign[:, :, :], gates, 0.0, 2.0, ALU.is_ge, ALU.mult).then_inc(s_step, 1)
            dve.wait_ge(s_step, 2)
            dve.scalar_tensor_tensor(out=size[:, :, :], in0=sign[:, :, :], scalar=-1.0, in1=gates, op0=ALU.add, op1=ALU.mult).then_inc(s_step, 1)
            dve.wait_ge(s_step, 3)
            dve.tensor_scalar(size[:, :, :], size[:, :, :], 0.25, None, ALU.max).then_inc(s_step, 1)
            dve.wait_ge(s_step, 4)
            dve.scalar_tensor_tensor(out=gates, in0=sign[:, :, :], scalar=-1.0, in1=size[:, :, :], op0=ALU.add, op1=ALU.mult)


def adaln_kernel(nc, ins, out):
    at, n_vec = vector_columns()
    with ExitStack() as ctx:
        sb = lambda n, s, d=F32: ctx.enter_context(nc.sbuf_tensor(n, s, d))
        dram = lambda n, s, d=F32: nc.dram_tensor(n, s, d, kind="Internal").ap()
        x = sb("x", [P, S])
        vectors = sb("vectors", [P, n_vec])
        consts = sb("consts", [P, sum(w for _, w in CONST_F32)])
        consts_bf = sb("consts_bf", [P, sum(w for _, w in CONST_BF16)], BF16)
        w_mod = sb("w_mod", [P, 2, 6 * D])
        w_qkv = sb("w_qkv", [P, 2, 3 * D])
        w_out = sb("w_out", [P, 2, D])
        w_ctx = sb("w_ctx", [P, D]); w_x = sb("w_x", [P, D])
        ff_w1 = sb("ff_w1", [P, 4 * P]); ff_w2 = sb("ff_w2", [P, 4, D])
        modulations = sb("modulations", [P, 2, 6])
        s_load = ctx.enter_context(nc.semaphore("inputs_loaded"))
        s_store = ctx.enter_context(nc.semaphore("output_stored"))
        q_rows = dram("q_rows", [H, NROW, S], BF16); k_rows = dram("k_rows", [H, NROW, S], BF16)
        o_dram = dram("o_parts", [H, 4, HD + 1, S]); rden_dram = dram("inverse_sums", [H, S])
        band_dram = dram("band", [NT, P, 2 * P]); gates_dram = dram("gate_rows", [8, S])

        c = Constants(consts, consts_bf)

        def vec(name, k=0): return vectors[:, at[name] + k:at[name] + k + 1]
        def mod(layer, i): return modulations[:, layer, i:i + 1]

        with nc.Block() as block:
            @block.sync
            def _(sp):
                loads = [(vectors[:, :], ins["vectors"]), (w_mod[:, 0, :], ins["L0_wmod"]), (w_mod[:, 1, :], ins["L1_wmod"]),
                         (consts[:, :], ins["consts"]), (x[:, :], ins["x"]), (consts_bf[:, :], ins["consts_bf"].bitcast(BF16)),
                         (w_qkv[:, 0, :], ins["L0_attn_qkv_w"]), (w_qkv[:, 1, :], ins["L1_attn_W_attn"]),
                         (w_out[:, 0, :], ins["L0_attn_out_w"]), (w_out[:, 1, :], ins["L1_attn_W_proj"]),
                         (w_ctx[:, :], ins["L0_attn_w_ctx"]), (w_x[:, :], ins["L0_attn_w_x"]), (ff_w1[:, :], ins["L0_attn_ff_w1"]),
                         (ff_w2[:, :, :], ins["L0_attn_ff_w2"].rearrange("(f p) d -> p f d", p=P))]
                for dst, src in loads: sp.dma_start(dst, src).then_inc(s_load, 16)
                sp.wait_ge(s_load, 16 * len(loads))

        modulation(nc, c, modulations, vectors, at, w_mod, s_load, 16)

        def dump(t):
            with nc.Block() as block:
                @block.sync
                def _(sp):
                    sp.dma_start(out, t).then_inc(s_store, 16)
                    sp.wait_ge(s_store, 16)

        def causal_attention(layer, src, q_bias, k_bias, v_bias, out_bias, ctx_out, gain, base, dst):
            with ExitStack() as own:
                v_all = own.enter_context(nc.sbuf_tensor(f"v_all{layer}", [P, NT, D], F32))
                qkv(nc, f"qkv{layer}_", c, src, w_qkv[:, layer, :], q_bias, k_bias, v_all, q_rows, k_rows)
                consts_of = lambda name: (lambda n: ins[name].bitcast(BF16)[bass.ds(n, 1)].rearrange("o r s -> (o r) s")) if layer else (lambda n: ins[name].bitcast(BF16))
                attention(nc, f"att{layer}_", q_rows, k_rows, consts_of(f"q_const{layer}"), consts_of(f"k_const{layer}"),
                          v_all, c.ident_bf, c.mask_q, c.mask_k, o_dram)
            attention_out(nc, f"out{layer}_", c, o_dram, rden_dram, w_out[:, layer, :], v_bias, out_bias, ctx_out, gain, base, dst)

        with ExitStack() as own:
            t = lambda n: own.enter_context(nc.sbuf_tensor(n, [P, S], F32))
            h, normed, attended = t("h0"), t("normed0"), t("attended0")
            layer_norms(nc, "ln0_", c, [(x, h, mod(0, 1), mod(0, 0)), (h, normed, vec("g_attn"), vec("b_attn"))])
            causal_attention(0, normed, vec("qkv_b", 0), vec("qkv_b", 1), vec("qkv_b", 2), vec("out_b"), attended, c.one, h, h)
            layer_norms(nc, "ln1_", c, [(h, normed, vec("g1"), vec("b1"))])
            liquid(nc, "liq_", c, attended, w_ctx, w_x, vec("b_inl"), normed, h, h)
            layer_norms(nc, "ln2_", c, [(h, normed, vec("g2"), vec("b2"))])
            gelu_ffn(nc, "ffn_", c, normed, ff_w1, lambda f: vec("ff_b1", f), ff_w2, vec("ff_b2"), h, mod(0, 2), x)

        with ExitStack() as own:
            t = lambda n, s=[P, S], d=F32: own.enter_context(nc.sbuf_tensor(n, s, d))
            h, normed, moved = t("h1"), t("normed1"), t("moved1")
            rows = t("moa_rows", [32, S]); rows_bf = t("moa_rows_bf", [32, S], BF16); moe_rows = t("moe_rows", [16, S])
            moe_w1 = t("moe_w1", [P, 8, P]); moe_w2 = t("moe_w2", [P, 8, D]); moe_b2 = t("moe_b2", [16, D]); moe_gate = t("moe_gate", [P, 16])
            with ExitStack() as inner:
                u = lambda n, s: inner.enter_context(nc.sbuf_tensor(n, s, F32))
                gate_w = u("gate_w", [P, EA]); q_w = u("q_w", [P, EA, D]); kv_w = u("kv_w", [P, 2, D]); rel = u("rel", [P, 2 * P])
                o_w = u("o_w", [P, EA, D]); o_b = u("o_b", [32, D])
                keys = u("keys", [P, 3, S]); values = u("values", [P, NT, D]); queries = u("queries", [P, 2, S])
                with nc.Block() as block:
                    s_w = inner.enter_context(nc.semaphore("moa_weights"))
                    s_z = inner.enter_context(nc.semaphore("o_b_zeroed"))
                    @block.gpsimd
                    def _(pool):
                        pool.memset(o_b[:, :], 0.0).then_inc(s_z, 1)
                    @block.sync
                    def _(sp):
                        sp.wait_ge(s_z, 1)
                        loads = [(gate_w[:, :], ins["L0_ffn_attn_gate_w"]), (q_w[:, :, :], ins["L0_ffn_q_w"].rearrange("e d h -> d e h")),
                                 (kv_w[:, 0, :], ins["L0_ffn_k_w"]), (kv_w[:, 1, :], ins["L0_ffn_v_w"]), (rel[:, :], ins["rel"]),
                                 (o_w[:, :, :], ins["L0_ffn_o_w"].rearrange("e h d -> h e d")), (o_b[0:EA, :], ins["L0_ffn_o_b"]),
                                 (moe_w1[:, :, :].rearrange("p e (t f) -> p (e t) f", t=2), ins["L0_ffn_ff_w1"].rearrange("e d f -> d e f")),
                                 (moe_w2[:, :, :], ins["L0_ffn_ff_w2"].rearrange("(e t) f d -> (t f) e d", t=2)),
                                 (moe_b2[:, :], ins["L0_ffn_ff_b2"]), (moe_gate[:, :], ins["L0_ffn_ff_gate_w"])]
                        for dst, src in loads: sp.dma_start(dst, src).then_inc(s_w, 16)
                        sp.wait_ge(s_w, 16 * len(loads))
                layer_norms(nc, "ln3_", c, [(x, h, mod(0, 4), mod(0, 3)), (h, normed, vec("ln1_w"), vec("ln1_b"))])
                top2_gates(nc, "g1_", c, normed, gate_w[:, :], EA, rows, rows_bf)
                moa_keys(nc, "keys_", c, normed, kv_w[:, 0, :], vec("k_b"), kv_w[:, 1, :], rel, keys, values)
                scaled_q_bias = u("scaled_q_bias", [P, EA])
                with nc.Block() as block:
                    @block.vector
                    def _(dve):
                        dve.tensor_scalar(scaled_q_bias[:, :], vectors[:, at["q_b"]:at["q_b"] + EA], float(D) ** -0.5, None, ALU.mult)
                moa_queries(nc, "queries_", c, normed, q_w, lambda e: scaled_q_bias[:, e:e + 1], rows_bf, queries)
                with ExitStack() as deep:
                    near = deep.enter_context(nc.sbuf_tensor("near", [P, NT, WINDOW], F32))
                    for slot in range(2):
                        moa_near_bias(nc, f"near{slot}_", c, rel[:, :], queries, slot, near, band_dram)
                        moa_attention(nc, f"moa{slot}_", c, keys, values, queries, slot, near, rows, vec("v_b"), queries)
                moa_out(nc, "mo_", c, queries, rows, rows_bf, o_w, o_b, h, moved)
            layer_norms(nc, "ln4_", c, [(moved, normed, vec("ln2_w"), vec("ln2_b"))])
            top2_gates(nc, "g2_", c, normed, moe_gate[:, :], 16, moe_rows)
            moe_ffn(nc, "moe_", c, normed, moe_rows, moe_w1, lambda e: vec("moe_b1", e), moe_w2, moe_b2, moved, mod(0, 5), x)

        with ExitStack() as own:
            t = lambda n, s=[P, S], d=F32: own.enter_context(nc.sbuf_tensor(n, s, d))
            h, attended = t("h2"), t("attended1")
            layer_norms(nc, "ln5_", c, [(x, h, mod(1, 1), mod(1, 0))])
            causal_attention(1, h, vec("L1_b_attn", 0), vec("L1_b_attn", 1), vec("L1_b_attn", 2), vec("L1_b_proj"), attended, mod(1, 2), x, x)
            gates = t("expert_gates", [8, S]); gate_w = t("expert_gate_w", [P, 8])
            with nc.Block() as block:
                s_w = own.enter_context(nc.semaphore("gate_w_loaded"))
                @block.sync
                def _(sp):
                    sp.dma_start(gate_w[:, :], ins["L1_ffn_gate_kernel"]).then_inc(s_w, 16)
                    sp.wait_ge(s_w, 16)
            layer_norms(nc, "ln6_", c, [(x, h, mod(1, 4), mod(1, 3))])
            top2_gates(nc, "g3_", c, h, gate_w[:, :], 8, gates)
            swiglu_experts(nc, "exp_", c, h, gates, gates_dram, ins["L1_ffn_w0"], ins["L1_ffn_w1"], ins["L1_ffn_wo"], mod(1, 5), x)
        dump(x[:, :])


def host_constants():
    f = {name: np.zeros((P, w), np.float32) for name, w in CONST_F32}
    f["ident"][:] = np.eye(P)
    f["averages"][:] = 1.0 / P
    f["ones"][:] = 1.0
    f["strip_heads"][::32] = 1.0
    for h in range(H): f["spread_heads"][h, h * HD:(h + 1) * HD] = 1.0
    f["counting"][:] = np.arange(16)
    f["eps"][:] = EPS
    f["one"][:] = 1.0
    for k in range(2): f["pick_gate"][3 * EA + k, k * P:(k + 1) * P] = 1.0
    for e in range(8):
        for k in range(2): f["pick_pair"][2 * e + k, e * P + k * 64:e * P + (k + 1) * 64] = 1.0
    b = {name: np.zeros((P, w), np.float32) for name, w in CONST_BF16}
    b["ident_bf"][:] = np.eye(P)
    b["ones_bf"][:] = 1.0
    i = np.arange(P)
    b["mask_q"][:] = np.where(i[None, :] > i[:, None], NEG, 0)
    b["mask_k"][:] = np.where(i[None, :] < i[:, None], NEG, 0)
    for r in range(24): b["pick_bf"][r, r * P:(r + 1) * P] = 1.0
    pos = np.arange(S)
    slopes = 2.0 ** -np.arange(1, H + 1)
    q1, k1 = np.zeros((2, H, CROWS, S), np.float32)
    high, low = pos // 256 * 256, pos % 256
    q1[:, 0:2] = 1.0
    k1[:, 0], k1[:, 1] = slopes[:, None] * high, slopes[:, None] * low
    q1[:, 2], q1[:, 3] = -slopes[:, None] * high, -slopes[:, None] * low
    k1[:, 2:4] = 1.0
    k1[:, MROW - NROW:MROW - NROW + 2] = 1.0
    q0, k0 = np.zeros((2, CROWS, S), np.float32)
    k0[MROW - NROW:MROW - NROW + 2] = 1.0
    bits = lambda a: (np.ascontiguousarray(a).view(np.uint32) >> 16).astype(np.uint16)
    return {"consts": np.concatenate([f[n] for n, _ in CONST_F32], 1),
            "consts_bf": bits(np.concatenate([b[n] for n, _ in CONST_BF16], 1)),
            "q_const0": bits(q0), "k_const0": bits(k0), "q_const1": bits(q1), "k_const1": bits(k1)}


AS_THEY_ARE = ["L0_wmod", "L1_wmod", "L0_attn_qkv_w", "L1_attn_W_attn", "L0_attn_out_w", "L1_attn_W_proj", "L0_attn_w_ctx",
               "L0_attn_w_x", "L0_attn_ff_w1", "L0_attn_ff_w2", "L0_ffn_attn_gate_w", "L0_ffn_q_w", "L0_ffn_k_w", "L0_ffn_v_w",
               "L0_ffn_o_w", "L0_ffn_o_b", "L0_ffn_ff_w1", "L0_ffn_ff_w2", "L0_ffn_ff_b2", "L0_ffn_ff_gate_w",
               "L1_ffn_gate_kernel", "L1_ffn_w0", "L1_ffn_w1", "L1_ffn_wo"]
SOURCES = {"L0_c": "L0_c", "L1_c": "L1_c", "q_b": "L0_ffn_q_b", "k_b": "L0_ffn_k_b", "v_b": "L0_ffn_v_b",
           "moe_b1": "L0_ffn_ff_b1", "ln1_w": "L0_ffn_ln1_w", "ln1_b": "L0_ffn_ln1_b", "ln2_w": "L0_ffn_ln2_w",
           "ln2_b": "L0_ffn_ln2_b", "L1_b_attn": "L1_attn_b_attn", "L1_b_proj": "L1_attn_b_proj"}


def lay_out(inputs):
    a = {name: np.ascontiguousarray(inputs[name]) for name in AS_THEY_ARE}
    a["x"] = np.ascontiguousarray(np.asarray(inputs["L0_attn_x"])[0].T)
    columns = []
    for name in VECTORS:
        v = np.asarray(inputs[SOURCES.get(name, "L0_attn_" + name)])
        columns.append(v.reshape(WIDTHS.get(name, 1), P).T)
    a["vectors"] = np.ascontiguousarray(np.concatenate(columns, 1))
    rel = np.asarray(inputs["L0_ffn_rel_table"])
    a["rel"] = np.ascontiguousarray(rel[np.clip(np.arange(-P, P), -NEAR, NEAR) + NEAR].T)
    a.update(host_constants())
    return a


def kernel(**inputs):
    import concourse.bacc as bacc
    from concourse.bass_utils import run_bass_kernel_spmd

    nc = bacc.Bacc("TRN2", target_bir_lowering=False, num_devices=1)
    arrays = lay_out(inputs)
    ins = {n: nc.dram_tensor("in_" + n, a.shape, mybir.dt.from_np(a.dtype), kind="ExternalInput").ap() for n, a in arrays.items()}
    out = nc.dram_tensor("out_0_dram", (P, S), F32, kind="ExternalOutput").ap()
    adaln_kernel(nc, ins, out)
    r = run_bass_kernel_spmd(nc, [{"in_" + n: a for n, a in arrays.items()}], core_ids=[0])
    return np.ascontiguousarray(r.results[0]["out_0_dram"].T)[None]
```

```python
from contextlib import ExitStack

import numpy as np

import concourse.bass as bass
from concourse import mybir

F32 = mybir.dt.float32
BF16 = mybir.dt.bfloat16
F32R = mybir.dt.float32r
U32 = mybir.dt.uint32
ALU = mybir.AluOpType
ACT = mybir.ActivationFunctionType
AX = mybir.AxisListType


def cleared_semaphores(nc, ctx, tag):
    taken = []

    def make(name):
        taken.append(nc.alloc_semaphore(name=tag + name))
        return taken[-1]

    ctx.callback(nc.all_engine_barrier)
    ctx.callback(nc.clear_and_free_semaphores, taken)
    return make

P=128; S=2048; H=16; HD=8; QB=512; NT=S//P
GROUPS_Q="hhmmhl"; GROUPS_K="hmhmlh"
NROW=48; CROWS=16; MROW=52
NEG=-3.0e38

def pieces():
    return [(i,k,min(QB,P*(i+1)-k)) for i in range(NT) for k in range(0,P*(i+1),QB)]
PIECES=pieces()
N_PIECE=len(PIECES)
A_TILES=12
A_LAST=sum(1 for i,_,_ in PIECES if i<A_TILES)
def slot_items(first):
    out=[]
    for n in range(N_PIECE):
        if n==6 and not first: out.append(("turn_b",None))
        if n==A_LAST+6: out.append(("turn_a",None))
        out.append(("piece",n))
    return out
N_ITEM=N_PIECE+2
P1_BANKS=3
ITEM_PRICE=64
LAG=-0.04
def item_count(n,k):
    return k if isinstance(n,int) and n==0 else n*N_ITEM-1+k
def item_bank(first,k): return (k if first else k+N_ITEM-1)%P1_BANKS
def groups():
    out=[]
    for c in range(S//QB):
        for j in range(0,4*c+4,2):
            out.append((c,[(t,max(0,P*(t-4*c))) for t in (j,j+1)]))
    return out
GROUPS=groups(); N_GROUP=len(GROUPS)
N_PAIR=N_GROUP//2
PAIRS_DONE=[sum(c+1 for c in range(b+1)) for b in range(4)]
def group_cols(g):
    (_, ts)=GROUPS[g]
    w=[QB-f for _,f in ts]
    return [0,w[0]], w, sum(w)

EARLY=H-3

def load_parts(sp, o_dram, strips, sums, h0, h1, signal):
    rows=slice(HD*h0,HD*h1)
    for g in range(4):
        signal(sp.dma_start(sums[rows,g,:],o_dram[h0:h1,g,HD,:].rearrange("h (e s) -> h e s",e=8)),None)
    for g in range(4):
        signal(sp.dma_start(strips[rows,g,:],o_dram[h0:h1,g,0:HD,:]),g)

def attention(nc, tag, q_rows, k_rows, q_const, k_const, v_all, ident, mask_q, mask_k, o_dram, strips, sums):
    with ExitStack() as ctx:
        sb=lambda n,s,d: ctx.enter_context(nc.sbuf_tensor(tag+n,s,d))
        sem=cleared_semaphores(nc, ctx, tag)
        ps=lambda n,s,d: ctx.enter_context(nc.psum_tensor(tag+n,s,d))
        qb=sb("qb",[P,3,S],BF16); kb=sb("kb",[P,3,S],BF16)
        vb=sb("vb",[P,3,NT,32],F32)
        probs=sb("probs",[P,4,2*QB],F32)
        o_sb=sb("o_sb",[P,3,S],F32)
        pmax=sb("pmax",[P,NT,4],F32)
        negmax=sb("negmax",[P,NT],F32)
        zeros=sb("zeros",[P,QB],BF16)
        nothing=sb("nothing",[P,A_TILES],F32)
        split_a=sb("split_a",[P,2,A_TILES],BF16); split_b=sb("split_b",[P,2,NT-A_TILES],BF16)
        turned_a=sb("turned_a",[2*A_TILES,P],BF16); turned_b=sb("turned_b",[2*(NT-A_TILES),P],BF16)
        p1=ps("p1",[P,P1_BANKS,QB],F32)
        s2=ps("s2",[P,2,2*QB],F32)
        acc=ps("acc",[P,QB],F32)
        s_load=[sem(f"heads_loaded{i}") for i in range(3)]
        s_zero=sem("buffers_zeroed"); s_pmax=sem("pmax_set"); s_item=sem("p1_filled"); s_free=sem("p1_read")
        s_nm=sem("negmax_ready"); s_split=sem("negmax_split") 
        s_ma=sem("max_rows_a"); s_mb=sem("max_rows_b")
        s_scores=sem("scores_ready"); s_exp=sem("probs_ready"); s_pv=sem("pv_done"); s_evac=sem("out_copied")
        s_out=sem("out_stored"); s_v=sem("v_ready"); s_early=sem("first_heads_back")
        block=ctx.enter_context(nc.Block())
        A=A_TILES; B=NT-A_TILES
        BIAS=2
        def turned(n,part):
            if part=="b": return item_count_next(n,6 if not (isinstance(n,int) and n==H-1) else 0)+1
            first=isinstance(n,int) and n==0
            return item_count(n,[k for k,_ in slot_items(first)].index("turn_a"))+1
        def item_count_next(n,k): return (n+1)*N_ITEM-1+k
        def last_pair(n): return BIAS+(n+1)*N_PAIR

        @block.sync
        def _(sp):
            def load(n,u):
                for dst,rows,const in ((kb,k_rows,k_const),(qb,q_rows,q_const)):
                    sp.dma_start(dst[0:NROW,u,:],rows[bass.ds(n,1)].rearrange("o r s -> (o r) s")).then_inc(s_load[u],16)
                    sp.dma_start(dst[NROW:NROW+CROWS,u,:],const(n)).then_inc(s_load[u],16)
            def max_rows(n,u,part):
                t0,t1,src,s_m=(0,A,turned_a,s_ma) if part=="a" else (A,NT,turned_b,s_mb)
                sp.wait_ge(s_free,turned(n,part))
                for j in range(2):
                    sp.dma_start(qb[MROW+j:MROW+j+1,u,t0*P:t1*P],
                                 src[j*(t1-t0):(j+1)*(t1-t0),:]).then_inc(s_m,16)
            def store(n,u):
                sp.wait_ge(s_evac,1+4*n+4)
                for g in range(4):
                    sp.dma_start(o_dram[bass.ds(n,1),g,:,:].rearrange("o r s -> (o r) s"),
                                 o_sb[32*g:32*g+9,u,:]).then_inc(s_out,16)
            def slot(n,u):
                max_rows(n-1,(u+2)%3,"b")
                store(n-2,(u+1)%3)
                sp.wait_ge(s_out,64*(n-1))
                load(n+1,(u+1)%3)
                max_rows(n,u,"a")
            load(0,0); load(1,1)
            sp.wait_ge(s_zero,5)
            max_rows(0,0,"a")
            load(2,2)
            max_rows(0,0,"b")
            max_rows(1,1,"a")
            slot(2,2)
            with sp.Fori(1,(H-1)//3) as it:
                for j in range(3): slot(it*3+j,j)
            max_rows(H-2,2,"b")
            sp.wait_ge(s_out,64*EARLY)
            load_parts(sp,o_dram,strips,sums,0,EARLY,lambda dma,g: dma.then_inc(s_early,16))
            store(H-3,1)
            max_rows(H-1,0,"a")
            max_rows(H-1,0,"b")
            store(H-2,2); store(H-1,0)
            sp.wait_ge(s_out,64*H)
            sp.wait_ge(s_early,16*8)

        @block.gpsimd
        def _(pool):
            def split(n,part):
                t0,t1,dst,w=(0,A,split_a,2*n+1) if part=="a" else (A,NT,split_b,2*n+2)
                pool.wait_ge(s_nm,w)
                if not(isinstance(n,int) and n==0): pool.wait_ge(s_free,turned(n-1,part))
                pool.tensor_tensor(dst[:,0,:],negmax[:,t0:t1],nothing[:,0:t1-t0],ALU.add).then_inc(s_split,1)
                pool.wait_ge(s_split,2*w-1)
                pool.tensor_tensor(dst[:,1,:],negmax[:,t0:t1],dst[:,0,:],ALU.subtract).then_inc(s_split,1)
            def v_copy(n,u):
                pool.wait_ge(s_zero,5)
                if not(isinstance(n,int) and n<3): pool.wait_ge(s_pv,last_pair(n-3))
                pool.tensor_copy(vb[:,u,:,0:HD],v_all[:,:,bass.ds(n*HD,HD)]).then_inc(s_v,1)
            pool.memset(nothing[:],0.0).then_inc(s_zero,1)
            pool.wait_ge(s_zero,1)
            pool.memset(qb[64:128,:,:],0.0).then_inc(s_zero,1)
            pool.wait_ge(s_zero,2)
            pool.memset(kb[64:128,:,:],0.0).then_inc(s_zero,1)
            pool.wait_ge(s_zero,3)
            pool.memset(vb[:],0.0).then_inc(s_zero,1)
            pool.wait_ge(s_zero,4)
            pool.memset(vb[:,:,:,HD:HD+1],1.0).then_inc(s_zero,1)
            pool.wait_ge(s_zero,5)
            pool.memset(zeros[:],0.0).then_inc(s_zero,1)
            pool.wait_ge(s_zero,6)
            def slot(n,u):
                v_copy(n,u)
                split(n,"a"); split(n,"b")
            slot(0,0); slot(1,1); slot(2,2)
            with pool.Fori(1,(H-1)//3) as it:
                for j in range(3): slot(it*3+j,j)
            slot(H-1,0)

        @block.vector
        def _(dve):
            dve.memset(pmax[:],NEG).then_inc(s_pmax,1)
            dve.wait_ge(s_pmax,1)
            def items(n,first=False):
                for k,(kind,x) in enumerate(slot_items(first)):
                    at=item_count(n,k); bank=item_bank(first,k)
                    if kind=="piece":
                        i,k0,w=PIECES[x]
                        dve.wait_ge(s_item,at+1)
                        dve.tensor_reduce(pmax[:,i,k0//QB:k0//QB+1],p1[:,bank,0:w],AX.X,ALU.max).then_inc(s_free,1)
                        if x==A_LAST-1: negate(n,"a",at)
                        if x==N_PIECE-1: negate(n,"b",at)
                    elif kind=="turn_a": copy_turned(n,"a",bank,at)
                    else: copy_turned(n-1,"b",bank,at)
            def copy_turned(n,part,bank,at):
                dst,w=(turned_a,2*A) if part=="a" else (turned_b,2*B)
                dve.wait_ge(s_item,at+1)
                dve.tensor_copy(dst[:,:],p1[:,bank,:].bitcast(BF16)[0:w,0:P]).then_inc(s_free,1)
            def negate(n,part,at):
                t0,t1=(0,A) if part=="a" else (A,NT)
                dve.wait_ge(s_free,at+1)
                if not(isinstance(n,int) and n==0): dve.wait_ge(s_split,4*n)
                dve.tensor_reduce(negmax[:,t0:t1],pmax[:,t0:t1,:],AX.X,ALU.max,negate=True).then_inc(s_nm,1)
            items(0,True)
            with dve.Fori(0,(H-1)//3) as it:
                for j in range(3): items(it*3+(1+j))
            copy_turned(H-1,"b",item_bank(False,0),item_count(H,0))

        @block.scalar
        def _(act):
            act.sem_inc(s_exp,BIAS)
            act.sem_inc(s_evac,1)
            def exp(m,g):
                _,_,w=group_cols(g)
                act.wait_ge(s_scores,m*N_GROUP+g+1)
                act.wait_ge(s_pv,BIAS+m*N_PAIR+g//2-1)
                act.activation(probs[:,g%4,0:w],s2[:,g%2,0:w],ACT.Exp).then_inc(s_exp,1)
            def evac(m,u,c):
                act.wait_ge(s_pv,BIAS+m*N_PAIR+PAIRS_DONE[c])
                act.activation(o_sb[:,u,QB*c:QB*c+QB],acc[:,:],ACT.Copy).then_inc(s_evac,1)
            def body(m,u,more=True):
                for g in range(2,N_GROUP):
                    exp(m,g)
                    if g%2 and g//2 in PAIRS_DONE: evac(m,u,PAIRS_DONE.index(g//2))
                if more: exp(m+1,0); exp(m+1,1)
                evac(m,u,3)
            exp(0,0); exp(0,1)
            with act.Fori(0,(H-1)//3) as it:
                for j in range(3): body(it*3+j,j)
            body(H-1,0,False)

        @block.tensor
        def _(pe):
            pe.sem_inc(s_pv,BIAS)
            def item(n,u,k,kind,x,first):
                at=item_count(n,k); bank=item_bank(first,k)
                if not(first and k<P1_BANKS): pe.wait_ge(s_free,at+1-P1_BANKS)
                if kind=="piece":
                    i,k0,w=PIECES[x]
                    diagonal=k0+w==P*(i+1)
                    mm=pe.matmul(p1[:,bank,0:w],qb[:,u,i*P:(i+1)*P],kb[:,u,k0:k0+w],start=True,stop=True)
                    if diagonal: mm=pe.matmul(p1[:,bank,w-P:w],ident[:,:],mask_q[:,:],start=False,stop=True,skip_group_check=True)
                    mm.then_inc(s_item,1)
                elif kind=="turn_a": turn(n,"a",bank)
                else: turn(n-1,"b",bank)
            def turn(n,part,bank):
                src,w,t=(split_a,2*A,4*n+2) if part=="a" else (split_b,2*B,4*n+4)
                pe.wait_ge(s_split,t)
                pe.transpose(p1[:,bank,:].bitcast(BF16)[0:w,0:P],src[:,:,:].rearrange("p a t -> p (a t)"),ident[:,:]).then_inc(s_item,1)
            def scores(m,u,g):
                c,ts=GROUPS[g]
                at,w,_=group_cols(g)
                if g==0: pe.wait_ge(s_ma,32*m+32)
                if c==3 and GROUPS[g-1][0]==2: pe.wait_ge(s_mb,32*m+32)
                pe.wait_ge(s_exp,BIAS+m*N_GROUP+g-1)
                for (t,f),a,n in zip(ts,at,w):
                    diagonal=t>=4*c
                    mm=pe.matmul(s2[:,g%2,a:a+n],kb[:,u,t*P:(t+1)*P],qb[:,u,c*QB+f:(c+1)*QB],start=True,stop=True)
                    if diagonal: mm=pe.matmul(s2[:,g%2,a:a+P],ident[:,:],mask_k[:,:],start=False,stop=True,skip_group_check=True)
                mm.then_inc(s_scores,1)
            def pv(m,u,p):
                c=GROUPS[2*p][0]
                first=p==0 or GROUPS[2*p-1][0]!=c
                if p==0: pe.wait_ge(s_v,m+1)
                pe.wait_ge(s_exp,BIAS+m*N_GROUP+2*p+2)
                if first: pe.wait_ge(s_evac,1+4*m+c)
                if p==0: pe.matmul(acc[:,:],zeros[:,0:P],zeros[:,:],start=True,stop=True)
                for g in (2*p,2*p+1):
                    at,w,_=group_cols(g)
                    for j,(t,f) in enumerate(GROUPS[g][1]):
                        strip=32*(t%4)
                        st=c>0 and t<4; last=t>=4*c
                        mm=pe.matmul(acc[strip:strip+32,f:QB],vb[:,u,t,:],probs[:,g%4,at[j]:at[j]+w[j]],
                                     start=st,stop=last,skip_group_check=True)
                mm.then_inc(s_pv,1)
            def body(m,u,more=True):
                un=(u+1)%3
                todo=[(m+1,un,k,kind,x) for k,(kind,x) in enumerate(slot_items(False))] if more else []
                steps=[]
                for s in range(2,N_GROUP+2):
                    if s<N_GROUP: steps.append((group_cols(s)[2],scores,(m,u,s)))
                    elif more: steps.append((group_cols(s-N_GROUP)[2],scores,(m+1,un,s-N_GROUP)))
                    if s%2:
                        p=(s-3)//2
                        steps.append((4*QB,pv,(m,u,p)))
                    if s==2 and not more: steps.append((0,last_turn,()))
                work=lambda kind,x: PIECES[x][2]+ITEM_PRICE if kind=="piece" else ITEM_PRICE+P
                share=1/sum(work(t[3],t[4]) for t in todo) if todo else 0
                total=sum(w for w,_,_ in steps)
                mine=theirs=0
                for w,step,args in steps:
                    step(*args)
                    mine+=w/total
                    while todo and theirs<mine-LAG:
                        theirs+=share*work(todo[0][3],todo[0][4])
                        item(*todo.pop(0),False)
                for t in todo: item(*t,False)
            def last_turn():
                k=item_count(H,0)
                pe.wait_ge(s_free,k+1-P1_BANKS)
                turn(H-1,"b",item_bank(False,0))
            for u in range(1): pe.wait_ge(s_load[u],64)
            pe.wait_ge(s_zero,6)
            for k,(kind,x) in enumerate(slot_items(True)): item(0,0,k,kind,x,True)
            scores(0,0,0); scores(0,0,1)
            with pe.Fori(0,(H-1)//3) as it:
                for j in range(3):
                    pe.wait_ge(s_load[(j+1)%3],it*64+64*((j+1)//3+1))
                    body(it*3+j,j)
            body(H-1,0,False)


NB = S // QB
D = P
EPS = 1e-5


def layer_norms(nc, tag, c, norms):
    with ExitStack() as ctx:
        sb = lambda n, s: ctx.enter_context(nc.sbuf_tensor(tag + n, s, F32))
        ps = lambda n, s: ctx.enter_context(nc.psum_tensor(tag + n, s, F32))
        sem = cleared_semaphores(nc, ctx, tag)
        centred = sb("centred", [P, 4, QB])
        squares = sb("squares", [P, 2, QB])
        deviation = sb("deviation", [P, 2, 4])
        rstd = sb("rstd", [P, 2, 4])
        diagonal = sb("diagonal", [P, 2, QB])
        scaled = sb("scaled", [P, 2, QB])
        mean_ps = ps("mean_ps", [P, 2, QB])
        var_ps = ps("var_ps", [P, 2, QB])
        bcast_ps = ps("bcast_ps", [P, 2, QB])
        s_mean = sem("mean_ready"); s_cent = sem("centred"); s_sq = sem("squared"); s_var = sem("var_ready")
        s_dev = sem("deviation_ready"); s_rstd = sem("rstd_ready"); s_diag = sem("diagonal_ready")
        s_bc = sem("rstd_broadcast"); s_mul = sem("scaled"); s_out = sem("normed")
        n_all = NB * len(norms)
        at = lambda i: (norms[i // NB], slice(i % NB * QB, (i % NB + 1) * QB))
        block = ctx.enter_context(nc.Block())

        @block.tensor
        def _(pe):
            for t in range(n_all + 2):
                if t < n_all:
                    i = t
                    (src, _, _, _), cols = at(i)
                    if i >= NB: pe.wait_ge(s_out, i - NB + 1)
                    if i >= 2: pe.wait_ge(s_cent, i - 1)
                    pe.matmul(mean_ps[:, i % 2, :], c.averages[:, :], src[:, cols], start=True, stop=True).then_inc(s_mean, 1)
                if 1 <= t <= n_all:
                    i = t - 1
                    pe.wait_ge(s_sq, i + 1)
                    if i >= 2: pe.wait_ge(s_dev, i - 1)
                    for k in range(4):
                        mm = pe.matmul(var_ps[:, i % 2, k:k + 1], squares[:, i % 2, k * P:(k + 1) * P],
                                       c.averages[:, 0:1], start=True, stop=True)
                    mm.then_inc(s_var, 1)
                if t >= 2:
                    i = t - 2
                    pe.wait_ge(s_diag, i + 1)
                    if i >= 2: pe.wait_ge(s_mul, i - 1)
                    pe.matmul(bcast_ps[:, i % 2, :], c.ones[:, :], diagonal[:, i % 2, :], start=True, stop=True).then_inc(s_bc, 1)

        @block.vector
        def _(dve):
            for t in range(n_all + 2):
                if t < n_all:
                    i = t
                    (src, _, _, _), cols = at(i)
                    dve.wait_ge(s_mean, i + 1)
                    if i >= 4: dve.wait_ge(s_sq, i - 3)
                    dve.tensor_tensor(centred[:, i % 4, :], src[:, cols], mean_ps[:, i % 2, :], ALU.subtract).then_inc(s_cent, 1)
                if 1 <= t <= n_all:
                    i = t - 1
                    dve.wait_ge(s_dev, i + 1)
                    dve.reciprocal(rstd[:, i % 2, :], deviation[:, i % 2, :]).then_inc(s_rstd, 1)
                    dve.wait_ge(s_rstd, i + 1)
                    if i >= 2: dve.wait_ge(s_bc, i - 1)
                    for k in range(4):
                        ins = dve.tensor_scalar(diagonal[:, i % 2, k * P:(k + 1) * P], c.ident[:, :],
                                                rstd[:, i % 2, k:k + 1], None, ALU.mult)
                    ins.then_inc(s_diag, 1)
                if t >= 2:
                    i = t - 2
                    dve.wait_ge(s_bc, i + 1)
                    if i >= 2: dve.wait_ge(s_out, i - 1)
                    dve.tensor_tensor(scaled[:, i % 2, :], centred[:, i % 4, :], bcast_ps[:, i % 2, :], ALU.mult).then_inc(s_mul, 1)

        @block.scalar
        def _(act):
            for t in range(n_all + 2):
                if t < n_all:
                    i = t
                    act.wait_ge(s_cent, i + 1)
                    if i >= 2: act.wait_ge(s_var, i - 1)
                    act.activation(squares[:, i % 2, :], centred[:, i % 4, :], ACT.Square).then_inc(s_sq, 1)
                if 1 <= t <= n_all:
                    i = t - 1
                    act.wait_ge(s_var, i + 1)
                    act.activation(deviation[:, i % 2, :], var_ps[:, i % 2, 0:4], ACT.Sqrt, bias=c.eps).then_inc(s_dev, 1)
                if t >= 2:
                    i = t - 2
                    (_, dst, scale, bias), cols = at(i)
                    act.wait_ge(s_mul, i + 1)
                    act.activation(dst[:, cols], scaled[:, i % 2, :], ACT.Identity, scale=scale, bias=bias).then_inc(s_out, 1)


def qkv(nc, tag, c, src, weights, q_bias, k_bias, v_all, q_rows, k_rows):
    with ExitStack() as ctx:
        sb = lambda n, s, d: ctx.enter_context(nc.sbuf_tensor(tag + n, s, d))
        sem = cleared_semaphores(nc, ctx, tag)
        full = sb("full", [P, 2, QB], F32)
        rest = sb("rest", [P, 2, QB], F32)
        parts = {k: sb("part_" + k, [P, 2, S], BF16) for k in "hml"}
        qk_ps = ctx.enter_context(nc.psum_tensor(tag + "qk_ps", [P, 2, QB], F32))
        v_ps = ctx.enter_context(nc.psum_tensor(tag + "v_ps", [P, 2, QB], F32))
        s_qk = sem("qk_ready"); s_full = sem("full_ready"); s_high = sem("high_ready"); s_rest = sem("rest_ready")
        s_mid = sem("mid_ready"); s_low = sem("low_ready"); s_v = sem("v_ready"); s_vcopy = sem("v_copied"); s_store = sem("rows_stored")
        units = [(w, b) for w in range(2) for b in range(NB)]
        block = ctx.enter_context(nc.Block())

        @block.tensor
        def _(pe):
            for i, (w, b) in enumerate(units):
                if i >= 2: pe.wait_ge(s_full, i - 1)
                pe.matmul(qk_ps[:, i % 2, :], weights[:, w * D:(w + 1) * D], src[:, b * QB:(b + 1) * QB],
                          start=True, stop=True).then_inc(s_qk, 1)
                if i % 2:
                    v = i // 2
                    if v >= 2: pe.wait_ge(s_vcopy, v - 1)
                    for k in range(4):
                        t = 4 * v + k
                        mm = pe.matmul(v_ps[:, v % 2, k * D:(k + 1) * D], src[:, t * P:(t + 1) * P],
                                       weights[:, 2 * D:3 * D], start=True, stop=True)
                    mm.then_inc(s_v, 1)

        @block.vector
        def _(dve):
            for i, (w, b) in enumerate(units):
                dve.wait_ge(s_qk, i + 1)
                if i >= 2: dve.wait_ge(s_rest, i - 1)
                dve.tensor_scalar(full[:, i % 2, :], qk_ps[:, i % 2, :], q_bias if w == 0 else k_bias,
                                  HD ** -0.5 if w == 0 else 1.0, ALU.add, ALU.mult).then_inc(s_full, 1)
                dve.wait_ge(s_high, i + 1)
                if i >= 2: dve.wait_ge(s_low, i - 1)
                dve.tensor_tensor(rest[:, i % 2, :], full[:, i % 2, :], parts["h"][:, w, b * QB:(b + 1) * QB],
                                  ALU.subtract).then_inc(s_rest, 1)

        @block.scalar
        def _(act):
            for i, (w, b) in enumerate(units):
                cols = slice(b * QB, (b + 1) * QB)
                act.wait_ge(s_full, i + 1)
                act.activation(parts["h"][:, w, cols], full[:, i % 2, :], ACT.Copy).then_inc(s_high, 1)
                if i % 2:
                    v = i // 2
                    act.wait_ge(s_v, v + 1)
                    act.activation(v_all[:, 4 * v:4 * v + 4, :], v_ps[:, v % 2, :].rearrange("p (t d) -> p t d", t=4),
                                   ACT.Copy).then_inc(s_vcopy, 1)
                act.wait_ge(s_rest, i + 1)
                act.activation(parts["m"][:, w, cols], rest[:, i % 2, :], ACT.Copy).then_inc(s_mid, 1)

        @block.gpsimd
        def _(pool):
            for i, (w, b) in enumerate(units):
                cols = slice(b * QB, (b + 1) * QB)
                pool.wait_ge(s_mid, i + 1)
                if i: pool.wait_ge(s_low, i)
                pool.tensor_tensor(parts["l"][:, w, cols], rest[:, i % 2, :], parts["m"][:, w, cols],
                                   ALU.subtract).then_inc(s_low, 1)

        @block.sync
        def _(sp):
            for w, (rows, groups) in enumerate(((q_rows, GROUPS_Q), (k_rows, GROUPS_K))):
                for kind, s in (("h", s_high), ("m", s_mid), ("l", s_low)):
                    sp.wait_ge(s, NB * (w + 1))
                    for g, part in enumerate(groups):
                        if part == kind:
                            sp.dma_start(rows[:, g * HD:(g + 1) * HD, :], parts[kind][:, w, :]).then_inc(s_store, 16)
            sp.wait_ge(s_store, 16 * 12)


def attention_out(nc, tag, c, o_dram, strips, sums, rden_dram, weights, v_bias, out_bias, ctx_out, gain, base, dst):
    with ExitStack() as ctx:
        sb = lambda n, s, d=F32: ctx.enter_context(nc.sbuf_tensor(tag + n, s, d))
        sem = cleared_semaphores(nc, ctx, tag)
        total = sb("total", [P, S // 8])
        inverse = sb("inverse", [P, S // 8])
        inverse_rows = sb("inverse_rows", [H, S])
        bias = sb("bias", [P, 1])
        bcast_ps = ctx.enter_context(nc.psum_tensor(tag + "bcast_ps", [P, 2, QB], F32))
        out_ps = ctx.enter_context(nc.psum_tensor(tag + "out_ps", [P, 2, QB], F32))
        bias_ps = ctx.enter_context(nc.psum_tensor(tag + "bias_ps", [P, QB], F32))
        s_sums = sem("sums_loaded"); s_strips = [sem(f"strips_loaded{i}") for i in range(4)]
        s_step = sem("sums_step"); s_inv = sem("inverse_stored"); s_rows = sem("inverse_rows_loaded")
        s_half = sem("half_summed"); s_add = sem("strips_summed"); s_bc = sem("inverse_broadcast"); s_norm = sem("divided")
        s_bias_ps = sem("bias_product"); s_bias = sem("bias_ready"); s_out = sem("projected"); s_ctx = sem("ctx_written"); s_dst = sem("dst_written")
        block = ctx.enter_context(nc.Block())

        @block.sync
        def _(sp):
            load_parts(sp, o_dram, strips, sums, EARLY, H, lambda dma, g: dma.then_inc(s_sums if g is None else s_strips[g], 16))
            sp.wait_ge(s_step, 4)
            sp.dma_start(rden_dram.rearrange("h (e s) -> (h e) s", e=8), inverse[:, :]).then_inc(s_inv, 16)
            sp.wait_ge(s_inv, 16)
            sp.dma_start(inverse_rows[:, :], rden_dram).then_inc(s_rows, 16)

        @block.gpsimd
        def _(pool):
            pool.wait_ge(s_strips[2], 16)
            pool.wait_ge(s_strips[3], 16)
            pool.tensor_tensor(strips[:, 2, :], strips[:, 2, :], strips[:, 3, :], ALU.add).then_inc(s_half, 1)

        @block.vector
        def _(dve):
            dve.wait_ge(s_sums, 64)
            dve.tensor_tensor(total[:, :], sums[:, 0, :], sums[:, 1, :], ALU.add).then_inc(s_step, 1)
            for g in (2, 3):
                dve.wait_ge(s_step, g - 1)
                dve.tensor_tensor(total[:, :], total[:, :], sums[:, g, :], ALU.add).then_inc(s_step, 1)
            dve.wait_ge(s_step, 3)
            dve.reciprocal(inverse[:, :], total[:, :]).then_inc(s_step, 1)
            dve.wait_ge(s_bias_ps, 1)
            dve.tensor_tensor(bias[:, :], bias_ps[:, 0:1], out_bias, ALU.add).then_inc(s_bias, 1)
            dve.wait_ge(s_strips[0], 16)
            dve.wait_ge(s_strips[1], 16)
            dve.tensor_tensor(strips[:, 0, :], strips[:, 0, :], strips[:, 1, :], ALU.add).then_inc(s_add, 1)
            dve.wait_ge(s_add, 1)
            dve.wait_ge(s_half, 1)
            dve.tensor_tensor(strips[:, 0, :], strips[:, 0, :], strips[:, 2, :], ALU.add).then_inc(s_add, 1)
            dve.wait_ge(s_add, 2)
            for b in range(NB + 1):
                if b < NB:
                    cols = slice(b * QB, (b + 1) * QB)
                    dve.wait_ge(s_bc, b + 1)
                    dve.tensor_tensor(strips[:, 1, cols], strips[:, 0, cols], bcast_ps[:, b % 2, :], ALU.mult).then_inc(s_norm, 1)
                if b:
                    cols = slice((b - 1) * QB, b * QB)
                    dve.wait_ge(s_ctx, b)
                    dve.scalar_tensor_tensor(out=dst[:, cols], in0=ctx_out[:, cols], scalar=gain, in1=base[:, cols],
                                             op0=ALU.mult, op1=ALU.add).then_inc(s_dst, 1)

        @block.scalar
        def _(act):
            act.wait_ge(s_bias, 1)
            for b in range(NB):
                act.wait_ge(s_out, b + 1)
                act.activation(ctx_out[:, b * QB:(b + 1) * QB], out_ps[:, b % 2, :], ACT.Identity, bias=bias[:, 0:1]).then_inc(s_ctx, 1)

        @block.tensor
        def _(pe):
            pe.matmul(bias_ps[:, 0:1], weights[:, :], v_bias, start=True, stop=True).then_inc(s_bias_ps, 1)
            pe.wait_ge(s_rows, 16)
            for b in range(NB + 1):
                if b < NB:
                    if b >= 2: pe.wait_ge(s_norm, b - 1)
                    pe.matmul(bcast_ps[:, b % 2, :], c.spread_heads[0:H, :], inverse_rows[:, b * QB:(b + 1) * QB],
                              start=True, stop=True).then_inc(s_bc, 1)
                if b:
                    pe.wait_ge(s_norm, b)
                    if b >= 3: pe.wait_ge(s_ctx, b - 2)
                    pe.matmul(out_ps[:, (b - 1) % 2, :], weights[:, :], strips[:, 1, (b - 1) * QB:b * QB],
                              start=True, stop=True).then_inc(s_out, 1)


def liquid(nc, tag, c, ctx_in, w_ctx, w_x, bias, xs, x2, dst):
    STEPS = 8
    with ExitStack() as ctx:
        sb = lambda n, s: ctx.enter_context(nc.sbuf_tensor(tag + n, s, F32))
        sem = cleared_semaphores(nc, ctx, tag)
        drive = sb("drive", [P, S])
        change = sb("change", [P, 2, QB])
        u_ps = ctx.enter_context(nc.psum_tensor(tag + "u_ps", [P, NB, QB], F32))
        v_ps = ctx.enter_context(nc.psum_tensor(tag + "v_ps", [P, NB, QB], F32))
        s_drive_ps = sem("drive_product"); s_drive = sem("drive_ready"); s_zero = sem("v_zeroed")
        s_pre = sem("before_tanh"); s_u = sem("u_ready"); s_change = sem("change_ready"); s_v = sem("v_ready"); s_xs = sem("xs_ready")
        block = ctx.enter_context(nc.Block())

        @block.tensor
        def _(pe):
            for b in range(NB):
                mm = pe.matmul(u_ps[:, b, :], w_ctx[:, :], ctx_in[:, b * QB:(b + 1) * QB], start=True, stop=True)
                mm.then_inc(s_drive_ps, 1)
            with pe.Fori(0, STEPS) as n:
                for b in range(NB):
                    cols = slice(b * QB, (b + 1) * QB)
                    pe.wait_ge(s_xs, n * NB + b + 1)
                    pe.matmul(u_ps[:, b, :], c.ident[:, :], drive[:, cols], start=True, stop=False)
                    pe.matmul(u_ps[:, b, :], w_x[:, :], xs[:, cols], start=False, stop=True).then_inc(s_pre, 1)

        @block.scalar
        def _(act):
            for b in range(NB):
                act.wait_ge(s_drive_ps, b + 1)
                act.activation(drive[:, b * QB:(b + 1) * QB], u_ps[:, b, :], ACT.Identity, bias=bias).then_inc(s_xs, 1)
            with act.Fori(0, STEPS) as n:
                for b in range(NB):
                    act.wait_ge(s_pre, n * NB + b + 1)
                    act.activation(u_ps[:, b, :], u_ps[:, b, :], ACT.Tanh).then_inc(s_u, 1)

        @block.vector
        def _(dve):
            dve.memset(v_ps[:, :, :], 0.0).then_inc(s_zero, 1)
            dve.wait_ge(s_zero, 1)
            with dve.Fori(0, STEPS) as n:
                for b in range(NB):
                    cols = slice(b * QB, (b + 1) * QB)
                    dve.wait_ge(s_u, n * NB + b + 1)
                    dve.tensor_tensor(change[:, b % 2, :], u_ps[:, b, :], xs[:, cols], ALU.subtract).then_inc(s_change, 1)
                    dve.wait_ge(s_change, n * NB + b + 1)
                    dve.scalar_tensor_tensor(out=v_ps[:, b, :], in0=v_ps[:, b, :], scalar=0.9, in1=change[:, b % 2, :],
                                             op0=ALU.mult, op1=ALU.add).then_inc(s_v, 1)
                    dve.wait_ge(s_v, n * NB + b + 1)
                    dve.scalar_tensor_tensor(out=xs[:, cols], in0=v_ps[:, b, :], scalar=0.01, in1=xs[:, cols],
                                             op0=ALU.mult, op1=ALU.add).then_inc(s_xs, 1)
            dve.wait_ge(s_xs, (STEPS + 1) * NB)
            dve.tensor_tensor(dst[:, :], x2[:, :], xs[:, :], ALU.add).then_inc(s_zero, 1)


def gelu_ffn(nc, tag, c, src, w1, b1, w2, b2, base, gain, x):
    F = 4
    with ExitStack() as ctx:
        sb = lambda n, s: ctx.enter_context(nc.sbuf_tensor(tag + n, s, F32))
        sem = cleared_semaphores(nc, ctx, tag)
        hidden = sb("hidden", [P, 2 * F, QB])
        total = sb("total", [P, 2, QB])
        h_ps = ctx.enter_context(nc.psum_tensor(tag + "h_ps", [P, F, QB], F32))
        o_ps = ctx.enter_context(nc.psum_tensor(tag + "o_ps", [P, 2, QB], F32))
        s_h = sem("h_ready"); s_g = sem("gelu_ready"); s_o = sem("o_ready"); s_total = sem("total_ready"); s_x = sem("x_ready")
        block = ctx.enter_context(nc.Block())

        @block.tensor
        def _(pe):
            for b in range(NB + 1):
                if b < NB:
                    for f in range(F):
                        if b: pe.wait_ge(s_g, F * (b - 1) + f + 1)
                        pe.matmul(h_ps[:, f, :], w1[:, f * P:(f + 1) * P], src[:, b * QB:(b + 1) * QB],
                                  start=True, stop=True).then_inc(s_h, 1)
                if b:
                    n = b - 1
                    if n >= 2: pe.wait_ge(s_total, n - 1)
                    pe.wait_ge(s_g, F * b)
                    for f in range(F):
                        mm = pe.matmul(o_ps[:, n % 2, :], w2[:, f, :], hidden[:, n % 2 * F + f, :],
                                       start=(f == 0), stop=(f == F - 1))
                    mm.then_inc(s_o, 1)

        @block.scalar
        def _(act):
            for b in range(NB):
                if b >= 2: act.wait_ge(s_o, b - 1)
                for f in range(F):
                    act.wait_ge(s_h, F * b + f + 1)
                    act.activation(hidden[:, b % 2 * F + f, :], h_ps[:, f, :], ACT.Gelu, bias=b1(f)).then_inc(s_g, 1)

        @block.vector
        def _(dve):
            for b in range(NB):
                cols = slice(b * QB, (b + 1) * QB)
                dve.wait_ge(s_o, b + 1)
                dve.scalar_tensor_tensor(out=total[:, b % 2, :], in0=o_ps[:, b % 2, :], scalar=b2, in1=base[:, cols],
                                         op0=ALU.add, op1=ALU.add).then_inc(s_total, 1)
                dve.wait_ge(s_total, b + 1)
                dve.scalar_tensor_tensor(out=x[:, cols], in0=total[:, b % 2, :], scalar=gain, in1=x[:, cols],
                                         op0=ALU.mult, op1=ALU.add).then_inc(s_x, 1)


def top2_gates(nc, tag, c, src, gate_w, n_experts, rows, rows_bf=None, in_parts=False, token_gates=None):
    E = n_experts
    R = rows.shape[0]
    chosen = rows_bf is not None and not in_parts
    with ExitStack() as ctx:
        sb = lambda n, s, d=F32: ctx.enter_context(nc.sbuf_tensor(tag + n, s, d))
        sem = cleared_semaphores(nc, ctx, tag)
        logits = sb("logits", [P, NT, E])
        best = sb("best", [P, NT, 8])
        index = sb("index", [P, NT, 8], U32)
        index_f = sb("index_f", [P, NT, 2])
        gap = sb("gap", [P, NT]); ratio = sb("ratio", [P, NT]); whole = sb("whole", [P, NT])
        gate = sb("gate", [P, NT, 2]) if token_gates is None else token_gates
        hot = sb("hot", [P, 2, NT, E])
        weighed = sb("weighed", [P, 2, NT, E])
        token = sb("token", [P, NT, R])
        total = sb("total", [P, NT, E]); rest = sb("rest", [P, NT, E]); part = sb("part", [P, 2, NT, E], BF16)
        logit_ps = ctx.enter_context(nc.psum_tensor(tag + "logit_ps", [P, NT, E], F32))
        turn_ps = ctx.enter_context(nc.psum_tensor(tag + "turn_ps", [P, 2, QB], F32))
        s_logit = sem("logits_ready"); s_step = sem("step"); s_gap = sem("gap_ready"); s_ratio = sem("ratio_ready")
        s_token = sem("token_rows_ready"); s_turn = sem("turned"); s_rows = sem("rows_ready")
        block = ctx.enter_context(nc.Block())

        @block.tensor
        def _(pe):
            for t in range(NT):
                mm = pe.matmul(logit_ps[:, t, :], src[:, t * P:(t + 1) * P], gate_w, start=True, stop=True)
            mm.then_inc(s_logit, 1)
            pe.wait_ge(s_token, 1)
            for b in range(NB):
                if b >= 2: pe.wait_ge(s_rows, b - 1)
                for k in range(4):
                    mm = pe.transpose(turn_ps[0:R, b % 2, k * P:(k + 1) * P], token[:, 4 * b + k, :], c.ident[:, :])
                mm.then_inc(s_turn, 1)

        @block.scalar
        def _(act):
            act.wait_ge(s_gap, 1)
            act.activation(ratio[:, :], gap[:, :], ACT.Exp).then_inc(s_ratio, 1)
            for b in range(NB):
                act.wait_ge(s_turn, b + 1)
                if rows_bf is not None: act.activation(rows_bf[:, b * QB:(b + 1) * QB], turn_ps[0:R, b % 2, :], ACT.Copy)
                act.activation(rows[:, b * QB:(b + 1) * QB], turn_ps[0:R, b % 2, :], ACT.Copy).then_inc(s_rows, 1)

        @block.vector
        def _(dve):
            done = [0]

            def link(ins):
                done[0] += 1
                ins.then_inc(s_step, 1)
                dve.wait_ge(s_step, done[0])

            dve.wait_ge(s_logit, 1)
            if chosen:
                dve.memset(token[:, :, :], 0.0).then_inc(s_step, 1)
                done[0] += 1
            link(dve.tensor_copy(logits[:, :, :], logit_ps[:, :, :]))
            for t in range(NT):
                ins = dve.max(best[:, t, :], logits[:, t, :])
            link(ins)
            for t in range(NT):
                ins = dve.max_index(index[:, t, :], best[:, t, :], logits[:, t, :])
            link(ins)
            dve.tensor_tensor(gap[:, :], best[:, :, 1], best[:, :, 0], ALU.subtract).then_inc(s_gap, 1)
            link(dve.tensor_copy(index_f[:, :, :], index[:, :, 0:2]))
            for k in range(2):
                ins = dve.tensor_tensor(hot[:, k, :, :], c.counting[:, 0:E].unsqueeze(1).to_broadcast([P, NT, E]),
                                        index_f[:, :, k].unsqueeze(2).to_broadcast([P, NT, E]), ALU.is_equal)
            link(ins)
            dve.wait_ge(s_ratio, 1)
            link(dve.tensor_scalar(whole[:, :], ratio[:, :], 1.0, None, ALU.add))
            link(dve.reciprocal(gate[:, :, 0], whole[:, :]))
            link(dve.tensor_tensor(gate[:, :, 1], ratio[:, :], gate[:, :, 0], ALU.mult))
            for k in range(2):
                ins = dve.tensor_tensor(weighed[:, k, :, :], hot[:, k, :, :],
                                        gate[:, :, k].unsqueeze(2).to_broadcast([P, NT, E]), ALU.mult)
            link(ins)
            if chosen:
                for k in range(2):
                    dve.tensor_copy(token[:, :, E * (1 + k):E * (2 + k)], hot[:, k, :, :])
                dve.tensor_copy(token[:, :, 3 * E:3 * E + 2], gate[:, :, :])
            if in_parts:
                link(dve.tensor_tensor(total[:, :, :], weighed[:, 0, :, :], weighed[:, 1, :, :], ALU.add))
                link(dve.tensor_copy(part[:, 0, :, :], total[:, :, :]))
                link(dve.tensor_tensor(rest[:, :, :], total[:, :, :], part[:, 0, :, :], ALU.subtract))
                link(dve.tensor_copy(part[:, 1, :, :], rest[:, :, :]))
                for k in range(2):
                    dve.tensor_copy(token[:, :, k * E:(k + 1) * E], part[:, k, :, :])
                dve.tensor_tensor(token[:, :, 2 * E:3 * E], rest[:, :, :], part[:, 1, :, :], ALU.subtract).then_inc(s_token, 1)
            else:
                dve.tensor_tensor(token[:, :, 0:E], weighed[:, 0, :, :], weighed[:, 1, :, :], ALU.add).then_inc(s_token, 1)


EA = 8


def moa_keys(nc, tag, c, src, k_w, k_bias, v_w, v_bias, rel, keys, values):
    with ExitStack() as ctx:
        sem = cleared_semaphores(nc, ctx, tag)
        k_ps = ctx.enter_context(nc.psum_tensor(tag + "k_ps", [P, 2, QB], F32))
        v_ps = ctx.enter_context(nc.psum_tensor(tag + "v_ps", [P, 2, QB], F32))
        s_k = sem("k_ready"); s_copy = sem("k_copied"); s_v = sem("v_ready"); s_vcopy = sem("v_copied"); s_side = sem("sides_ready")
        block = ctx.enter_context(nc.Block())

        @block.tensor
        def _(pe):
            for b in range(NB):
                if b >= 2: pe.wait_ge(s_copy, b - 1)
                pe.matmul(k_ps[:, b % 2, :], k_w, src[:, b * QB:(b + 1) * QB], start=True, stop=True).then_inc(s_k, 1)
                if b >= 2: pe.wait_ge(s_vcopy, b - 1)
                for k in range(4):
                    t = 4 * b + k
                    mm = pe.matmul(v_ps[:, b % 2, k * D:(k + 1) * D], src[:, t * P:(t + 1) * P], v_w, start=True, stop=True)
                mm.then_inc(s_v, 1)

        @block.scalar
        def _(act):
            for b in range(NB):
                act.wait_ge(s_k, b + 1)
                act.activation(keys[:, 1, b * QB:(b + 1) * QB], k_ps[:, b % 2, :], ACT.Identity, bias=k_bias).then_inc(s_copy, 1)

        @block.vector
        def _(dve):
            for b in range(NB):
                cols = slice(b * QB, (b + 1) * QB)
                dve.wait_ge(s_copy, b + 1)
                dve.wait_ge(s_v, b + 1)
                dve.tensor_tensor(values[:, 4 * b:4 * b + 4, :], v_ps[:, b % 2, :].rearrange("p (t d) -> p t d", t=4),
                                  v_bias[:, :].unsqueeze(1).to_broadcast([P, 4, D]), ALU.add).then_inc(s_vcopy, 1)
                dve.tensor_scalar(keys[:, 0, cols], keys[:, 1, cols], rel[:, 0:1], None, ALU.add)
                dve.tensor_scalar(keys[:, 2, cols], keys[:, 1, cols], rel[:, 2 * P - 1:2 * P], None, ALU.add).then_inc(s_side, 1)


def moa_queries(nc, tag, c, src, q_w, q_bias, rows_bf, queries):
    with ExitStack() as ctx:
        sb = lambda n, s: ctx.enter_context(nc.sbuf_tensor(tag + n, s, F32))
        sem = cleared_semaphores(nc, ctx, tag)
        all_q = sb("all_q", [P, 2, QB])
        q_ps = ctx.enter_context(nc.psum_tensor(tag + "q_ps", [P, 2, QB], F32))
        mask_ps = ctx.enter_context(nc.psum_tensor(tag + "mask_ps", [P, 4, QB], F32))
        s_q = sem("q_ready"); s_copy = sem("q_copied"); s_mask = sem("masks_ready"); s_pick = sem("picked")
        units = [(b, e) for b in range(NB) for e in range(EA)]
        block = ctx.enter_context(nc.Block())

        @block.tensor
        def _(pe):
            for i, (b, e) in enumerate(units):
                cols = slice(b * QB, (b + 1) * QB)
                if i >= 2: pe.wait_ge(s_copy, i - 1)
                pe.matmul(q_ps[:, i % 2, :], q_w[:, e, :], src[:, cols], start=True, stop=True).then_inc(s_q, 1)
                if i >= 2: pe.wait_ge(s_pick, 2 * (i - 1))
                for k in range(2):
                    mm = pe.matmul(mask_ps[:, i % 2 * 2 + k, :], c.pick_bf[0:32, EA * (1 + k) + e, :], rows_bf[:, cols], start=True, stop=True)
                mm.then_inc(s_mask, 1)

        @block.scalar
        def _(act):
            for i, (b, e) in enumerate(units):
                act.wait_ge(s_q, i + 1)
                if i >= 2: act.wait_ge(s_pick, 2 * (i - 1))
                act.activation(all_q[:, i % 2, :], q_ps[:, i % 2, :], ACT.Identity, scale=float(D) ** -0.5, bias=q_bias(e)).then_inc(s_copy, 1)

        @block.vector
        def _(dve):
            for i, (b, e) in enumerate(units):
                cols = slice(b * QB, (b + 1) * QB)
                dve.wait_ge(s_copy, i + 1)
                dve.wait_ge(s_mask, i + 1)
                for k in range(2):
                    if e == 0:
                        dve.tensor_tensor(queries[:, k, cols], all_q[:, i % 2, :], mask_ps[:, i % 2 * 2 + k, :], ALU.mult).then_inc(s_pick, 1)
                    else:
                        if k == 0: dve.wait_ge(s_pick, 2 * i)
                        dve.copy_predicated(queries[:, k, cols], mask_ps[:, i % 2 * 2 + k, :].bitcast(U32), all_q[:, i % 2, :]).then_inc(s_pick, 1)


NEAR = 64
WINDOW = P + 2 * NEAR


def moa_near_bias(nc, tag, c, rel, queries, near, band_dram):
    W = 2 * P
    TILES = 2 * NT
    BATCHES = TILES // 4
    with ExitStack() as ctx:
        sb = lambda n, s: ctx.enter_context(nc.sbuf_tensor(tag + n, s, F32))
        sem = cleared_semaphores(nc, ctx, tag)
        band = sb("band", [P, 2, 4, W])
        far = sb("far", [P, TILES, 2])
        band_ps = ctx.enter_context(nc.psum_tensor(tag + "band_ps", [P, 4, QB], F32))
        s_band = sem("band_ready"); s_copy = sem("band_copied"); s_far = sem("far_copied")
        s_store = [sem(f"band_stored{b}") for b in range(BATCHES)]
        s_near = [sem(f"near_loaded{b}") for b in range(BATCHES)]
        s_zero = sem("corners_zeroed"); s_out = sem("near_ready")
        block = ctx.enter_context(nc.Block())

        @block.tensor
        def _(pe):
            for t in range(TILES):
                if t >= 4: pe.wait_ge(s_copy, t - 3)
                pe.matmul(band_ps[:, t % 4, 0:W], queries[:, t // NT, t % NT * P:(t % NT + 1) * P], rel,
                          start=True, stop=True).then_inc(s_band, 1)

        @block.scalar
        def _(act):
            for t in range(TILES):
                act.wait_ge(s_band, t + 1)
                if t % 4 == 0 and t >= 8:
                    act.wait_ge(s_store[t // 4 - 2], 16)
                    act.wait_ge(s_far, t - 4)
                act.activation(band[:, t // 4 % 2, t % 4, :], band_ps[:, t % 4, 0:W], ACT.Copy).then_inc(s_copy, 1)

        @block.sync
        def _(sp):
            def load(b):
                sp.wait_ge(s_store[b], 16)
                for half in range(2):
                    at = 4 * b * P * W + ((W - 1) * NEAR + P if half else P - NEAR)
                    src = bass.AP(band_dram.tensor, at, [[W - 1, NEAR], [P * W, 4], [1, P + NEAR]])
                    sp.dma_start(near[NEAR * half:NEAR * (half + 1), 4 * b:4 * b + 4, NEAR * half:NEAR * half + P + NEAR],
                                 src).then_inc(s_near[b], 16)
            for b in range(BATCHES):
                sp.wait_ge(s_copy, 4 * (b + 1))
                sp.dma_start(band_dram[4 * b:4 * b + 4].rearrange("t p w -> p t w"), band[:, b % 2, :, :]).then_inc(s_store[b], 16)
                if b: load(b - 1)
            load(BATCHES - 1)

        @block.gpsimd
        def _(pool):
            pool.memset(near[0:NEAR, :, P + NEAR:WINDOW], 0.0).then_inc(s_zero, 1)
            pool.wait_ge(s_zero, 1)
            pool.memset(near[NEAR:P, :, 0:NEAR], 0.0).then_inc(s_zero, 1)
            pool.wait_ge(s_zero, 2)

        def side(dve, b):
            dve.wait_ge(s_far, 4 * b + 4)
            dve.wait_ge(s_near[b], 32)
            for t in range(4 * b, 4 * b + 4):
                for rows, cols, k in ((slice(0, NEAR), slice(0, NEAR), 0), (slice(NEAR, P), slice(P + NEAR, WINDOW), 1)):
                    dve.tensor_scalar(near[rows, t, cols], near[rows, t, cols], far[rows, t, k:k + 1], None,
                                      ALU.subtract).then_inc(s_out, 1)

        @block.vector
        def _(dve):
            for t in range(TILES):
                dve.wait_ge(s_copy, t + 1)
                dve.tensor_copy(far[:, t, :], band[:, t // 4 % 2, t % 4, 0:W:W - 1]).then_inc(s_far, 1)
                if t >= 8 and t % 4 == 3: side(dve, t // 4 - 2)
            side(dve, BATCHES - 2)
            side(dve, BATCHES - 1)


def moa_attention(nc, tag, c, keys, values, queries, near, gates, out):
    TILES = 2 * NT
    C = S // QB
    with ExitStack() as ctx:
        sb = lambda n, s, d=F32: ctx.enter_context(nc.sbuf_tensor(tag + n, s, d))
        sem = cleared_semaphores(nc, ctx, tag)
        ps = lambda n, s: ctx.enter_context(nc.psum_tensor(tag + n, s, F32))
        probs = sb("probs", [P, 2, S])
        turned = sb("turned", [P, C, QB])
        pmax = sb("pmax", [P, 2, C]); negmax = sb("negmax", [P, 2])
        sums = sb("sums", [P, 2, C]); total = sb("total", [P, 2]); weight = sb("weight", [P, 2])
        s_ps = ps("s_ps", [P, C, QB]); turn_ps = ps("turn_ps", [P, 2, QB]); acc = ps("acc", [P, 2, QB])
        s_scores = sem("scores_ready"); s_max = sem("piece_maxima"); s_neg = sem("negmax_ready"); s_exp = sem("probs_ready")
        s_step = sem("weight_steps"); s_scaled = sem("probs_scaled"); s_turn = sem("turned")
        s_copy_v = sem("turned_copied_by_vector"); s_copy_a = sem("turned_copied_by_scalar")
        s_pv = sem("pv_done"); s_out = sem("out_ready")
        block = ctx.enter_context(nc.Block())

        def kinds(t, k0, k1):
            cuts = [k0] + [x for x in (t * P, (t + 1) * P) if k0 < x < k1] + [k1]
            return [(0 if a < t * P else 1 if a < (t + 1) * P else 2, a, z) for a, z in zip(cuts, cuts[1:])]

        @block.tensor
        def _(pe):
            def scores(i, k):
                slot, t, k0 = i // NT, i % NT, k * QB
                if i: pe.wait_ge(s_exp, C * (i - 1) + k + 1)
                q = queries[:, slot, t * P:(t + 1) * P]
                for which, a, z in kinds(t, k0, k0 + QB):
                    mm = pe.matmul(s_ps[:, k, a - k0:z - k0], q, keys[:, which, a:z], start=(a == k0), stop=True, skip_group_check=True)
                lo, hi = max(k0, t * P - NEAR), min(k0 + QB, t * P + P + NEAR)
                if lo < hi:
                    w0 = lo - (t * P - NEAR)
                    mm = pe.matmul(s_ps[:, k, lo - k0:hi - k0], c.ident[:, :], near[:, i, w0:w0 + hi - lo],
                                   start=False, stop=True, skip_group_check=True)
                mm.then_inc(s_scores, 1)

            def turn(i, k):
                pe.wait_ge(s_scaled, C * i + k + 1)
                if k >= 2: pe.wait_ge(s_copy_v, 2 * i + k - 1)
                elif i: pe.wait_ge(s_copy_a, 2 * (i - 1) + k + 1)
                for j in range(4):
                    mm = pe.transpose(turn_ps[:, k % 2, j * P:(j + 1) * P], probs[:, i % 2, k * QB + j * P:k * QB + (j + 1) * P], c.ident[:, :])
                mm.then_inc(s_turn, 1)

            def pv(i, k):
                if k < 2: pe.wait_ge(s_copy_v, 2 * i + k + 1)
                else: pe.wait_ge(s_copy_a, 2 * i + k - 1)
                if k == 0 and i >= 2: pe.wait_ge(s_out, i - 1)
                for j in range(4):
                    mm = pe.matmul(acc[:, i % 2, 0:P], values[:, 4 * k + j, :], turned[:, k, j * P:(j + 1) * P],
                                   start=(k == 0 and j == 0), stop=(k == C - 1 and j == 3))
                mm.then_inc(s_pv, 1)

            for i in range(TILES + 1):
                for k in range(C - 1):
                    if i < TILES: scores(i, k)
                if i: turn(i - 1, 0); turn(i - 1, 1)
                if i < TILES: scores(i, C - 1)
                if i:
                    pv(i - 1, 0); turn(i - 1, 2)
                    pv(i - 1, 1); turn(i - 1, 3)
                    pv(i - 1, 2); pv(i - 1, 3)

        @block.vector
        def _(dve):
            def copy(i, k):
                dve.wait_ge(s_turn, C * i + k + 1)
                if i: dve.wait_ge(s_pv, C * (i - 1) + k + 1)
                dve.tensor_copy(turned[:, k, :], turn_ps[:, k % 2, :]).then_inc(s_copy_v, 1)

            for i in range(TILES + 1):
                if i < TILES:
                    for k in range(C):
                        if i and k == C - 1: copy(i - 1, 0); copy(i - 1, 1)
                        dve.wait_ge(s_scores, C * i + k + 1)
                        if i >= 2 and k == 0: dve.wait_ge(s_neg, i - 1)
                        dve.tensor_reduce(pmax[:, i % 2, k:k + 1], s_ps[:, k, :], AX.X, ALU.max).then_inc(s_max, 1)
                    dve.wait_ge(s_max, C * (i + 1))
                    dve.tensor_reduce(negmax[:, i % 2:i % 2 + 1], pmax[:, i % 2, :], AX.X, ALU.max, negate=True).then_inc(s_neg, 1)
                else:
                    copy(i - 1, 0); copy(i - 1, 1)
                if i < TILES:
                    dve.wait_ge(s_exp, C * (i + 1))
                    dve.tensor_reduce(total[:, i % 2:i % 2 + 1], sums[:, i % 2, :], AX.X, ALU.add).then_inc(s_step, 1)
                    dve.wait_ge(s_step, 3 * i + 1)
                    dve.reciprocal(total[:, i % 2:i % 2 + 1], total[:, i % 2:i % 2 + 1]).then_inc(s_step, 1)
                    dve.wait_ge(s_step, 3 * i + 2)
                    dve.tensor_tensor(weight[:, i % 2:i % 2 + 1], total[:, i % 2:i % 2 + 1], gates[:, i % NT, i // NT:i // NT + 1],
                                      ALU.mult).then_inc(s_step, 1)
                    dve.wait_ge(s_step, 3 * i + 3)
                    for k in range(C):
                        piece = probs[:, i % 2, k * QB:(k + 1) * QB]
                        dve.tensor_scalar(piece, piece, weight[:, i % 2:i % 2 + 1], None, ALU.mult).then_inc(s_scaled, 1)

        @block.scalar
        def _(act):
            def copy(i, k):
                act.wait_ge(s_turn, C * i + k + 1)
                if i: act.wait_ge(s_pv, C * (i - 1) + k + 1)
                act.activation(turned[:, k, :], turn_ps[:, k % 2, :], ACT.Copy).then_inc(s_copy_a, 1)

            for i in range(TILES + 1):
                if i < TILES:
                    act.wait_ge(s_neg, i + 1)
                    if i >= 2: act.wait_ge(s_turn, C * (i - 1))
                    for k in range(C):
                        if i and k in (1, 2): copy(i - 1, k + 1)
                        act.activation(probs[:, i % 2, k * QB:(k + 1) * QB], s_ps[:, k, :], ACT.Exp, bias=negmax[:, i % 2:i % 2 + 1],
                                       accum_out=sums[:, i % 2, k:k + 1]).then_inc(s_exp, 1)
                else:
                    copy(i - 1, 2); copy(i - 1, 3)
                if i:
                    act.wait_ge(s_pv, C * i)
                    act.activation(out[:, (i - 1) // NT, (i - 1) % NT * P:((i - 1) % NT + 1) * P], acc[:, (i - 1) % 2, 0:P], ACT.Copy).then_inc(s_out, 1)


def moa_out(nc, tag, c, heads, rows, rows_bf, o_w, o_bias_rows, base, dst):
    with ExitStack() as ctx:
        sb = lambda n, s: ctx.enter_context(nc.sbuf_tensor(tag + n, s, F32))
        sem = cleared_semaphores(nc, ctx, tag)
        routed = sb("routed", [P, 2, QB])
        mask_ps = ctx.enter_context(nc.psum_tensor(tag + "mask_ps", [P, 4, QB], F32))
        o_ps = ctx.enter_context(nc.psum_tensor(tag + "o_ps", [P, 2, QB], F32))
        s_mask = sem("masks_ready"); s_first = sem("first_routed"); s_routed = sem("routed"); s_o = sem("o_ready"); s_used = sem("routed_used"); s_dst = sem("dst_ready")
        units = [(b, e) for b in range(NB) for e in range(EA)]
        block = ctx.enter_context(nc.Block())

        @block.tensor
        def _(pe):
            for i in range(len(units) + 1):
                if i < len(units):
                    b, e = units[i]
                    cols = slice(b * QB, (b + 1) * QB)
                    if i >= 2: pe.wait_ge(s_routed, i - 1)
                    for k in range(2):
                        mm = pe.matmul(mask_ps[:, i % 2 * 2 + k, :], c.pick_bf[0:32, EA * (1 + k) + e, :], rows_bf[:, cols], start=True, stop=True)
                    mm.then_inc(s_mask, 1)
                if i:
                    b, e = units[i - 1]
                    cols = slice(b * QB, (b + 1) * QB)
                    if e == 0:
                        if b >= 2: pe.wait_ge(s_dst, b - 1)
                        pe.matmul(o_ps[:, b % 2, :], o_bias_rows[:, :], rows[:, cols], start=True, stop=False)
                    pe.wait_ge(s_routed, i)
                    pe.matmul(o_ps[:, b % 2, :], o_w[:, e, :], routed[:, (i - 1) % 2, :], start=False, stop=(e == EA - 1)).then_inc(s_used, 1)

        def finish(dve, b):
            dve.wait_ge(s_used, EA * (b + 1))
            dve.tensor_tensor(dst[:, b * QB:(b + 1) * QB], base[:, b * QB:(b + 1) * QB], o_ps[:, b % 2, :], ALU.add).then_inc(s_dst, 1)

        @block.vector
        def _(dve):
            for i, (b, e) in enumerate(units):
                cols = slice(b * QB, (b + 1) * QB)
                dve.wait_ge(s_mask, i + 1)
                if i >= 2: dve.wait_ge(s_used, i - 1)
                dve.tensor_tensor(routed[:, i % 2, :], heads[:, 0, cols], mask_ps[:, i % 2 * 2, :], ALU.mult).then_inc(s_first, 1)
                dve.wait_ge(s_first, i + 1)
                dve.copy_predicated(routed[:, i % 2, :], mask_ps[:, i % 2 * 2 + 1, :].bitcast(U32), heads[:, 1, cols]).then_inc(s_routed, 1)
                if e == 1 and b: finish(dve, b - 1)
            finish(dve, NB - 1)



def moe_ffn(nc, tag, c, src, rows, rows_bf, w1, b1, w2, b2_rows, base, gain, x):
    PAIRS = 8
    with ExitStack() as ctx:
        sb = lambda n, s: ctx.enter_context(nc.sbuf_tensor(tag + n, s, F32))
        sem = cleared_semaphores(nc, ctx, tag)
        hidden = sb("hidden", [P, 2, QB]); gated = sb("gated", [P, 2, QB]); total = sb("total", [P, 2, QB])
        h_ps = ctx.enter_context(nc.psum_tensor(tag + "h_ps", [P, 2, QB], F32))
        g_ps = ctx.enter_context(nc.psum_tensor(tag + "g_ps", [P, 2, QB], F32))
        o_ps = ctx.enter_context(nc.psum_tensor(tag + "o_ps", [P, 2, QB], F32))
        s_h = sem("h_ready"); s_relu = sem("relu_ready"); s_g = sem("gates_ready"); s_gated = sem("gated"); s_used = sem("gated_used")
        s_total = sem("total_ready"); s_x = sem("x_ready")
        units = [(b, e) for b in range(NB) for e in range(PAIRS)]
        block = ctx.enter_context(nc.Block())

        @block.tensor
        def _(pe):
            for i in range(len(units) + 1):
                if i < len(units):
                    b, e = units[i]
                    cols = slice(b * QB, (b + 1) * QB)
                    if i >= 2: pe.wait_ge(s_relu, i - 1)
                    pe.matmul(h_ps[:, i % 2, :], w1[:, e, :], src[:, cols], start=True, stop=True).then_inc(s_h, 1)
                    if i >= 2: pe.wait_ge(s_gated, i - 1)
                    pe.matmul(g_ps[:, i % 2, :], c.pick_pair[0:48, e, :], rows_bf[:, cols], start=True, stop=True).then_inc(s_g, 1)
                if i:
                    b, e = units[i - 1]
                    cols = slice(b * QB, (b + 1) * QB)
                    if e == 0:
                        if b >= 2: pe.wait_ge(s_total, b - 1)
                        pe.matmul(o_ps[:, b % 2, :], b2_rows[:, :], rows[:, cols], start=True, stop=False)
                    pe.wait_ge(s_gated, i)
                    pe.matmul(o_ps[:, b % 2, :], w2[:, e, :], gated[:, (i - 1) % 2, :], start=False, stop=(e == PAIRS - 1)).then_inc(s_used, 1)

        @block.scalar
        def _(act):
            for i, (b, e) in enumerate(units):
                act.wait_ge(s_h, i + 1)
                if i >= 2: act.wait_ge(s_gated, i - 1)
                act.activation(hidden[:, i % 2, :], h_ps[:, i % 2, :], ACT.Relu, bias=b1(e)).then_inc(s_relu, 1)

        def finish(dve, b):
            cols = slice(b * QB, (b + 1) * QB)
            dve.wait_ge(s_used, PAIRS * (b + 1))
            dve.tensor_tensor(total[:, b % 2, :], base[:, cols], o_ps[:, b % 2, :], ALU.add).then_inc(s_total, 1)
            dve.wait_ge(s_total, b + 1)
            dve.scalar_tensor_tensor(out=x[:, cols], in0=total[:, b % 2, :], scalar=gain, in1=x[:, cols],
                                     op0=ALU.mult, op1=ALU.add).then_inc(s_x, 1)

        @block.vector
        def _(dve):
            for i, (b, e) in enumerate(units):
                dve.wait_ge(s_relu, i + 1)
                dve.wait_ge(s_g, i + 1)
                if i >= 2: dve.wait_ge(s_used, i - 1)
                dve.tensor_tensor(gated[:, i % 2, :], hidden[:, i % 2, :], g_ps[:, i % 2, :], ALU.mult).then_inc(s_gated, 1)
                if e == 1 and b: finish(dve, b - 1)
            finish(dve, NB - 1)



def swiglu_experts(nc, tag, c, src, rows, rows_dram, w0, w1, wo, gain, x):
    E = 8
    F = 4
    with ExitStack() as ctx:
        sb = lambda n, s, d=F32: ctx.enter_context(nc.sbuf_tensor(tag + n, s, d))
        sem = cleared_semaphores(nc, ctx, tag)
        ps = lambda n, s: ctx.enter_context(nc.psum_tensor(tag + n, s, F32))
        w_sb = sb("w_sb", [P, 2, 2, F * P]); wo_sb = sb("wo_sb", [P, 2, F, D])
        w_high = sb("w_high", [P, 2, 2, F * P], F32R); w_low = sb("w_low", [P, 2, 2, F * P], F32R)
        src_high = sb("src_high", [P, S], F32R); src_low = sb("src_low", [P, S], F32R)
        gates = sb("gates", [P, 2, S]); gated = sb("gated", [P, 2, QB])
        gated_high = sb("gated_high", [P, 2, QB], F32R); gated_low = sb("gated_low", [P, 2, QB], F32R)
        silu = sb("silu", [P, 4, QB]); hidden = sb("hidden", [P, 2 * F, QB]); zeros = sb("zeros", [P, QB])
        a_ps = ps("a_ps", [P, 2, QB]); b_ps = ps("b_ps", [P, 2, QB]); o_ps = ps("o_ps", [P, NB, QB])
        s_store = sem("gates_stored"); s_load = [sem(f"expert_loaded{i}") for i in range(2)]; s_zero = sem("zeroed")
        s_src_high = sem("src_high_ready"); s_src_low = sem("src_low_ready")
        s_w_high = sem("w_high_ready"); s_w_low = sem("w_low_ready")
        s_gated = sem("src_gated"); s_g_high = sem("gated_high_ready"); s_g_low = sem("gated_low_ready")
        s_a = sem("a_ready"); s_b = sem("b_ready"); s_silu = sem("silu_ready"); s_hidden = sem("hidden_ready")
        s_o = sem("o_ready"); s_x = sem("x_ready")
        UNITS = NB * F
        AHEAD = 2
        block = ctx.enter_context(nc.Block())

        def experts(engine, body):
            with engine.Fori(0, E // 2 - 1) as it: body(it, False)
            body(E // 2 - 1, True)

        @block.sync
        def _(sp):
            def load(e, u):
                one = lambda a: a[bass.ds(e, 1)]
                sp.dma_start(w_sb[:, u, 0, :], one(w0).rearrange("e d f -> (e d) f")).then_inc(s_load[u], 16)
                sp.dma_start(w_sb[:, u, 1, :], one(w1).rearrange("e d f -> (e d) f")).then_inc(s_load[u], 16)
                sp.dma_start(gates[:, u, :], one(rows_dram).rearrange("e s -> (e s)").partition_broadcast(P)).then_inc(s_load[u], 16)
                sp.dma_start(wo_sb[:, u, :, :], one(wo).rearrange("e (f p) d -> (e p) f d", p=P)).then_inc(s_load[u], 16)
            sp.dma_start(rows_dram, rows[0:E, :]).then_inc(s_store, 16)
            sp.wait_ge(s_store, 16)
            load(0, 0); load(1, 1)
            with sp.Fori(0, E // 2 - 1) as it:
                for u in range(2):
                    sp.wait_ge(s_o, it * 2 * NB + (u + 1) * NB)
                    load(it * 2 + (u + 2), u)

        @block.gpsimd
        def _(pool):
            pool.memset(zeros[:, :], 0.0).then_inc(s_zero, 1)

            def body(it, last):
                for u in range(2):
                    for b in range(NB):
                        cols = slice(b * QB, (b + 1) * QB)
                        n = it * 2 * NB + (u * NB + b)
                        if b == 0: pool.wait_ge(s_load[u], it * 64 + 64)
                        pool.wait_ge(s_g_low, n + (AHEAD - 1))
                        pool.tensor_tensor(gated[:, b % 2, :], src[:, cols], gates[:, u, cols], ALU.mult).then_inc(s_gated, 1)
            experts(pool, body)

        @block.tensor
        def _(pe):
            pe.wait_ge(s_zero, 1)
            for b in range(NB):
                pe.matmul(o_ps[:, b, :], zeros[:, 0:P], zeros[:, :], start=True, stop=True)
            pe.wait_ge(s_src_low, NB)

            def product(dst, w, high, low):
                pe.matmul(dst, w_high[w], high, start=True, stop=False)
                pe.matmul(dst, w_high[w], low, start=False, stop=False)
                return pe.matmul(dst, w_low[w], high, start=False, stop=True)

            def hidden_products(u, b, f, U):
                cols, mine = slice(b * QB, (b + 1) * QB), slice(f * P, (f + 1) * P)
                pe.wait_ge(s_silu, U + (AHEAD - 1))
                product(a_ps[:, f % 2, :], (slice(None), u, 0, mine), src_high[:, cols], src_low[:, cols]).then_inc(s_a, 1)
                pe.wait_ge(s_hidden, U + (AHEAD - 1))
                product(b_ps[:, f % 2, :], (slice(None), u, 1, mine), gated_high[:, b % 2, :], gated_low[:, b % 2, :]).then_inc(s_b, 1)

            def out_products(u, b, n):
                pe.wait_ge(s_hidden, n * F + (F + AHEAD))
                for f in range(F):
                    mm = pe.matmul(o_ps[:, b, :], wo_sb[:, u, f, :], hidden[:, b % 2 * F + f, :], start=False, stop=True, skip_group_check=True)
                mm.then_inc(s_o, 1)

            def body(it, last):
                for u in range(2):
                    pe.wait_ge(s_load[u], it * 64 + 64)
                    pe.wait_ge(s_w_low, it * 4 + 2 * (u + 1))
                    for b in range(NB):
                        n = it * 2 * NB + (u * NB + b)
                        pe.wait_ge(s_g_low, n + (1 + AHEAD))
                        for f in range(F): hidden_products(u, b, f, n * F + f)
                        if b: out_products(u, b - 1, n - 1)
                    out_products(u, NB - 1, n)
            experts(pe, body)

        @block.scalar
        def _(act):
            act.sem_inc(s_silu, AHEAD)

            def weights_high(u, loads):
                act.wait_ge(s_load[u], loads)
                for w in range(2):
                    act.activation(w_high[:, u, w, :], w_sb[:, u, w, :], ACT.Copy).then_inc(s_w_high, 1)

            def gated_high_part(n, parity):
                act.wait_ge(s_gated, n + 1)
                act.activation(gated_high[:, parity, :], gated[:, parity, :], ACT.Copy).then_inc(s_g_high, 1)

            for b in range(NB):
                act.activation(src_high[:, b * QB:(b + 1) * QB], src[:, b * QB:(b + 1) * QB], ACT.Copy).then_inc(s_src_high, 1)
            weights_high(0, 64)
            gated_high_part(0, 0)

            def body(it, last):
                for k in range(2 * UNITS):
                    u, b, f = k // UNITS, k // F % NB, k % F
                    act.wait_ge(s_a, it * 2 * UNITS + (k + 1))
                    act.activation(silu[:, k % 4, :], a_ps[:, k % 2, :], ACT.Silu).then_inc(s_silu, 1)
                    ends = last and u == 1
                    if f == 1 and not (ends and b == NB - 1): gated_high_part(it * 2 * NB + (u * NB + b + 1), (b + 1) % 2)
                    if f == 2 and b == 1 and not ends: weights_high(1 - u, it * 64 + 64 * (u + 1))
            experts(act, body)

        @block.vector
        def _(dve):
            dve.sem_inc(s_hidden, AHEAD)
            dve.sem_inc(s_g_low, AHEAD)

            def weights_low(u, n):
                for w in range(2):
                    dve.wait_ge(s_w_high, n + (w + 1))
                    dve.tensor_tensor(w_low[:, u, w, :], w_sb[:, u, w, :], w_high[:, u, w, :].bitcast(F32), ALU.subtract).then_inc(s_w_low, 1)

            def gated_low_part(n, parity):
                dve.wait_ge(s_g_high, n + 1)
                dve.tensor_tensor(gated_low[:, parity, :], gated[:, parity, :], gated_high[:, parity, :].bitcast(F32), ALU.subtract).then_inc(s_g_low, 1)

            for b in range(NB):
                cols = slice(b * QB, (b + 1) * QB)
                dve.wait_ge(s_src_high, b + 1)
                dve.tensor_tensor(src_low[:, cols], src[:, cols], src_high[:, cols].bitcast(F32), ALU.subtract).then_inc(s_src_low, 1)
            weights_low(0, 0)
            gated_low_part(0, 0)

            def body(it, last):
                for k in range(2 * UNITS):
                    u, b, f = k // UNITS, k // F % NB, k % F
                    U = it * 2 * UNITS + k
                    dve.wait_ge(s_silu, U + (1 + AHEAD))
                    dve.wait_ge(s_b, U + 1)
                    dve.tensor_tensor(hidden[:, b % 2 * F + f, :], silu[:, k % 4, :], b_ps[:, k % 2, :], ALU.mult).then_inc(s_hidden, 1)
                    ends = last and u == 1
                    if f == 1 and not (ends and b == NB - 1): gated_low_part(it * 2 * NB + (u * NB + b + 1), (b + 1) % 2)
                    if f == 2 and b == 1 and not ends: weights_low(1 - u, it * 4 + 2 * (u + 1))
            experts(dve, body)
            dve.wait_ge(s_o, E * NB)
            for b in range(NB):
                cols = slice(b * QB, (b + 1) * QB)
                dve.scalar_tensor_tensor(out=x[:, cols], in0=o_ps[:, b, :], scalar=gain, in1=x[:, cols],
                                         op0=ALU.mult, op1=ALU.add).then_inc(s_x, 1)


VECTORS = ["L0_c", "L1_c", "qkv_b", "out_b", "g_attn", "b_attn", "g1", "b1", "g2", "b2", "b_inl", "ff_b1", "ff_b2",
           "ln1_w", "ln1_b", "ln2_w", "ln2_b", "q_b", "k_b", "moe_b1", "L1_b_attn", "L1_b_proj"]
WIDTHS = {"qkv_b": 3, "ff_b1": 4, "q_b": 8, "moe_b1": 8, "L1_b_attn": 3}


def vector_columns():
    at, n = {}, 0
    for name in VECTORS:
        at[name] = n
        n += WIDTHS.get(name, 1)
    return at, n


CONST_F32 = [("ident", P), ("averages", P), ("ones", P), ("strip_heads", P), ("spread_heads", P), ("counting", 16),
             ("eps", 1), ("one", 1), ("pick_gate", 2 * P)]
CONST_BF16 = [("ident_bf", P), ("ones_bf", P), ("mask_q", P), ("mask_k", P), ("pick_bf", 24 * P), ("pick_pair", 8 * P)]


class Constants:

    def __init__(self, consts, consts_bf):
        cut = {}
        for names, tensor in ((CONST_F32, consts), (CONST_BF16, consts_bf)):
            n = 0
            for name, w in names:
                cut[name] = tensor[:, n:n + w]
                n += w
        self.ident, self.averages, self.ones = cut["ident"], cut["averages"], cut["ones"]
        self.strip_heads, self.spread_heads = cut["strip_heads"], cut["spread_heads"]
        self.counting, self.eps, self.one = cut["counting"], cut["eps"], cut["one"]
        self.pick_gate = cut["pick_gate"].rearrange("p (k m) -> p k m", m=P)
        self.pick_pair = cut["pick_pair"].rearrange("p (k m) -> p k m", m=P)
        self.ident_bf, self.ones_bf, self.mask_q, self.mask_k = cut["ident_bf"], cut["ones_bf"], cut["mask_q"], cut["mask_k"]
        self.pick_bf = cut["pick_bf"].rearrange("p (k m) -> p k m", m=P)


def modulation(nc, c, modulations, vectors, at, weights):
    with ExitStack() as ctx:
        sem = cleared_semaphores(nc, ctx, "mod_")
        silu = ctx.enter_context(nc.sbuf_tensor("mod_silu", [P, 2], F32))
        sign = ctx.enter_context(nc.sbuf_tensor("mod_sign", [P, 2, 2], F32))
        size = ctx.enter_context(nc.sbuf_tensor("mod_size", [P, 2, 2], F32))
        mod_ps = ctx.enter_context(nc.psum_tensor("mod_ps", [P, 2, 6], F32))
        s_silu = sem("silu_ready"); s_mod = sem("product"); s_step = sem("step")
        block = ctx.enter_context(nc.Block())

        @block.scalar
        def _(act):
            act.activation(silu[:, :], vectors[:, at["L0_c"]:at["L1_c"] + 1], ACT.Silu).then_inc(s_silu, 1)

        @block.tensor
        def _(pe):
            pe.wait_ge(s_silu, 1)
            for layer in range(2):
                for i in range(6):
                    mm = pe.matmul(mod_ps[:, layer, i:i + 1], weights[:, layer, i * P:(i + 1) * P], silu[:, layer:layer + 1],
                                   start=True, stop=True)
            mm.then_inc(s_mod, 1)

        @block.vector
        def _(dve):
            dve.wait_ge(s_mod, 1)
            dve.tensor_copy(modulations[:, :, :], mod_ps[:, :, :]).then_inc(s_step, 1)
            dve.wait_ge(s_step, 1)
            gates = modulations[:, :, 2:6:3]
            dve.tensor_scalar(modulations[:, :, 1:5:3], mod_ps[:, :, 1:5:3], 1.0, None, ALU.add)
            dve.tensor_scalar(sign[:, :, :], gates, 0.0, 2.0, ALU.is_ge, ALU.mult).then_inc(s_step, 1)
            dve.wait_ge(s_step, 2)
            dve.scalar_tensor_tensor(out=size[:, :, :], in0=sign[:, :, :], scalar=-1.0, in1=gates, op0=ALU.add, op1=ALU.mult).then_inc(s_step, 1)
            dve.wait_ge(s_step, 3)
            dve.tensor_scalar(size[:, :, :], size[:, :, :], 0.25, None, ALU.max).then_inc(s_step, 1)
            dve.wait_ge(s_step, 4)
            dve.scalar_tensor_tensor(out=gates, in0=sign[:, :, :], scalar=-1.0, in1=size[:, :, :], op0=ALU.add, op1=ALU.mult)


def adaln_kernel(nc, ins, out):
    at, n_vec = vector_columns()
    with ExitStack() as ctx:
        sb = lambda n, s, d=F32: ctx.enter_context(nc.sbuf_tensor(n, s, d))
        dram = lambda n, s, d=F32: nc.dram_tensor(n, s, d, kind="Internal").ap()
        x = sb("x", [P, S])
        vectors = sb("vectors", [P, n_vec])
        consts = sb("consts", [P, sum(w for _, w in CONST_F32)])
        consts_bf = sb("consts_bf", [P, sum(w for _, w in CONST_BF16)], BF16)
        w_mod = sb("w_mod", [P, 2, 6 * D])
        w_qkv = sb("w_qkv", [P, 2, 3 * D])
        w_out = sb("w_out", [P, 2, D])
        w_ctx = sb("w_ctx", [P, D]); w_x = sb("w_x", [P, D])
        ff_w1 = sb("ff_w1", [P, 4 * P]); ff_w2 = sb("ff_w2", [P, 4, D])
        modulations = sb("modulations", [P, 2, 6]); gate_w1 = sb("gate_w1", [P, 8])
        s_load = ctx.enter_context(nc.semaphore("inputs_loaded"))
        s_later = ctx.enter_context(nc.semaphore("later_inputs_loaded"))
        s_store = ctx.enter_context(nc.semaphore("output_stored"))
        q_rows = dram("q_rows", [H, NROW, S], BF16); k_rows = dram("k_rows", [H, NROW, S], BF16)
        o_dram = dram("o_parts", [H, 4, HD + 1, S]); rden_dram = dram("inverse_sums", [H, S])
        band_dram = dram("band", [2 * NT, P, 2 * P]); gates_dram = dram("gate_rows", [8, S])

        c = Constants(consts, consts_bf)

        def vec(name, k=0): return vectors[:, at[name] + k:at[name] + k + 1]
        def mod(layer, i): return modulations[:, layer, i:i + 1]

        def start_loads(sp, loads, signal):
            for dst, src in loads: sp.dma_start(dst, src).then_inc(signal, 16)

        first = [(vectors[:, :], ins["vectors"]), (w_mod[:, 0, :], ins["L0_wmod"]), (w_mod[:, 1, :], ins["L1_wmod"]),
                 (consts[:, :], ins["consts"]), (x[:, :], ins["x"])]
        later = [(w_qkv[:, 0, :], ins["L0_attn_qkv_w"]), (w_qkv[:, 1, :], ins["L1_attn_W_attn"]),
                 (consts_bf[:, :], ins["consts_bf"].bitcast(BF16)),
                 (w_out[:, 0, :], ins["L0_attn_out_w"]), (w_out[:, 1, :], ins["L1_attn_W_proj"]),
                 (w_ctx[:, :], ins["L0_attn_w_ctx"]), (w_x[:, :], ins["L0_attn_w_x"]), (ff_w1[:, :], ins["L0_attn_ff_w1"]),
                 (ff_w2[:, :, :], ins["L0_attn_ff_w2"].rearrange("(f p) d -> p f d", p=P)), (gate_w1[:, :], ins["L1_ffn_gate_kernel"])]
        with nc.Block() as block:
            @block.sync
            def _(sp):
                start_loads(sp, first, s_load)
                start_loads(sp, later, s_later)
                sp.wait_ge(s_load, 16 * len(first))

        def await_loads(signal, loads):
            with nc.Block() as block:
                @block.sync
                def _(sp):
                    sp.wait_ge(signal, 16 * len(loads))

        modulation(nc, c, modulations, vectors, at, w_mod)

        def dump(t):
            with nc.Block() as block:
                @block.sync
                def _(sp):
                    sp.dma_start(out, t).then_inc(s_store, 16)
                    sp.wait_ge(s_store, 16)

        def causal_attention(layer, src, q_bias, k_bias, v_bias, out_bias, ctx_out, gain, base, dst):
            with ExitStack() as own:
                strips = own.enter_context(nc.sbuf_tensor(f"strips{layer}", [P, 4, S], F32))
                sums = own.enter_context(nc.sbuf_tensor(f"sums{layer}", [P, 4, S // 8], F32))
                v_all = own.enter_context(nc.sbuf_tensor(f"v_all{layer}", [P, NT, D], F32))
                qkv(nc, f"qkv{layer}_", c, src, w_qkv[:, layer, :], q_bias, k_bias, v_all, q_rows, k_rows)
                consts_of = lambda name: (lambda n: ins[name].bitcast(BF16)[bass.ds(n, 1)].rearrange("o r s -> (o r) s")) if layer else (lambda n: ins[name].bitcast(BF16))
                attention(nc, f"att{layer}_", q_rows, k_rows, consts_of(f"q_const{layer}"), consts_of(f"k_const{layer}"),
                          v_all, c.ident_bf, c.mask_q, c.mask_k, o_dram, strips, sums)
                attention_out(nc, f"out{layer}_", c, o_dram, strips, sums, rden_dram, w_out[:, layer, :], v_bias, out_bias, ctx_out, gain, base, dst)

        with ExitStack() as own:
            t = lambda n: own.enter_context(nc.sbuf_tensor(n, [P, S], F32))
            h, normed, attended = t("h0"), t("normed0"), t("attended0")
            layer_norms(nc, "ln0_", c, [(x, h, mod(0, 1), mod(0, 0)), (h, normed, vec("g_attn"), vec("b_attn"))])
            await_loads(s_later, later)
            causal_attention(0, normed, vec("qkv_b", 0), vec("qkv_b", 1), vec("qkv_b", 2), vec("out_b"), attended, c.one, h, h)
            layer_norms(nc, "ln1_", c, [(h, normed, vec("g1"), vec("b1"))])
            liquid(nc, "liq_", c, attended, w_ctx, w_x, vec("b_inl"), normed, h, h)
            layer_norms(nc, "ln2_", c, [(h, normed, vec("g2"), vec("b2"))])
            gelu_ffn(nc, "ffn_", c, normed, ff_w1, lambda f: vec("ff_b1", f), ff_w2, vec("ff_b2"), h, mod(0, 2), x)

        with ExitStack() as own:
            t = lambda n, s=[P, S], d=F32: own.enter_context(nc.sbuf_tensor(n, s, d))
            h, normed = t("h1"), t("normed1")
            rows = t("moa_rows", [32, S]); rows_bf = t("moa_rows_bf", [32, S], BF16); moe_rows = t("moe_rows", [48, S]); moe_rows_bf = t("moe_rows_bf", [48, S], BF16)
            moe_w1 = t("moe_w1", [P, 8, P]); moe_w2 = t("moe_w2", [P, 8, D]); moe_b2 = t("moe_b2", [48, D]); moe_gate = t("moe_gate", [P, 16])
            with ExitStack() as inner:
                u = lambda n, s: inner.enter_context(nc.sbuf_tensor(n, s, F32))
                gate_w = u("gate_w", [P, EA]); q_w = u("q_w", [P, EA, D]); kv_w = u("kv_w", [P, 2, D]); rel = u("rel", [P, 2 * P])
                o_w = u("o_w", [P, EA, D]); o_b = u("o_b", [32, D])
                token_gates = u("token_gates", [P, NT, 2]); v_bias = u("v_bias", [P, D])
                keys = u("keys", [P, 3, S]); values = u("values", [P, NT, D]); queries = u("queries", [P, 2, S])
                loads = []
                with nc.Block() as block:
                    s_w = inner.enter_context(nc.semaphore("moa_weights"))
                    s_z = inner.enter_context(nc.semaphore("o_b_zeroed"))
                    @block.gpsimd
                    def _(pool):
                        pool.memset(o_b[:, :], 0.0).then_inc(s_z, 1)
                    @block.sync
                    def _(sp):
                        sp.wait_ge(s_z, 1)
                        loads[:] = [(gate_w[:, :], ins["L0_ffn_attn_gate_w"]), (q_w[:, :, :], ins["L0_ffn_q_w"].rearrange("e d h -> d e h")),
                                 (kv_w[:, 0, :], ins["L0_ffn_k_w"]), (kv_w[:, 1, :], ins["L0_ffn_v_w"]), (rel[:, :], ins["rel"]),
                                 (v_bias[:, :], ins["L0_ffn_v_b"].partition_broadcast(P)),
                                 (o_w[:, :, :], ins["L0_ffn_o_w"].rearrange("e h d -> h e d")), (o_b[0:EA, :], ins["L0_ffn_o_b"]),
                                 (moe_w1[:, :, :].rearrange("p e (t f) -> p (e t) f", t=2), ins["L0_ffn_ff_w1"].rearrange("e d f -> d e f")),
                                 (moe_w2[:, :, :], ins["L0_ffn_ff_w2"].rearrange("(e t) f d -> (t f) e d", t=2)),
                                 *((moe_b2[16 * k:16 * k + 16, :], ins["L0_ffn_ff_b2"]) for k in range(3)), (moe_gate[:, :], ins["L0_ffn_ff_gate_w"])]
                        start_loads(sp, loads, s_w)
                layer_norms(nc, "ln3_", c, [(x, h, mod(0, 4), mod(0, 3)), (h, normed, vec("ln1_w"), vec("ln1_b"))])
                await_loads(s_w, loads)
                top2_gates(nc, "g1_", c, normed, gate_w[:, :], EA, rows, rows_bf, token_gates=token_gates)
                moa_keys(nc, "keys_", c, normed, kv_w[:, 0, :], vec("k_b"), kv_w[:, 1, :], v_bias, rel, keys, values)
                scaled_q_bias = u("scaled_q_bias", [P, EA])
                with nc.Block() as block:
                    @block.vector
                    def _(dve):
                        dve.tensor_scalar(scaled_q_bias[:, :], vectors[:, at["q_b"]:at["q_b"] + EA], float(D) ** -0.5, None, ALU.mult)
                moa_queries(nc, "queries_", c, normed, q_w, lambda e: scaled_q_bias[:, e:e + 1], rows_bf, queries)
                with ExitStack() as deep:
                    near = deep.enter_context(nc.sbuf_tensor("near", [P, 2 * NT, WINDOW], F32))
                    moa_near_bias(nc, "near_", c, rel[:, :], queries, near, band_dram)
                    moa_attention(nc, "moa_", c, keys, values, queries, near, token_gates, queries)
                moa_out(nc, "mo_", c, queries, rows, rows_bf, o_w, o_b, h, h)
            layer_norms(nc, "ln4_", c, [(h, normed, vec("ln2_w"), vec("ln2_b"))])
            top2_gates(nc, "g2_", c, normed, moe_gate[:, :], 16, moe_rows, moe_rows_bf, in_parts=True)
            moe_ffn(nc, "moe_", c, normed, moe_rows, moe_rows_bf, moe_w1, lambda e: vec("moe_b1", e), moe_w2, moe_b2, h, mod(0, 5), x)

        with ExitStack() as own:
            t = lambda n, s=[P, S], d=F32: own.enter_context(nc.sbuf_tensor(n, s, d))
            h, attended = t("h2"), t("attended1")
            layer_norms(nc, "ln5_", c, [(x, h, mod(1, 1), mod(1, 0))])
            causal_attention(1, h, vec("L1_b_attn", 0), vec("L1_b_attn", 1), vec("L1_b_attn", 2), vec("L1_b_proj"), attended, mod(1, 2), x, x)
            gates = t("expert_gates", [8, S])
            layer_norms(nc, "ln6_", c, [(x, h, mod(1, 4), mod(1, 3))])
            top2_gates(nc, "g3_", c, h, gate_w1[:, :], 8, gates)
            swiglu_experts(nc, "exp_", c, h, gates, gates_dram, ins["L1_ffn_w0"], ins["L1_ffn_w1"], ins["L1_ffn_wo"], mod(1, 5), x)
        dump(x[:, :])


def host_constants():
    f = {name: np.zeros((P, w), np.float32) for name, w in CONST_F32}
    f["ident"][:] = np.eye(P)
    f["averages"][:] = 1.0 / P
    f["ones"][:] = 1.0
    f["strip_heads"][::32] = 1.0
    for h in range(H): f["spread_heads"][h, h * HD:(h + 1) * HD] = 1.0
    f["counting"][:] = np.arange(16)
    f["eps"][:] = EPS
    f["one"][:] = 1.0
    for k in range(2): f["pick_gate"][3 * EA + k, k * P:(k + 1) * P] = 1.0
    b = {name: np.zeros((P, w), np.float32) for name, w in CONST_BF16}
    b["ident_bf"][:] = np.eye(P)
    b["ones_bf"][:] = 1.0
    i = np.arange(P)
    b["mask_q"][:] = np.where(i[None, :] > i[:, None], NEG, 0)
    b["mask_k"][:] = np.where(i[None, :] < i[:, None], NEG, 0)
    for e in range(8):
        for k in range(2): b["pick_pair"][2 * e + k:48:16, e * P + k * 64:e * P + (k + 1) * 64] = 1.0
    for r in range(24): b["pick_bf"][r, r * P:(r + 1) * P] = 1.0
    pos = np.arange(S)
    slopes = 2.0 ** -np.arange(1, H + 1)
    q1, k1 = np.zeros((2, H, CROWS, S), np.float32)
    high, low = pos // 256 * 256, pos % 256
    q1[:, 0:2] = 1.0
    k1[:, 0], k1[:, 1] = slopes[:, None] * high, slopes[:, None] * low
    q1[:, 2], q1[:, 3] = -slopes[:, None] * high, -slopes[:, None] * low
    k1[:, 2:4] = 1.0
    k1[:, MROW - NROW:MROW - NROW + 2] = 1.0
    q0, k0 = np.zeros((2, CROWS, S), np.float32)
    k0[MROW - NROW:MROW - NROW + 2] = 1.0
    bits = lambda a: (np.ascontiguousarray(a).view(np.uint32) >> 16).astype(np.uint16)
    return {"consts": np.concatenate([f[n] for n, _ in CONST_F32], 1),
            "consts_bf": bits(np.concatenate([b[n] for n, _ in CONST_BF16], 1)),
            "q_const0": bits(q0), "k_const0": bits(k0), "q_const1": bits(q1), "k_const1": bits(k1)}


AS_THEY_ARE = ["L0_wmod", "L1_wmod", "L0_attn_qkv_w", "L1_attn_W_attn", "L0_attn_out_w", "L1_attn_W_proj", "L0_attn_w_ctx",
               "L0_attn_w_x", "L0_attn_ff_w1", "L0_attn_ff_w2", "L0_ffn_attn_gate_w", "L0_ffn_q_w", "L0_ffn_k_w", "L0_ffn_v_w",
               "L0_ffn_v_b", "L0_ffn_o_w", "L0_ffn_o_b", "L0_ffn_ff_w1", "L0_ffn_ff_w2", "L0_ffn_ff_b2", "L0_ffn_ff_gate_w",
               "L1_ffn_gate_kernel", "L1_ffn_w0", "L1_ffn_w1", "L1_ffn_wo"]
SOURCES = {"L0_c": "L0_c", "L1_c": "L1_c", "q_b": "L0_ffn_q_b", "k_b": "L0_ffn_k_b",
           "moe_b1": "L0_ffn_ff_b1", "ln1_w": "L0_ffn_ln1_w", "ln1_b": "L0_ffn_ln1_b", "ln2_w": "L0_ffn_ln2_w",
           "ln2_b": "L0_ffn_ln2_b", "L1_b_attn": "L1_attn_b_attn", "L1_b_proj": "L1_attn_b_proj"}


def lay_out(inputs):
    a = {name: np.ascontiguousarray(inputs[name]) for name in AS_THEY_ARE}
    a["x"] = np.ascontiguousarray(np.asarray(inputs["L0_attn_x"])[0].T)
    columns = []
    for name in VECTORS:
        v = np.asarray(inputs[SOURCES.get(name, "L0_attn_" + name)])
        columns.append(v.reshape(WIDTHS.get(name, 1), P).T)
    a["vectors"] = np.ascontiguousarray(np.concatenate(columns, 1))
    rel = np.asarray(inputs["L0_ffn_rel_table"])
    a["rel"] = np.ascontiguousarray(rel[np.clip(np.arange(-P, P), -NEAR, NEAR) + NEAR].T)
    a.update(host_constants())
    return a


def kernel(**inputs):
    import concourse.bacc as bacc
    from concourse.bass_utils import run_bass_kernel_spmd

    nc = bacc.Bacc("TRN2", target_bir_lowering=False, num_devices=1)
    arrays = lay_out(inputs)
    ins = {n: nc.dram_tensor("in_" + n, a.shape, mybir.dt.from_np(a.dtype), kind="ExternalInput").ap() for n, a in arrays.items()}
    out = nc.dram_tensor("out_0_dram", (P, S), F32, kind="ExternalOutput").ap()
    adaln_kernel(nc, ins, out)
    r = run_bass_kernel_spmd(nc, [{"in_" + n: a for n, a in arrays.items()}], core_ids=[0])
    return np.ascontiguousarray(r.results[0]["out_0_dram"].T)[None]
```

```python
from contextlib import ExitStack

import numpy as np

import concourse.bass as bass
from concourse import mybir

F32 = mybir.dt.float32
BF16 = mybir.dt.bfloat16
F32R = mybir.dt.float32r
U32 = mybir.dt.uint32
ALU = mybir.AluOpType
ACT = mybir.ActivationFunctionType
AX = mybir.AxisListType


class Semaphores:

    def __init__(self, nc):
        self.nc, self.taken = nc, []

    def of(self, tag):
        def make(name):
            self.taken.append(self.nc.alloc_semaphore(name=tag + name))
            return self.taken[-1]
        return make

    def end_section(self):
        self.nc.clear_and_free_semaphores(self.taken)
        self.nc.all_engine_barrier()
        self.taken = []



P = 128; S = 2048; H = 16; HD = 8
QB = 512
NT = S//P
GROUPS_Q = "hhmmhl"; GROUPS_K = "hmhmlh"
NROW = 48
CROWS = 16
MROW = 52
NEG = -3.0e38


def pieces():
    return [(i, k, min(QB, P*(i+1)-k)) for i in range(NT) for k in range(0, P*(i+1), QB)]
PIECES = pieces()
N_PIECE = len(PIECES)
A_TILES = 12
A_LAST = sum(1 for i, _, _ in PIECES if i < A_TILES)

def slot_items(first):
    out = []
    for n in range(N_PIECE):
        if n == 6 and not first: out.append(("turn_b", None))
        if n == A_LAST+6: out.append(("turn_a", None))
        out.append(("piece", n))
    return out
N_ITEM = N_PIECE+2
P1_BANKS = 3
ITEM_PRICE = 64
LAG = -0.04

def item_count(n, k):
    return k if isinstance(n, int) and n == 0 else n*N_ITEM-1+k

def item_bank(first, k): return (k if first else k+N_ITEM-1)%P1_BANKS

def groups():
    out = []
    for c in range(S//QB):
        for j in range(0, 4*c+4, 2):
            out.append((c, [(t, max(0, P*(t-4*c))) for t in (j, j+1)]))
    return out
GROUPS = groups(); N_GROUP = len(GROUPS)
N_PAIR = N_GROUP//2
PAIRS_DONE = [sum(c+1 for c in range(b+1)) for b in range(4)]

def group_cols(g):
    (_, ts) = GROUPS[g]
    w = [QB-f for _, f in ts]
    return [0, w[0]], w, sum(w)

EARLY = H-3


def load_parts(sp, o_dram, strips, sums, h0, h1, signal):
    rows = slice(HD*h0, HD*h1)
    for g in range(4):
        signal(sp.dma_start(sums[rows, g, :], o_dram[h0:h1, g, HD, :].rearrange("h (e s) -> h e s", e=8)), None)
    for g in range(4):
        signal(sp.dma_start(strips[rows, g, :], o_dram[h0:h1, g, 0:HD, :]), g)


def items_after():
    steps = []
    for s in range(2, N_GROUP+2):
        steps.append(((s, "scores"), group_cols(s%N_GROUP)[2]))
        if s%2: steps.append(((s, "pv"), 4*QB))
    works = [ITEM_PRICE+(PIECES[x][2] if kind == "piece" else P) for kind, x in slot_items(False)]
    counts, done, taken, mine, theirs = {}, 0, 0, 0, 0
    for at, work in steps:
        mine += work/sum(w for _, w in steps)
        while taken < len(works) and theirs < mine-LAG:
            theirs += works[taken]/sum(works)
            taken += 1
        counts[at], done = taken-done, taken
    counts[steps[-1][0]] += len(works)-taken
    return counts

ITEMS_AFTER = items_after()


def attention(nc, tag, c, q_rows, k_rows, q_const, k_const, v_all, ident, mask_q, mask_k, o_dram, strips, sums):
    with ExitStack() as ctx:
        sb = lambda n, s, d: ctx.enter_context(nc.sbuf_tensor(tag+n, s, d))
        sem = c.semaphores.of(tag)
        ps = lambda n, s, d: ctx.enter_context(nc.psum_tensor(tag+n, s, d))
        qb = sb("qb", [P, 3, S], BF16); kb = sb("kb", [P, 3, S], BF16)
        vb = sb("vb", [P, 3, NT, 32], F32)
        probs = sb("probs", [P, 4, 2*QB], F32)
        o_sb = sb("o_sb", [P, 3, S], F32)
        pmax = sb("pmax", [P, NT, 4], F32)
        negmax = sb("negmax", [P, NT], F32)
        zeros = sb("zeros", [P, QB], BF16)
        nothing = sb("nothing", [P, A_TILES], F32)
        split_a = sb("split_a", [P, 2, A_TILES], BF16); split_b = sb("split_b", [P, 2, NT-A_TILES], BF16)
        turned_a = sb("turned_a", [2*A_TILES, P], BF16); turned_b = sb("turned_b", [2*(NT-A_TILES), P], BF16)
        p1 = ps("p1", [P, P1_BANKS, QB], F32)
        s2 = ps("s2", [P, 2, 2*QB], F32)
        acc = ps("acc", [P, QB], F32)
        s_load = [sem(f"heads_loaded{i}") for i in range(3)]
        s_zero = sem("buffers_zeroed"); s_pmax = sem("pmax_set"); s_item = sem("p1_filled"); s_free = sem("p1_read")
        s_nm = sem("negmax_ready"); s_split = sem("negmax_split")
        s_ma = sem("max_rows_a"); s_mb = sem("max_rows_b")
        s_scores = sem("scores_ready"); s_exp = sem("probs_ready"); s_pv = sem("pv_done"); s_evac = sem("out_copied")
        s_out = sem("out_stored"); s_v = sem("v_ready"); s_early = sem("first_heads_back")
        block = ctx.enter_context(nc.Block())
        A = A_TILES; B = NT-A_TILES
        BIAS = 2
        def turned(n, part):
            if part == "b": return item_count_next(n, 6 if not (isinstance(n, int) and n == H-1) else 0)+1
            first = isinstance(n, int) and n == 0
            return item_count(n, [k for k, _ in slot_items(first)].index("turn_a"))+1
        def item_count_next(n, k): return (n+1)*N_ITEM-1+k
        def last_pair(n): return BIAS+(n+1)*N_PAIR

        @block.sync
        def _(sp):
            def load(n, u):
                for dst, rows, const in ((kb, k_rows, k_const), (qb, q_rows, q_const)):
                    sp.dma_start(dst[0:NROW, u, :], rows[bass.ds(n, 1)].rearrange("o r s -> (o r) s")).then_inc(s_load[u], 16)
                    sp.dma_start(dst[NROW:NROW+CROWS, u, :], const(n)).then_inc(s_load[u], 16)
            def max_rows(n, u, part):
                t0, t1, src, s_m = (0, A, turned_a, s_ma) if part == "a" else (A, NT, turned_b, s_mb)
                sp.wait_ge(s_free, turned(n, part))
                for j in range(2):
                    sp.dma_start(qb[MROW+j:MROW+j+1, u, t0*P:t1*P],
                                 src[j*(t1-t0):(j+1)*(t1-t0), :]).then_inc(s_m, 16)
            def store(n, u):
                sp.wait_ge(s_evac, 1+4*n+4)
                for g in range(4):
                    sp.dma_start(o_dram[bass.ds(n, 1), g, :, :].rearrange("o r s -> (o r) s"),
                                 o_sb[32*g:32*g+9, u, :]).then_inc(s_out, 16)
            def slot(n, u):
                max_rows(n-1, (u+2)%3, "b")
                store(n-2, (u+1)%3)
                sp.wait_ge(s_out, 64*(n-1))
                load(n+1, (u+1)%3)
                max_rows(n, u, "a")
            load(0, 0); load(1, 1)
            sp.wait_ge(s_zero, 5)
            max_rows(0, 0, "a")
            load(2, 2)
            max_rows(0, 0, "b")
            max_rows(1, 1, "a")
            slot(2, 2)
            with sp.Fori(1, (H-1)//3) as it:
                for j in range(3): slot(it*3+j, j)
            max_rows(H-2, 2, "b")
            sp.wait_ge(s_out, 64*EARLY)
            load_parts(sp, o_dram, strips, sums, 0, EARLY, lambda dma, g: dma.then_inc(s_early, 16))
            store(H-3, 1)
            max_rows(H-1, 0, "a")
            max_rows(H-1, 0, "b")
            store(H-2, 2); store(H-1, 0)
            sp.wait_ge(s_out, 64*H)
            sp.wait_ge(s_early, 16*8)

        @block.gpsimd
        def _(pool):
            def split(n, part):
                t0, t1, dst, w = (0, A, split_a, 2*n+1) if part == "a" else (A, NT, split_b, 2*n+2)
                pool.wait_ge(s_nm, w)
                if not (isinstance(n, int) and n == 0): pool.wait_ge(s_free, turned(n-1, part))
                pool.tensor_tensor(dst[:, 0, :], negmax[:, t0:t1], nothing[:, 0:t1-t0], ALU.add).then_inc(s_split, 1)
                pool.wait_ge(s_split, 2*w-1)
                pool.tensor_tensor(dst[:, 1, :], negmax[:, t0:t1], dst[:, 0, :], ALU.subtract).then_inc(s_split, 1)
            def v_copy(n, u):
                pool.wait_ge(s_zero, 5)
                if not (isinstance(n, int) and n < 3): pool.wait_ge(s_pv, last_pair(n-3))
                pool.tensor_copy(vb[:, u, :, 0:HD], v_all[:, :, bass.ds(n*HD, HD)]).then_inc(s_v, 1)
            pool.memset(nothing[:], 0.0).then_inc(s_zero, 1)
            pool.wait_ge(s_zero, 1)
            pool.memset(qb[64:128, :, :], 0.0).then_inc(s_zero, 1)
            pool.wait_ge(s_zero, 2)
            pool.memset(kb[64:128, :, :], 0.0).then_inc(s_zero, 1)
            pool.wait_ge(s_zero, 3)
            pool.memset(vb[:], 0.0).then_inc(s_zero, 1)
            pool.wait_ge(s_zero, 4)
            pool.memset(vb[:, :, :, HD:HD+1], 1.0).then_inc(s_zero, 1)
            pool.wait_ge(s_zero, 5)
            pool.memset(zeros[:], 0.0).then_inc(s_zero, 1)
            pool.wait_ge(s_zero, 6)
            def slot(n, u):
                v_copy(n, u)
                split(n, "a"); split(n, "b")
            slot(0, 0); slot(1, 1); slot(2, 2)
            with pool.Fori(1, (H-1)//3) as it:
                for j in range(3): slot(it*3+j, j)
            slot(H-1, 0)

        @block.vector
        def _(dve):
            dve.memset(pmax[:], NEG).then_inc(s_pmax, 1)
            dve.wait_ge(s_pmax, 1)
            def items(n, first=False):
                for k, (kind, x) in enumerate(slot_items(first)):
                    at = item_count(n, k); bank = item_bank(first, k)
                    if kind == "piece":
                        i, k0, w = PIECES[x]
                        dve.wait_ge(s_item, at+1)
                        dve.tensor_reduce(pmax[:, i, k0//QB:k0//QB+1], p1[:, bank, 0:w], AX.X, ALU.max).then_inc(s_free, 1)
                        if x == A_LAST-1: negate(n, "a", at)
                        if x == N_PIECE-1: negate(n, "b", at)
                    elif kind == "turn_a": copy_turned(n, "a", bank, at)
                    else: copy_turned(n-1, "b", bank, at)
            def copy_turned(n, part, bank, at):
                dst, w = (turned_a, 2*A) if part == "a" else (turned_b, 2*B)
                dve.wait_ge(s_item, at+1)
                dve.tensor_copy(dst[:, :], p1[:, bank, :].bitcast(BF16)[0:w, 0:P]).then_inc(s_free, 1)
            def negate(n, part, at):
                t0, t1 = (0, A) if part == "a" else (A, NT)
                dve.wait_ge(s_free, at+1)
                if not (isinstance(n, int) and n == 0): dve.wait_ge(s_split, 4*n)
                dve.tensor_reduce(negmax[:, t0:t1], pmax[:, t0:t1, :], AX.X, ALU.max, negate=True).then_inc(s_nm, 1)
            items(0, True)
            with dve.Fori(0, (H-1)//3) as it:
                for j in range(3): items(it*3+(1+j))
            copy_turned(H-1, "b", item_bank(False, 0), item_count(H, 0))

        @block.scalar
        def _(act):
            act.sem_inc(s_exp, BIAS)
            act.sem_inc(s_evac, 1)
            def exp(m, g):
                _, _, w = group_cols(g)
                act.wait_ge(s_scores, m*N_GROUP+g+1)
                act.wait_ge(s_pv, BIAS+m*N_PAIR+g//2-1)
                act.activation(probs[:, g%4, 0:w], s2[:, g%2, 0:w], ACT.Exp).then_inc(s_exp, 1)
            def evac(m, u, c):
                act.wait_ge(s_pv, BIAS+m*N_PAIR+PAIRS_DONE[c])
                act.activation(o_sb[:, u, QB*c:QB*c+QB], acc[:, :], ACT.Copy).then_inc(s_evac, 1)
            def body(m, u, more=True):
                for g in range(2, N_GROUP):
                    exp(m, g)
                    if g%2 and g//2 in PAIRS_DONE: evac(m, u, PAIRS_DONE.index(g//2))
                if more: exp(m+1, 0); exp(m+1, 1)
                evac(m, u, 3)
            exp(0, 0); exp(0, 1)
            with act.Fori(0, (H-1)//3) as it:
                for j in range(3): body(it*3+j, j)
            body(H-1, 0, False)

        @block.tensor
        def _(pe):
            pe.sem_inc(s_pv, BIAS)
            def item(n, u, k, kind, x, first):
                at = item_count(n, k); bank = item_bank(first, k)
                if not(first and k < P1_BANKS): pe.wait_ge(s_free, at+1-P1_BANKS)
                if kind == "piece":
                    i, k0, w = PIECES[x]
                    diagonal = k0+w == P*(i+1)
                    mm = pe.matmul(p1[:, bank, 0:w], qb[:, u, i*P:(i+1)*P], kb[:, u, k0:k0+w], start=True, stop=True)
                    if diagonal: mm = pe.matmul(p1[:, bank, w-P:w], ident[:, :], mask_q[:, :], start=False, stop=True, skip_group_check=True)
                    mm.then_inc(s_item, 1)
                elif kind == "turn_a": turn(n, "a", bank)
                else: turn(n-1, "b", bank)
            def turn(n, part, bank):
                src, w, t = (split_a, 2*A, 4*n+2) if part == "a" else (split_b, 2*B, 4*n+4)
                pe.wait_ge(s_split, t)
                pe.transpose(p1[:, bank, :].bitcast(BF16)[0:w, 0:P], src[:, :, :].rearrange("p a t -> p (a t)"), ident[:, :]).then_inc(s_item, 1)
            def scores(m, u, g):
                c, ts = GROUPS[g]
                at, w, _ = group_cols(g)
                if g == 0: pe.wait_ge(s_ma, 32*m+32)
                if c == 3 and GROUPS[g-1][0] == 2: pe.wait_ge(s_mb, 32*m+32)
                pe.wait_ge(s_exp, BIAS+m*N_GROUP+g-1)
                for (t, f), a, n in zip(ts, at, w):
                    diagonal = t >= 4*c
                    mm = pe.matmul(s2[:, g%2, a:a+n], kb[:, u, t*P:(t+1)*P], qb[:, u, c*QB+f:(c+1)*QB], start=True, stop=True)
                    if diagonal: mm = pe.matmul(s2[:, g%2, a:a+P], ident[:, :], mask_k[:, :], start=False, stop=True, skip_group_check=True)
                mm.then_inc(s_scores, 1)
            def pv(m, u, p):
                c = GROUPS[2*p][0]
                first = p == 0 or GROUPS[2*p-1][0] != c
                if p == 0: pe.wait_ge(s_v, m+1)
                pe.wait_ge(s_exp, BIAS+m*N_GROUP+2*p+2)
                if first: pe.wait_ge(s_evac, 1+4*m+c)
                if p == 0: pe.matmul(acc[:, :], zeros[:, 0:P], zeros[:, :], start=True, stop=True)
                for g in (2*p, 2*p+1):
                    at, w, _ = group_cols(g)
                    for j, (t, f) in enumerate(GROUPS[g][1]):
                        strip = 32*(t%4)
                        st = c > 0 and t < 4; last = t >= 4*c
                        mm = pe.matmul(acc[strip:strip+32, f:QB], vb[:, u, t, :], probs[:, g%4, at[j]:at[j]+w[j]],
                                     start=st, stop=last, skip_group_check=True)
                mm.then_inc(s_pv, 1)
            def body(m, u, more=True):
                un = (u+1)%3
                coming = iter(enumerate(slot_items(False)) if more else ())
                def items(count):
                    for _, (k, (kind, x)) in zip(range(count), coming): item(m+1, un, k, kind, x, False)
                for s in range(2, N_GROUP+2):
                    if s < N_GROUP: scores(m, u, s)
                    elif more: scores(m+1, un, s-N_GROUP)
                    items(ITEMS_AFTER[s, "scores"])
                    if s%2:
                        pv(m, u, (s-3)//2)
                        items(ITEMS_AFTER[s, "pv"])
                    if s == 2 and not more: last_turn()
            def last_turn():
                k = item_count(H, 0)
                pe.wait_ge(s_free, k+1-P1_BANKS)
                turn(H-1, "b", item_bank(False, 0))
            for u in range(1): pe.wait_ge(s_load[u], 64)
            pe.wait_ge(s_zero, 6)
            for k, (kind, x) in enumerate(slot_items(True)): item(0, 0, k, kind, x, True)
            scores(0, 0, 0); scores(0, 0, 1)
            with pe.Fori(0, (H-1)//3) as it:
                for j in range(3):
                    pe.wait_ge(s_load[(j+1)%3], it*64+64*((j+1)//3+1))
                    body(it*3+j, j)
            body(H-1, 0, False)


NB = S // QB
D = P
EPS = 1e-5


def layer_norms(nc, tag, c, norms):
    with ExitStack() as ctx:
        sb = lambda n, s: ctx.enter_context(nc.sbuf_tensor(tag + n, s, F32))
        ps = lambda n, s: ctx.enter_context(nc.psum_tensor(tag + n, s, F32))
        sem = c.semaphores.of(tag)
        centred = sb("centred", [P, 4, QB])
        squares = sb("squares", [P, 2, QB])
        deviation = sb("deviation", [P, 2, 4])
        rstd = sb("rstd", [P, 2, 4])
        diagonal = sb("diagonal", [P, 2, QB])
        scaled = sb("scaled", [P, 2, QB])
        mean_ps = ps("mean_ps", [P, 2, QB])
        var_ps = ps("var_ps", [P, 2, QB])
        bcast_ps = ps("bcast_ps", [P, 2, QB])
        s_mean = sem("mean_ready"); s_cent = sem("centred"); s_sq = sem("squared"); s_var = sem("var_ready")
        s_dev = sem("deviation_ready"); s_rstd = sem("rstd_ready"); s_diag = sem("diagonal_ready")
        s_bc = sem("rstd_broadcast"); s_mul = sem("scaled"); s_out = sem("normed")
        n_all = NB * len(norms)
        at = lambda i: (norms[i // NB], slice(i % NB * QB, (i % NB + 1) * QB))
        block = ctx.enter_context(nc.Block())

        @block.tensor
        def _(pe):
            for t in range(n_all + 2):
                if t < n_all:
                    i = t
                    (src, _, _, _), cols = at(i)
                    if i >= NB: pe.wait_ge(s_out, i - NB + 1)
                    if i >= 2: pe.wait_ge(s_cent, i - 1)
                    pe.matmul(mean_ps[:, i % 2, :], c.averages[:, :], src[:, cols], start=True, stop=True).then_inc(s_mean, 1)
                if 1 <= t <= n_all:
                    i = t - 1
                    pe.wait_ge(s_sq, i + 1)
                    if i >= 2: pe.wait_ge(s_dev, i - 1)
                    for k in range(4):
                        mm = pe.matmul(var_ps[:, i % 2, k:k + 1], squares[:, i % 2, k * P:(k + 1) * P],
                                       c.averages[:, 0:1], start=True, stop=True)
                    mm.then_inc(s_var, 1)
                if t >= 2:
                    i = t - 2
                    pe.wait_ge(s_diag, i + 1)
                    if i >= 2: pe.wait_ge(s_mul, i - 1)
                    pe.matmul(bcast_ps[:, i % 2, :], c.ones[:, :], diagonal[:, i % 2, :], start=True, stop=True).then_inc(s_bc, 1)

        @block.vector
        def _(dve):
            for t in range(n_all + 2):
                if t < n_all:
                    i = t
                    (src, _, _, _), cols = at(i)
                    dve.wait_ge(s_mean, i + 1)
                    if i >= 4: dve.wait_ge(s_sq, i - 3)
                    dve.tensor_tensor(centred[:, i % 4, :], src[:, cols], mean_ps[:, i % 2, :], ALU.subtract).then_inc(s_cent, 1)
                if 1 <= t <= n_all:
                    i = t - 1
                    dve.wait_ge(s_dev, i + 1)
                    dve.reciprocal(rstd[:, i % 2, :], deviation[:, i % 2, :]).then_inc(s_rstd, 1)
                    dve.wait_ge(s_rstd, i + 1)
                    if i >= 2: dve.wait_ge(s_bc, i - 1)
                    for k in range(4):
                        ins = dve.tensor_scalar(diagonal[:, i % 2, k * P:(k + 1) * P], c.ident[:, :],
                                                rstd[:, i % 2, k:k + 1], None, ALU.mult)
                    ins.then_inc(s_diag, 1)
                if t >= 2:
                    i = t - 2
                    dve.wait_ge(s_bc, i + 1)
                    if i >= 2: dve.wait_ge(s_out, i - 1)
                    dve.tensor_tensor(scaled[:, i % 2, :], centred[:, i % 4, :], bcast_ps[:, i % 2, :], ALU.mult).then_inc(s_mul, 1)

        @block.scalar
        def _(act):
            for t in range(n_all + 2):
                if t < n_all:
                    i = t
                    act.wait_ge(s_cent, i + 1)
                    if i >= 2: act.wait_ge(s_var, i - 1)
                    act.activation(squares[:, i % 2, :], centred[:, i % 4, :], ACT.Square).then_inc(s_sq, 1)
                if 1 <= t <= n_all:
                    i = t - 1
                    act.wait_ge(s_var, i + 1)
                    act.activation(deviation[:, i % 2, :], var_ps[:, i % 2, 0:4], ACT.Sqrt, bias=c.eps).then_inc(s_dev, 1)
                if t >= 2:
                    i = t - 2
                    (_, dst, scale, bias), cols = at(i)
                    act.wait_ge(s_mul, i + 1)
                    act.activation(dst[:, cols], scaled[:, i % 2, :], ACT.Identity, scale=scale, bias=bias).then_inc(s_out, 1)


def qkv(nc, tag, c, src, weights, q_bias, k_bias, v_all, q_rows, k_rows):
    with ExitStack() as ctx:
        sb = lambda n, s, d: ctx.enter_context(nc.sbuf_tensor(tag + n, s, d))
        sem = c.semaphores.of(tag)
        full = sb("full", [P, 2, QB], F32)
        rest = sb("rest", [P, 2, QB], F32)
        parts = {k: sb("part_" + k, [P, 2, S], BF16) for k in "hml"}
        qk_ps = ctx.enter_context(nc.psum_tensor(tag + "qk_ps", [P, 2, QB], F32))
        v_ps = ctx.enter_context(nc.psum_tensor(tag + "v_ps", [P, 2, QB], F32))
        s_qk = sem("qk_ready"); s_full = sem("full_ready"); s_high = sem("high_ready"); s_rest = sem("rest_ready")
        s_mid = sem("mid_ready"); s_low = sem("low_ready"); s_v = sem("v_ready"); s_vcopy = sem("v_copied"); s_store = sem("rows_stored")
        units = [(w, b) for w in range(2) for b in range(NB)]
        block = ctx.enter_context(nc.Block())

        @block.tensor
        def _(pe):
            for i, (w, b) in enumerate(units):
                if i >= 2: pe.wait_ge(s_full, i - 1)
                pe.matmul(qk_ps[:, i % 2, :], weights[:, w * D:(w + 1) * D], src[:, b * QB:(b + 1) * QB],
                          start=True, stop=True).then_inc(s_qk, 1)
                if i % 2:
                    v = i // 2
                    if v >= 2: pe.wait_ge(s_vcopy, v - 1)
                    for k in range(4):
                        t = 4 * v + k
                        mm = pe.matmul(v_ps[:, v % 2, k * D:(k + 1) * D], src[:, t * P:(t + 1) * P],
                                       weights[:, 2 * D:3 * D], start=True, stop=True)
                    mm.then_inc(s_v, 1)

        @block.vector
        def _(dve):
            for i, (w, b) in enumerate(units):
                dve.wait_ge(s_qk, i + 1)
                if i >= 2: dve.wait_ge(s_rest, i - 1)
                dve.tensor_scalar(full[:, i % 2, :], qk_ps[:, i % 2, :], q_bias if w == 0 else k_bias,
                                  HD ** -0.5 if w == 0 else 1.0, ALU.add, ALU.mult).then_inc(s_full, 1)
                dve.wait_ge(s_high, i + 1)
                if i >= 2: dve.wait_ge(s_low, i - 1)
                dve.tensor_tensor(rest[:, i % 2, :], full[:, i % 2, :], parts["h"][:, w, b * QB:(b + 1) * QB],
                                  ALU.subtract).then_inc(s_rest, 1)

        @block.scalar
        def _(act):
            for i, (w, b) in enumerate(units):
                cols = slice(b * QB, (b + 1) * QB)
                act.wait_ge(s_full, i + 1)
                act.activation(parts["h"][:, w, cols], full[:, i % 2, :], ACT.Copy).then_inc(s_high, 1)
                if i % 2:
                    v = i // 2
                    act.wait_ge(s_v, v + 1)
                    act.activation(v_all[:, 4 * v:4 * v + 4, :], v_ps[:, v % 2, :].rearrange("p (t d) -> p t d", t=4),
                                   ACT.Copy).then_inc(s_vcopy, 1)
                act.wait_ge(s_rest, i + 1)
                act.activation(parts["m"][:, w, cols], rest[:, i % 2, :], ACT.Copy).then_inc(s_mid, 1)

        @block.gpsimd
        def _(pool):
            for i, (w, b) in enumerate(units):
                cols = slice(b * QB, (b + 1) * QB)
                pool.wait_ge(s_mid, i + 1)
                if i: pool.wait_ge(s_low, i)
                pool.tensor_tensor(parts["l"][:, w, cols], rest[:, i % 2, :], parts["m"][:, w, cols],
                                   ALU.subtract).then_inc(s_low, 1)

        @block.sync
        def _(sp):
            for w, (rows, groups) in enumerate(((q_rows, GROUPS_Q), (k_rows, GROUPS_K))):
                for kind, s in (("h", s_high), ("m", s_mid), ("l", s_low)):
                    sp.wait_ge(s, NB * (w + 1))
                    for g, part in enumerate(groups):
                        if part == kind:
                            sp.dma_start(rows[:, g * HD:(g + 1) * HD, :], parts[kind][:, w, :]).then_inc(s_store, 16)
            sp.wait_ge(s_store, 16 * 12)


def attention_out(nc, tag, c, o_dram, strips, sums, rden_dram, weights, v_bias, out_bias, ctx_out, gain, base, dst):
    with ExitStack() as ctx:
        sb = lambda n, s, d=F32: ctx.enter_context(nc.sbuf_tensor(tag + n, s, d))
        sem = c.semaphores.of(tag)
        total = sb("total", [P, S // 8])
        inverse = sb("inverse", [P, S // 8])
        inverse_rows = sb("inverse_rows", [H, S])
        bias = sb("bias", [P, 1])
        bcast_ps = ctx.enter_context(nc.psum_tensor(tag + "bcast_ps", [P, 2, QB], F32))
        out_ps = ctx.enter_context(nc.psum_tensor(tag + "out_ps", [P, 2, QB], F32))
        bias_ps = ctx.enter_context(nc.psum_tensor(tag + "bias_ps", [P, QB], F32))
        s_sums = sem("sums_loaded"); s_strips = [sem(f"strips_loaded{i}") for i in range(4)]
        s_step = sem("sums_step"); s_inv = sem("inverse_stored"); s_rows = sem("inverse_rows_loaded")
        s_half = sem("half_summed"); s_add = sem("strips_summed"); s_bc = sem("inverse_broadcast"); s_norm = sem("divided")
        s_bias_ps = sem("bias_product"); s_bias = sem("bias_ready"); s_out = sem("projected"); s_ctx = sem("ctx_written"); s_dst = sem("dst_written")
        block = ctx.enter_context(nc.Block())

        @block.sync
        def _(sp):
            load_parts(sp, o_dram, strips, sums, EARLY, H, lambda dma, g: dma.then_inc(s_sums if g is None else s_strips[g], 16))
            sp.wait_ge(s_step, 4)
            sp.dma_start(rden_dram.rearrange("h (e s) -> (h e) s", e=8), inverse[:, :]).then_inc(s_inv, 16)
            sp.wait_ge(s_inv, 16)
            sp.dma_start(inverse_rows[:, :], rden_dram).then_inc(s_rows, 16)

        @block.gpsimd
        def _(pool):
            pool.wait_ge(s_strips[2], 16)
            pool.wait_ge(s_strips[3], 16)
            pool.tensor_tensor(strips[:, 2, :], strips[:, 2, :], strips[:, 3, :], ALU.add).then_inc(s_half, 1)

        @block.vector
        def _(dve):
            dve.wait_ge(s_sums, 64)
            dve.tensor_tensor(total[:, :], sums[:, 0, :], sums[:, 1, :], ALU.add).then_inc(s_step, 1)
            for g in (2, 3):
                dve.wait_ge(s_step, g - 1)
                dve.tensor_tensor(total[:, :], total[:, :], sums[:, g, :], ALU.add).then_inc(s_step, 1)
            dve.wait_ge(s_step, 3)
            dve.reciprocal(inverse[:, :], total[:, :]).then_inc(s_step, 1)
            dve.wait_ge(s_bias_ps, 1)
            dve.tensor_tensor(bias[:, :], bias_ps[:, 0:1], out_bias, ALU.add).then_inc(s_bias, 1)
            dve.wait_ge(s_strips[0], 16)
            dve.wait_ge(s_strips[1], 16)
            dve.tensor_tensor(strips[:, 0, :], strips[:, 0, :], strips[:, 1, :], ALU.add).then_inc(s_add, 1)
            dve.wait_ge(s_add, 1)
            dve.wait_ge(s_half, 1)
            dve.tensor_tensor(strips[:, 0, :], strips[:, 0, :], strips[:, 2, :], ALU.add).then_inc(s_add, 1)
            dve.wait_ge(s_add, 2)
            for b in range(NB + 1):
                if b < NB:
                    cols = slice(b * QB, (b + 1) * QB)
                    dve.wait_ge(s_bc, b + 1)
                    dve.tensor_tensor(strips[:, 1, cols], strips[:, 0, cols], bcast_ps[:, b % 2, :], ALU.mult).then_inc(s_norm, 1)
                if b:
                    cols = slice((b - 1) * QB, b * QB)
                    dve.wait_ge(s_ctx, b)
                    dve.scalar_tensor_tensor(out=dst[:, cols], in0=ctx_out[:, cols], scalar=gain, in1=base[:, cols],
                                             op0=ALU.mult, op1=ALU.add).then_inc(s_dst, 1)

        @block.scalar
        def _(act):
            act.wait_ge(s_bias, 1)
            for b in range(NB):
                act.wait_ge(s_out, b + 1)
                act.activation(ctx_out[:, b * QB:(b + 1) * QB], out_ps[:, b % 2, :], ACT.Identity, bias=bias[:, 0:1]).then_inc(s_ctx, 1)

        @block.tensor
        def _(pe):
            pe.matmul(bias_ps[:, 0:1], weights[:, :], v_bias, start=True, stop=True).then_inc(s_bias_ps, 1)
            pe.wait_ge(s_rows, 16)
            for b in range(NB + 1):
                if b < NB:
                    if b >= 2: pe.wait_ge(s_norm, b - 1)
                    pe.matmul(bcast_ps[:, b % 2, :], c.spread_heads[0:H, :], inverse_rows[:, b * QB:(b + 1) * QB],
                              start=True, stop=True).then_inc(s_bc, 1)
                if b:
                    pe.wait_ge(s_norm, b)
                    if b >= 3: pe.wait_ge(s_ctx, b - 2)
                    pe.matmul(out_ps[:, (b - 1) % 2, :], weights[:, :], strips[:, 1, (b - 1) * QB:b * QB],
                              start=True, stop=True).then_inc(s_out, 1)


def liquid(nc, tag, c, ctx_in, w_ctx, w_x, bias, xs, x2, dst):
    STEPS = 8
    with ExitStack() as ctx:
        sb = lambda n, s: ctx.enter_context(nc.sbuf_tensor(tag + n, s, F32))
        sem = c.semaphores.of(tag)
        drive = sb("drive", [P, S])
        change = sb("change", [P, 2, QB])
        u_ps = ctx.enter_context(nc.psum_tensor(tag + "u_ps", [P, NB, QB], F32))
        v_ps = ctx.enter_context(nc.psum_tensor(tag + "v_ps", [P, NB, QB], F32))
        s_drive_ps = sem("drive_product"); s_zero = sem("v_zeroed")
        s_pre = sem("before_tanh"); s_u = sem("u_ready"); s_change = sem("change_ready"); s_v = sem("v_ready"); s_xs = sem("xs_ready")
        block = ctx.enter_context(nc.Block())

        @block.tensor
        def _(pe):
            for b in range(NB):
                mm = pe.matmul(u_ps[:, b, :], w_ctx[:, :], ctx_in[:, b * QB:(b + 1) * QB], start=True, stop=True)
                mm.then_inc(s_drive_ps, 1)
            with pe.Fori(0, STEPS) as n:
                for b in range(NB):
                    cols = slice(b * QB, (b + 1) * QB)
                    pe.wait_ge(s_xs, n * NB + b + 1)
                    pe.matmul(u_ps[:, b, :], c.ident[:, :], drive[:, cols], start=True, stop=False)
                    pe.matmul(u_ps[:, b, :], w_x[:, :], xs[:, cols], start=False, stop=True).then_inc(s_pre, 1)

        @block.scalar
        def _(act):
            for b in range(NB):
                act.wait_ge(s_drive_ps, b + 1)
                act.activation(drive[:, b * QB:(b + 1) * QB], u_ps[:, b, :], ACT.Identity, bias=bias).then_inc(s_xs, 1)
            with act.Fori(0, STEPS) as n:
                for b in range(NB):
                    act.wait_ge(s_pre, n * NB + b + 1)
                    act.activation(u_ps[:, b, :], u_ps[:, b, :], ACT.Tanh).then_inc(s_u, 1)

        @block.vector
        def _(dve):
            dve.memset(v_ps[:, :, :], 0.0).then_inc(s_zero, 1)
            dve.wait_ge(s_zero, 1)
            with dve.Fori(0, STEPS) as n:
                for b in range(NB):
                    cols = slice(b * QB, (b + 1) * QB)
                    dve.wait_ge(s_u, n * NB + b + 1)
                    dve.tensor_tensor(change[:, b % 2, :], u_ps[:, b, :], xs[:, cols], ALU.subtract).then_inc(s_change, 1)
                    dve.wait_ge(s_change, n * NB + b + 1)
                    dve.scalar_tensor_tensor(out=v_ps[:, b, :], in0=v_ps[:, b, :], scalar=0.9, in1=change[:, b % 2, :],
                                             op0=ALU.mult, op1=ALU.add).then_inc(s_v, 1)
                    dve.wait_ge(s_v, n * NB + b + 1)
                    dve.scalar_tensor_tensor(out=xs[:, cols], in0=v_ps[:, b, :], scalar=0.01, in1=xs[:, cols],
                                             op0=ALU.mult, op1=ALU.add).then_inc(s_xs, 1)
            dve.wait_ge(s_xs, (STEPS + 1) * NB)
            dve.tensor_tensor(dst[:, :], x2[:, :], xs[:, :], ALU.add).then_inc(s_zero, 1)


def gelu_ffn(nc, tag, c, src, w1, b1, w2, b2, base, gain, x):
    F = 4
    with ExitStack() as ctx:
        sb = lambda n, s: ctx.enter_context(nc.sbuf_tensor(tag + n, s, F32))
        sem = c.semaphores.of(tag)
        hidden = sb("hidden", [P, 2 * F, QB])
        total = sb("total", [P, 2, QB])
        h_ps = ctx.enter_context(nc.psum_tensor(tag + "h_ps", [P, F, QB], F32))
        o_ps = ctx.enter_context(nc.psum_tensor(tag + "o_ps", [P, 2, QB], F32))
        s_h = sem("h_ready"); s_g = sem("gelu_ready"); s_o = sem("o_ready"); s_total = sem("total_ready"); s_x = sem("x_ready")
        block = ctx.enter_context(nc.Block())

        @block.tensor
        def _(pe):
            for b in range(NB + 1):
                if b < NB:
                    for f in range(F):
                        if b: pe.wait_ge(s_g, F * (b - 1) + f + 1)
                        pe.matmul(h_ps[:, f, :], w1[:, f * P:(f + 1) * P], src[:, b * QB:(b + 1) * QB],
                                  start=True, stop=True).then_inc(s_h, 1)
                if b:
                    n = b - 1
                    if n >= 2: pe.wait_ge(s_total, n - 1)
                    pe.wait_ge(s_g, F * b)
                    for f in range(F):
                        mm = pe.matmul(o_ps[:, n % 2, :], w2[:, f, :], hidden[:, n % 2 * F + f, :],
                                       start=(f == 0), stop=(f == F - 1))
                    mm.then_inc(s_o, 1)

        @block.scalar
        def _(act):
            for b in range(NB):
                if b >= 2: act.wait_ge(s_o, b - 1)
                for f in range(F):
                    act.wait_ge(s_h, F * b + f + 1)
                    act.activation(hidden[:, b % 2 * F + f, :], h_ps[:, f, :], ACT.Gelu, bias=b1(f)).then_inc(s_g, 1)

        @block.vector
        def _(dve):
            for b in range(NB):
                cols = slice(b * QB, (b + 1) * QB)
                dve.wait_ge(s_o, b + 1)
                dve.scalar_tensor_tensor(out=total[:, b % 2, :], in0=o_ps[:, b % 2, :], scalar=b2, in1=base[:, cols],
                                         op0=ALU.add, op1=ALU.add).then_inc(s_total, 1)
                dve.wait_ge(s_total, b + 1)
                dve.scalar_tensor_tensor(out=x[:, cols], in0=total[:, b % 2, :], scalar=gain, in1=x[:, cols],
                                         op0=ALU.mult, op1=ALU.add).then_inc(s_x, 1)


def top2_gates(nc, tag, c, src, gate_w, n_experts, rows, rows_bf=None, in_parts=False, token_gates=None):
    E = n_experts
    R = rows.shape[0]
    chosen = rows_bf is not None and not in_parts
    with ExitStack() as ctx:
        sb = lambda n, s, d=F32: ctx.enter_context(nc.sbuf_tensor(tag + n, s, d))
        sem = c.semaphores.of(tag)
        logits = sb("logits", [P, NT, E])
        best = sb("best", [P, NT, 8])
        index = sb("index", [P, NT, 8], U32)
        index_f = sb("index_f", [P, NT, 2])
        gap = sb("gap", [P, NT]); ratio = sb("ratio", [P, NT]); whole = sb("whole", [P, NT])
        gate = sb("gate", [P, NT, 2]) if token_gates is None else token_gates
        hot = sb("hot", [P, 2, NT, E])
        weighed = sb("weighed", [P, 2, NT, E])
        token = sb("token", [P, NT, R])
        total = sb("total", [P, NT, E]); rest = sb("rest", [P, NT, E]); part = sb("part", [P, 2, NT, E], BF16)
        logit_ps = ctx.enter_context(nc.psum_tensor(tag + "logit_ps", [P, NT, E], F32))
        turn_ps = ctx.enter_context(nc.psum_tensor(tag + "turn_ps", [P, 2, QB], F32))
        s_logit = sem("logits_ready"); s_step = sem("step"); s_gap = sem("gap_ready"); s_ratio = sem("ratio_ready")
        s_token = sem("token_rows_ready"); s_turn = sem("turned"); s_rows = sem("rows_ready")
        block = ctx.enter_context(nc.Block())

        @block.tensor
        def _(pe):
            for t in range(NT):
                mm = pe.matmul(logit_ps[:, t, :], src[:, t * P:(t + 1) * P], gate_w, start=True, stop=True)
            mm.then_inc(s_logit, 1)
            pe.wait_ge(s_token, 1)
            for b in range(NB):
                if b >= 2: pe.wait_ge(s_rows, b - 1)
                for k in range(4):
                    mm = pe.transpose(turn_ps[0:R, b % 2, k * P:(k + 1) * P], token[:, 4 * b + k, :], c.ident[:, :])
                mm.then_inc(s_turn, 1)

        @block.scalar
        def _(act):
            act.wait_ge(s_gap, 1)
            act.activation(ratio[:, :], gap[:, :], ACT.Exp).then_inc(s_ratio, 1)
            for b in range(NB):
                act.wait_ge(s_turn, b + 1)
                if rows_bf is not None: act.activation(rows_bf[:, b * QB:(b + 1) * QB], turn_ps[0:R, b % 2, :], ACT.Copy)
                act.activation(rows[:, b * QB:(b + 1) * QB], turn_ps[0:R, b % 2, :], ACT.Copy).then_inc(s_rows, 1)

        @block.vector
        def _(dve):
            done = [0]

            def link(ins):
                done[0] += 1
                ins.then_inc(s_step, 1)
                dve.wait_ge(s_step, done[0])

            dve.wait_ge(s_logit, 1)
            if chosen:
                dve.memset(token[:, :, :], 0.0).then_inc(s_step, 1)
                done[0] += 1
            link(dve.tensor_copy(logits[:, :, :], logit_ps[:, :, :]))
            for t in range(NT):
                ins = dve.max(best[:, t, :], logits[:, t, :])
            link(ins)
            for t in range(NT):
                ins = dve.max_index(index[:, t, :], best[:, t, :], logits[:, t, :])
            link(ins)
            dve.tensor_tensor(gap[:, :], best[:, :, 1], best[:, :, 0], ALU.subtract).then_inc(s_gap, 1)
            link(dve.tensor_copy(index_f[:, :, :], index[:, :, 0:2]))
            for k in range(2):
                ins = dve.tensor_tensor(hot[:, k, :, :], c.counting[:, 0:E].unsqueeze(1).to_broadcast([P, NT, E]),
                                        index_f[:, :, k].unsqueeze(2).to_broadcast([P, NT, E]), ALU.is_equal)
            link(ins)
            dve.wait_ge(s_ratio, 1)
            link(dve.tensor_scalar(whole[:, :], ratio[:, :], 1.0, None, ALU.add))
            link(dve.reciprocal(gate[:, :, 0], whole[:, :]))
            link(dve.tensor_tensor(gate[:, :, 1], ratio[:, :], gate[:, :, 0], ALU.mult))
            for k in range(2):
                ins = dve.tensor_tensor(weighed[:, k, :, :], hot[:, k, :, :],
                                        gate[:, :, k].unsqueeze(2).to_broadcast([P, NT, E]), ALU.mult)
            link(ins)
            if chosen:
                for k in range(2):
                    dve.tensor_copy(token[:, :, E * (1 + k):E * (2 + k)], hot[:, k, :, :])
                dve.tensor_copy(token[:, :, 3 * E:3 * E + 2], gate[:, :, :])
            if in_parts:
                link(dve.tensor_tensor(total[:, :, :], weighed[:, 0, :, :], weighed[:, 1, :, :], ALU.add))
                link(dve.tensor_copy(part[:, 0, :, :], total[:, :, :]))
                link(dve.tensor_tensor(rest[:, :, :], total[:, :, :], part[:, 0, :, :], ALU.subtract))
                link(dve.tensor_copy(part[:, 1, :, :], rest[:, :, :]))
                for k in range(2):
                    dve.tensor_copy(token[:, :, k * E:(k + 1) * E], part[:, k, :, :])
                dve.tensor_tensor(token[:, :, 2 * E:3 * E], rest[:, :, :], part[:, 1, :, :], ALU.subtract).then_inc(s_token, 1)
            else:
                dve.tensor_tensor(token[:, :, 0:E], weighed[:, 0, :, :], weighed[:, 1, :, :], ALU.add).then_inc(s_token, 1)


EA = 8


def moa_keys(nc, tag, c, src, k_w, k_bias, v_w, v_bias, rel, keys, values):
    with ExitStack() as ctx:
        sem = c.semaphores.of(tag)
        k_ps = ctx.enter_context(nc.psum_tensor(tag + "k_ps", [P, 2, QB], F32))
        v_ps = ctx.enter_context(nc.psum_tensor(tag + "v_ps", [P, 2, QB], F32))
        s_k = sem("k_ready"); s_copy = sem("k_copied"); s_v = sem("v_ready"); s_vcopy = sem("v_copied"); s_side = sem("sides_ready")
        block = ctx.enter_context(nc.Block())

        @block.tensor
        def _(pe):
            for b in range(NB):
                if b >= 2: pe.wait_ge(s_copy, b - 1)
                pe.matmul(k_ps[:, b % 2, :], k_w, src[:, b * QB:(b + 1) * QB], start=True, stop=True).then_inc(s_k, 1)
                if b >= 2: pe.wait_ge(s_vcopy, b - 1)
                for k in range(4):
                    t = 4 * b + k
                    mm = pe.matmul(v_ps[:, b % 2, k * D:(k + 1) * D], src[:, t * P:(t + 1) * P], v_w, start=True, stop=True)
                mm.then_inc(s_v, 1)

        @block.scalar
        def _(act):
            for b in range(NB):
                act.wait_ge(s_k, b + 1)
                act.activation(keys[:, 1, b * QB:(b + 1) * QB], k_ps[:, b % 2, :], ACT.Identity, bias=k_bias).then_inc(s_copy, 1)

        @block.vector
        def _(dve):
            for b in range(NB):
                cols = slice(b * QB, (b + 1) * QB)
                dve.wait_ge(s_copy, b + 1)
                dve.wait_ge(s_v, b + 1)
                dve.tensor_tensor(values[:, 4 * b:4 * b + 4, :], v_ps[:, b % 2, :].rearrange("p (t d) -> p t d", t=4),
                                  v_bias[:, :].unsqueeze(1).to_broadcast([P, 4, D]), ALU.add).then_inc(s_vcopy, 1)
                dve.tensor_scalar(keys[:, 0, cols], keys[:, 1, cols], rel[:, 0:1], None, ALU.add)
                dve.tensor_scalar(keys[:, 2, cols], keys[:, 1, cols], rel[:, 2 * P - 1:2 * P], None, ALU.add).then_inc(s_side, 1)


def moa_queries(nc, tag, c, src, q_w, q_bias, rows_bf, queries):
    with ExitStack() as ctx:
        sb = lambda n, s: ctx.enter_context(nc.sbuf_tensor(tag + n, s, F32))
        sem = c.semaphores.of(tag)
        all_q = sb("all_q", [P, 2, QB])
        q_ps = ctx.enter_context(nc.psum_tensor(tag + "q_ps", [P, 2, QB], F32))
        mask_ps = ctx.enter_context(nc.psum_tensor(tag + "mask_ps", [P, 4, QB], F32))
        s_q = sem("q_ready"); s_copy = sem("q_copied"); s_mask = sem("masks_ready"); s_pick = sem("picked")
        units = [(b, e) for b in range(NB) for e in range(EA)]
        block = ctx.enter_context(nc.Block())

        @block.tensor
        def _(pe):
            for i, (b, e) in enumerate(units):
                cols = slice(b * QB, (b + 1) * QB)
                if i >= 2: pe.wait_ge(s_copy, i - 1)
                pe.matmul(q_ps[:, i % 2, :], q_w[:, e, :], src[:, cols], start=True, stop=True).then_inc(s_q, 1)
                if i >= 2: pe.wait_ge(s_pick, 2 * (i - 1))
                for k in range(2):
                    mm = pe.matmul(mask_ps[:, i % 2 * 2 + k, :], c.pick_bf[0:32, EA * (1 + k) + e, :], rows_bf[:, cols], start=True, stop=True)
                mm.then_inc(s_mask, 1)

        @block.scalar
        def _(act):
            for i, (b, e) in enumerate(units):
                act.wait_ge(s_q, i + 1)
                if i >= 2: act.wait_ge(s_pick, 2 * (i - 1))
                act.activation(all_q[:, i % 2, :], q_ps[:, i % 2, :], ACT.Identity, scale=float(D) ** -0.5, bias=q_bias(e)).then_inc(s_copy, 1)

        @block.vector
        def _(dve):
            for i, (b, e) in enumerate(units):
                cols = slice(b * QB, (b + 1) * QB)
                dve.wait_ge(s_copy, i + 1)
                dve.wait_ge(s_mask, i + 1)
                for k in range(2):
                    if e == 0:
                        dve.tensor_tensor(queries[:, k, cols], all_q[:, i % 2, :], mask_ps[:, i % 2 * 2 + k, :], ALU.mult).then_inc(s_pick, 1)
                    else:
                        if k == 0: dve.wait_ge(s_pick, 2 * i)
                        dve.copy_predicated(queries[:, k, cols], mask_ps[:, i % 2 * 2 + k, :].bitcast(U32), all_q[:, i % 2, :]).then_inc(s_pick, 1)


NEAR = 64
WINDOW = P + 2 * NEAR


def moa_near_bias(nc, tag, c, rel, queries, near, band_dram):
    W = 2 * P
    TILES = 2 * NT
    BATCHES = TILES // 4
    with ExitStack() as ctx:
        sb = lambda n, s: ctx.enter_context(nc.sbuf_tensor(tag + n, s, F32))
        sem = c.semaphores.of(tag)
        band = sb("band", [P, 2, 4, W])
        far = sb("far", [P, TILES, 2])
        band_ps = ctx.enter_context(nc.psum_tensor(tag + "band_ps", [P, 4, QB], F32))
        s_band = sem("band_ready"); s_copy = sem("band_copied"); s_far = sem("far_copied")
        s_store = [sem(f"band_stored{b}") for b in range(BATCHES)]
        s_near = [sem(f"near_loaded{b}") for b in range(BATCHES)]
        s_zero = sem("corners_zeroed"); s_out = sem("near_ready")
        block = ctx.enter_context(nc.Block())

        @block.tensor
        def _(pe):
            for t in range(TILES):
                if t >= 4: pe.wait_ge(s_copy, t - 3)
                pe.matmul(band_ps[:, t % 4, 0:W], queries[:, t // NT, t % NT * P:(t % NT + 1) * P], rel,
                          start=True, stop=True).then_inc(s_band, 1)

        @block.scalar
        def _(act):
            for t in range(TILES):
                act.wait_ge(s_band, t + 1)
                if t % 4 == 0 and t >= 8:
                    act.wait_ge(s_store[t // 4 - 2], 16)
                    act.wait_ge(s_far, t - 4)
                act.activation(band[:, t // 4 % 2, t % 4, :], band_ps[:, t % 4, 0:W], ACT.Copy).then_inc(s_copy, 1)

        @block.sync
        def _(sp):
            def load(b):
                sp.wait_ge(s_store[b], 16)
                for half in range(2):
                    at = 4 * b * P * W + ((W - 1) * NEAR + P if half else P - NEAR)
                    src = bass.AP(band_dram.tensor, at, [[W - 1, NEAR], [P * W, 4], [1, P + NEAR]])
                    sp.dma_start(near[NEAR * half:NEAR * (half + 1), 4 * b:4 * b + 4, NEAR * half:NEAR * half + P + NEAR],
                                 src).then_inc(s_near[b], 16)
            for b in range(BATCHES):
                sp.wait_ge(s_copy, 4 * (b + 1))
                sp.dma_start(band_dram[4 * b:4 * b + 4].rearrange("t p w -> p t w"), band[:, b % 2, :, :]).then_inc(s_store[b], 16)
                if b: load(b - 1)
            load(BATCHES - 1)

        @block.gpsimd
        def _(pool):
            pool.memset(near[0:NEAR, :, P + NEAR:WINDOW], 0.0).then_inc(s_zero, 1)
            pool.wait_ge(s_zero, 1)
            pool.memset(near[NEAR:P, :, 0:NEAR], 0.0).then_inc(s_zero, 1)
            pool.wait_ge(s_zero, 2)

        def side(dve, b):
            dve.wait_ge(s_far, 4 * b + 4)
            dve.wait_ge(s_near[b], 32)
            for t in range(4 * b, 4 * b + 4):
                for rows, cols, k in ((slice(0, NEAR), slice(0, NEAR), 0), (slice(NEAR, P), slice(P + NEAR, WINDOW), 1)):
                    dve.tensor_scalar(near[rows, t, cols], near[rows, t, cols], far[rows, t, k:k + 1], None,
                                      ALU.subtract).then_inc(s_out, 1)

        @block.vector
        def _(dve):
            for t in range(TILES):
                dve.wait_ge(s_copy, t + 1)
                dve.tensor_copy(far[:, t, :], band[:, t // 4 % 2, t % 4, 0:W:W - 1]).then_inc(s_far, 1)
                if t >= 8 and t % 4 == 3: side(dve, t // 4 - 2)
            side(dve, BATCHES - 2)
            side(dve, BATCHES - 1)


def moa_attention(nc, tag, c, keys, values, queries, near, gates, out):
    TILES = 2 * NT
    C = S // QB
    with ExitStack() as ctx:
        sb = lambda n, s, d=F32: ctx.enter_context(nc.sbuf_tensor(tag + n, s, d))
        sem = c.semaphores.of(tag)
        ps = lambda n, s: ctx.enter_context(nc.psum_tensor(tag + n, s, F32))
        probs = sb("probs", [P, 2, S])
        turned = sb("turned", [P, C, QB])
        pmax = sb("pmax", [P, 2, C]); negmax = sb("negmax", [P, 2])
        sums = sb("sums", [P, 2, C]); total = sb("total", [P, 2]); weight = sb("weight", [P, 2])
        s_ps = ps("s_ps", [P, C, QB]); turn_ps = ps("turn_ps", [P, 2, QB]); acc = ps("acc", [P, 2, QB])
        s_scores = sem("scores_ready"); s_max = sem("piece_maxima"); s_neg = sem("negmax_ready"); s_exp = sem("probs_ready")
        s_step = sem("weight_steps"); s_scaled = sem("probs_scaled"); s_turn = sem("turned")
        s_copy_v = sem("turned_copied_by_vector"); s_copy_a = sem("turned_copied_by_scalar")
        s_pv = sem("pv_done"); s_out = sem("out_ready")
        block = ctx.enter_context(nc.Block())

        def kinds(t, k0, k1):
            cuts = [k0] + [x for x in (t * P, (t + 1) * P) if k0 < x < k1] + [k1]
            return [(0 if a < t * P else 1 if a < (t + 1) * P else 2, a, z) for a, z in zip(cuts, cuts[1:])]

        @block.tensor
        def _(pe):
            def scores(i, k):
                slot, t, k0 = i // NT, i % NT, k * QB
                if i: pe.wait_ge(s_exp, C * (i - 1) + k + 1)
                q = queries[:, slot, t * P:(t + 1) * P]
                for which, a, z in kinds(t, k0, k0 + QB):
                    mm = pe.matmul(s_ps[:, k, a - k0:z - k0], q, keys[:, which, a:z], start=(a == k0), stop=True, skip_group_check=True)
                lo, hi = max(k0, t * P - NEAR), min(k0 + QB, t * P + P + NEAR)
                if lo < hi:
                    w0 = lo - (t * P - NEAR)
                    mm = pe.matmul(s_ps[:, k, lo - k0:hi - k0], c.ident[:, :], near[:, i, w0:w0 + hi - lo],
                                   start=False, stop=True, skip_group_check=True)
                mm.then_inc(s_scores, 1)

            def turn(i, k):
                pe.wait_ge(s_scaled, C * i + k + 1)
                if k >= 2: pe.wait_ge(s_copy_v, 2 * i + k - 1)
                elif i: pe.wait_ge(s_copy_a, 2 * (i - 1) + k + 1)
                for j in range(4):
                    mm = pe.transpose(turn_ps[:, k % 2, j * P:(j + 1) * P], probs[:, i % 2, k * QB + j * P:k * QB + (j + 1) * P], c.ident[:, :])
                mm.then_inc(s_turn, 1)

            def pv(i, k):
                if k < 2: pe.wait_ge(s_copy_v, 2 * i + k + 1)
                else: pe.wait_ge(s_copy_a, 2 * i + k - 1)
                if k == 0 and i >= 2: pe.wait_ge(s_out, i - 1)
                for j in range(4):
                    mm = pe.matmul(acc[:, i % 2, 0:P], values[:, 4 * k + j, :], turned[:, k, j * P:(j + 1) * P],
                                   start=(k == 0 and j == 0), stop=(k == C - 1 and j == 3))
                mm.then_inc(s_pv, 1)

            for i in range(TILES + 1):
                for k in range(C - 1):
                    if i < TILES: scores(i, k)
                if i: turn(i - 1, 0); turn(i - 1, 1)
                if i < TILES: scores(i, C - 1)
                if i:
                    pv(i - 1, 0); turn(i - 1, 2)
                    pv(i - 1, 1); turn(i - 1, 3)
                    pv(i - 1, 2); pv(i - 1, 3)

        @block.vector
        def _(dve):
            def copy(i, k):
                dve.wait_ge(s_turn, C * i + k + 1)
                if i: dve.wait_ge(s_pv, C * (i - 1) + k + 1)
                dve.tensor_copy(turned[:, k, :], turn_ps[:, k % 2, :]).then_inc(s_copy_v, 1)

            for i in range(TILES + 1):
                if i < TILES:
                    for k in range(C):
                        if i and k == C - 1: copy(i - 1, 0); copy(i - 1, 1)
                        dve.wait_ge(s_scores, C * i + k + 1)
                        if i >= 2 and k == 0: dve.wait_ge(s_neg, i - 1)
                        dve.tensor_reduce(pmax[:, i % 2, k:k + 1], s_ps[:, k, :], AX.X, ALU.max).then_inc(s_max, 1)
                    dve.wait_ge(s_max, C * (i + 1))
                    dve.tensor_reduce(negmax[:, i % 2:i % 2 + 1], pmax[:, i % 2, :], AX.X, ALU.max, negate=True).then_inc(s_neg, 1)
                else:
                    copy(i - 1, 0); copy(i - 1, 1)
                if i < TILES:
                    dve.wait_ge(s_exp, C * (i + 1))
                    dve.tensor_reduce(total[:, i % 2:i % 2 + 1], sums[:, i % 2, :], AX.X, ALU.add).then_inc(s_step, 1)
                    dve.wait_ge(s_step, 3 * i + 1)
                    dve.reciprocal(total[:, i % 2:i % 2 + 1], total[:, i % 2:i % 2 + 1]).then_inc(s_step, 1)
                    dve.wait_ge(s_step, 3 * i + 2)
                    dve.tensor_tensor(weight[:, i % 2:i % 2 + 1], total[:, i % 2:i % 2 + 1], gates[:, i % NT, i // NT:i // NT + 1],
                                      ALU.mult).then_inc(s_step, 1)
                    dve.wait_ge(s_step, 3 * i + 3)
                    for k in range(C):
                        piece = probs[:, i % 2, k * QB:(k + 1) * QB]
                        dve.tensor_scalar(piece, piece, weight[:, i % 2:i % 2 + 1], None, ALU.mult).then_inc(s_scaled, 1)

        @block.scalar
        def _(act):
            def copy(i, k):
                act.wait_ge(s_turn, C * i + k + 1)
                if i: act.wait_ge(s_pv, C * (i - 1) + k + 1)
                act.activation(turned[:, k, :], turn_ps[:, k % 2, :], ACT.Copy).then_inc(s_copy_a, 1)

            for i in range(TILES + 1):
                if i < TILES:
                    act.wait_ge(s_neg, i + 1)
                    if i >= 2: act.wait_ge(s_turn, C * (i - 1))
                    for k in range(C):
                        if i and k in (1, 2): copy(i - 1, k + 1)
                        act.activation(probs[:, i % 2, k * QB:(k + 1) * QB], s_ps[:, k, :], ACT.Exp, bias=negmax[:, i % 2:i % 2 + 1],
                                       accum_out=sums[:, i % 2, k:k + 1]).then_inc(s_exp, 1)
                else:
                    copy(i - 1, 2); copy(i - 1, 3)
                if i:
                    act.wait_ge(s_pv, C * i)
                    act.activation(out[:, (i - 1) // NT, (i - 1) % NT * P:((i - 1) % NT + 1) * P], acc[:, (i - 1) % 2, 0:P], ACT.Copy).then_inc(s_out, 1)


def moa_out(nc, tag, c, heads, rows, rows_bf, o_w, o_bias_rows, base, dst):
    with ExitStack() as ctx:
        sb = lambda n, s: ctx.enter_context(nc.sbuf_tensor(tag + n, s, F32))
        sem = c.semaphores.of(tag)
        routed = sb("routed", [P, 2, QB])
        mask_ps = ctx.enter_context(nc.psum_tensor(tag + "mask_ps", [P, 4, QB], F32))
        o_ps = ctx.enter_context(nc.psum_tensor(tag + "o_ps", [P, 2, QB], F32))
        s_mask = sem("masks_ready"); s_first = sem("first_routed"); s_routed = sem("routed"); s_o = sem("o_ready"); s_used = sem("routed_used"); s_dst = sem("dst_ready")
        units = [(b, e) for b in range(NB) for e in range(EA)]
        block = ctx.enter_context(nc.Block())

        @block.tensor
        def _(pe):
            for i in range(len(units) + 1):
                if i < len(units):
                    b, e = units[i]
                    cols = slice(b * QB, (b + 1) * QB)
                    if i >= 2: pe.wait_ge(s_routed, i - 1)
                    for k in range(2):
                        mm = pe.matmul(mask_ps[:, i % 2 * 2 + k, :], c.pick_bf[0:32, EA * (1 + k) + e, :], rows_bf[:, cols], start=True, stop=True)
                    mm.then_inc(s_mask, 1)
                if i:
                    b, e = units[i - 1]
                    cols = slice(b * QB, (b + 1) * QB)
                    if e == 0:
                        if b >= 2: pe.wait_ge(s_dst, b - 1)
                        pe.matmul(o_ps[:, b % 2, :], o_bias_rows[:, :], rows[:, cols], start=True, stop=False)
                    pe.wait_ge(s_routed, i)
                    pe.matmul(o_ps[:, b % 2, :], o_w[:, e, :], routed[:, (i - 1) % 2, :], start=False, stop=(e == EA - 1)).then_inc(s_used, 1)

        def finish(dve, b):
            dve.wait_ge(s_used, EA * (b + 1))
            dve.tensor_tensor(dst[:, b * QB:(b + 1) * QB], base[:, b * QB:(b + 1) * QB], o_ps[:, b % 2, :], ALU.add).then_inc(s_dst, 1)

        @block.vector
        def _(dve):
            for i, (b, e) in enumerate(units):
                cols = slice(b * QB, (b + 1) * QB)
                dve.wait_ge(s_mask, i + 1)
                if i >= 2: dve.wait_ge(s_used, i - 1)
                dve.tensor_tensor(routed[:, i % 2, :], heads[:, 0, cols], mask_ps[:, i % 2 * 2, :], ALU.mult).then_inc(s_first, 1)
                dve.wait_ge(s_first, i + 1)
                dve.copy_predicated(routed[:, i % 2, :], mask_ps[:, i % 2 * 2 + 1, :].bitcast(U32), heads[:, 1, cols]).then_inc(s_routed, 1)
                if e == 1 and b: finish(dve, b - 1)
            finish(dve, NB - 1)



def moe_ffn(nc, tag, c, src, rows, rows_bf, w1, b1, w2, b2_rows, base, gain, x):
    PAIRS = 8
    with ExitStack() as ctx:
        sb = lambda n, s: ctx.enter_context(nc.sbuf_tensor(tag + n, s, F32))
        sem = c.semaphores.of(tag)
        hidden = sb("hidden", [P, 2, QB]); gated = sb("gated", [P, 2, QB]); total = sb("total", [P, 2, QB])
        h_ps = ctx.enter_context(nc.psum_tensor(tag + "h_ps", [P, 2, QB], F32))
        g_ps = ctx.enter_context(nc.psum_tensor(tag + "g_ps", [P, 2, QB], F32))
        o_ps = ctx.enter_context(nc.psum_tensor(tag + "o_ps", [P, 2, QB], F32))
        s_h = sem("h_ready"); s_relu = sem("relu_ready"); s_g = sem("gates_ready"); s_gated = sem("gated"); s_used = sem("gated_used")
        s_total = sem("total_ready"); s_x = sem("x_ready")
        units = [(b, e) for b in range(NB) for e in range(PAIRS)]
        block = ctx.enter_context(nc.Block())

        @block.tensor
        def _(pe):
            for i in range(len(units) + 1):
                if i < len(units):
                    b, e = units[i]
                    cols = slice(b * QB, (b + 1) * QB)
                    if i >= 2: pe.wait_ge(s_relu, i - 1)
                    pe.matmul(h_ps[:, i % 2, :], w1[:, e, :], src[:, cols], start=True, stop=True).then_inc(s_h, 1)
                    if i >= 2: pe.wait_ge(s_gated, i - 1)
                    pe.matmul(g_ps[:, i % 2, :], c.pick_pair[0:48, e, :], rows_bf[:, cols], start=True, stop=True).then_inc(s_g, 1)
                if i:
                    b, e = units[i - 1]
                    cols = slice(b * QB, (b + 1) * QB)
                    if e == 0:
                        if b >= 2: pe.wait_ge(s_total, b - 1)
                        pe.matmul(o_ps[:, b % 2, :], b2_rows[:, :], rows[:, cols], start=True, stop=False)
                    pe.wait_ge(s_gated, i)
                    pe.matmul(o_ps[:, b % 2, :], w2[:, e, :], gated[:, (i - 1) % 2, :], start=False, stop=(e == PAIRS - 1)).then_inc(s_used, 1)

        @block.scalar
        def _(act):
            for i, (b, e) in enumerate(units):
                act.wait_ge(s_h, i + 1)
                if i >= 2: act.wait_ge(s_gated, i - 1)
                act.activation(hidden[:, i % 2, :], h_ps[:, i % 2, :], ACT.Relu, bias=b1(e)).then_inc(s_relu, 1)

        def finish(dve, b):
            cols = slice(b * QB, (b + 1) * QB)
            dve.wait_ge(s_used, PAIRS * (b + 1))
            dve.tensor_tensor(total[:, b % 2, :], base[:, cols], o_ps[:, b % 2, :], ALU.add).then_inc(s_total, 1)
            dve.wait_ge(s_total, b + 1)
            dve.scalar_tensor_tensor(out=x[:, cols], in0=total[:, b % 2, :], scalar=gain, in1=x[:, cols],
                                     op0=ALU.mult, op1=ALU.add).then_inc(s_x, 1)

        @block.vector
        def _(dve):
            for i, (b, e) in enumerate(units):
                dve.wait_ge(s_relu, i + 1)
                dve.wait_ge(s_g, i + 1)
                if i >= 2: dve.wait_ge(s_used, i - 1)
                dve.tensor_tensor(gated[:, i % 2, :], hidden[:, i % 2, :], g_ps[:, i % 2, :], ALU.mult).then_inc(s_gated, 1)
                if e == 1 and b: finish(dve, b - 1)
            finish(dve, NB - 1)



def swiglu_experts(nc, tag, c, src, rows, rows_dram, w0, w1, wo, gain, x):
    E = 8
    F = 4
    with ExitStack() as ctx:
        sb = lambda n, s, d=F32: ctx.enter_context(nc.sbuf_tensor(tag + n, s, d))
        sem = c.semaphores.of(tag)
        ps = lambda n, s: ctx.enter_context(nc.psum_tensor(tag + n, s, F32))
        w_sb = sb("w_sb", [P, 2, 2, F * P]); wo_sb = sb("wo_sb", [P, 2, F, D])
        w_high = sb("w_high", [P, 2, 2, F * P], F32R); w_low = sb("w_low", [P, 2, 2, F * P], F32R)
        src_high = sb("src_high", [P, S], F32R); src_low = sb("src_low", [P, S], F32R)
        gates = sb("gates", [P, 2, S]); gated = sb("gated", [P, 2, QB])
        gated_high = sb("gated_high", [P, 2, QB], F32R); gated_low = sb("gated_low", [P, 2, QB], F32R)
        silu = sb("silu", [P, 4, QB]); hidden = sb("hidden", [P, 2 * F, QB]); zeros = sb("zeros", [P, QB])
        a_ps = ps("a_ps", [P, 2, QB]); b_ps = ps("b_ps", [P, 2, QB]); o_ps = ps("o_ps", [P, NB, QB])
        s_store = sem("gates_stored"); s_load = [sem(f"expert_loaded{i}") for i in range(2)]; s_zero = sem("zeroed")
        s_src_high = sem("src_high_ready"); s_src_low = sem("src_low_ready")
        s_w_high = sem("w_high_ready"); s_w_low = sem("w_low_ready")
        s_gated = sem("src_gated"); s_g_high = sem("gated_high_ready"); s_g_low = sem("gated_low_ready")
        s_a = sem("a_ready"); s_b = sem("b_ready"); s_silu = sem("silu_ready"); s_hidden = sem("hidden_ready")
        s_o = sem("o_ready"); s_x = sem("x_ready")
        UNITS = NB * F
        AHEAD = 2
        block = ctx.enter_context(nc.Block())

        def experts(engine, body):
            with engine.Fori(0, E // 2 - 1) as it: body(it, False)
            body(E // 2 - 1, True)

        @block.sync
        def _(sp):
            def load(e, u):
                one = lambda a: a[bass.ds(e, 1)]
                sp.dma_start(w_sb[:, u, 0, :], one(w0).rearrange("e d f -> (e d) f")).then_inc(s_load[u], 16)
                sp.dma_start(w_sb[:, u, 1, :], one(w1).rearrange("e d f -> (e d) f")).then_inc(s_load[u], 16)
                sp.dma_start(gates[:, u, :], one(rows_dram).rearrange("e s -> (e s)").partition_broadcast(P)).then_inc(s_load[u], 16)
                sp.dma_start(wo_sb[:, u, :, :], one(wo).rearrange("e (f p) d -> (e p) f d", p=P)).then_inc(s_load[u], 16)
            sp.dma_start(rows_dram, rows[0:E, :]).then_inc(s_store, 16)
            sp.wait_ge(s_store, 16)
            load(0, 0); load(1, 1)
            with sp.Fori(0, E // 2 - 1) as it:
                for u in range(2):
                    sp.wait_ge(s_o, it * 2 * NB + (u + 1) * NB)
                    load(it * 2 + (u + 2), u)

        @block.gpsimd
        def _(pool):
            pool.memset(zeros[:, :], 0.0).then_inc(s_zero, 1)

            def body(it, last):
                for u in range(2):
                    for b in range(NB):
                        cols = slice(b * QB, (b + 1) * QB)
                        n = it * 2 * NB + (u * NB + b)
                        if b == 0: pool.wait_ge(s_load[u], it * 64 + 64)
                        pool.wait_ge(s_g_low, n + (AHEAD - 1))
                        pool.tensor_tensor(gated[:, b % 2, :], src[:, cols], gates[:, u, cols], ALU.mult).then_inc(s_gated, 1)
            experts(pool, body)

        @block.tensor
        def _(pe):
            pe.wait_ge(s_zero, 1)
            for b in range(NB):
                pe.matmul(o_ps[:, b, :], zeros[:, 0:P], zeros[:, :], start=True, stop=True)
            pe.wait_ge(s_src_low, NB)

            def product(dst, w, high, low):
                pe.matmul(dst, w_high[w], high, start=True, stop=False)
                pe.matmul(dst, w_high[w], low, start=False, stop=False)
                return pe.matmul(dst, w_low[w], high, start=False, stop=True)

            def hidden_products(u, b, f, U):
                cols, mine = slice(b * QB, (b + 1) * QB), slice(f * P, (f + 1) * P)
                pe.wait_ge(s_silu, U + (AHEAD - 1))
                product(a_ps[:, f % 2, :], (slice(None), u, 0, mine), src_high[:, cols], src_low[:, cols]).then_inc(s_a, 1)
                pe.wait_ge(s_hidden, U + (AHEAD - 1))
                product(b_ps[:, f % 2, :], (slice(None), u, 1, mine), gated_high[:, b % 2, :], gated_low[:, b % 2, :]).then_inc(s_b, 1)

            def out_products(u, b, n):
                pe.wait_ge(s_hidden, n * F + (F + AHEAD))
                for f in range(F):
                    mm = pe.matmul(o_ps[:, b, :], wo_sb[:, u, f, :], hidden[:, b % 2 * F + f, :], start=False, stop=True, skip_group_check=True)
                mm.then_inc(s_o, 1)

            def body(it, last):
                for u in range(2):
                    pe.wait_ge(s_load[u], it * 64 + 64)
                    pe.wait_ge(s_w_low, it * 4 + 2 * (u + 1))
                    for b in range(NB):
                        n = it * 2 * NB + (u * NB + b)
                        pe.wait_ge(s_g_low, n + (1 + AHEAD))
                        for f in range(F): hidden_products(u, b, f, n * F + f)
                        if b: out_products(u, b - 1, n - 1)
                    out_products(u, NB - 1, n)
            experts(pe, body)

        @block.scalar
        def _(act):
            act.sem_inc(s_silu, AHEAD)

            def weights_high(u, loads):
                act.wait_ge(s_load[u], loads)
                for w in range(2):
                    act.activation(w_high[:, u, w, :], w_sb[:, u, w, :], ACT.Copy).then_inc(s_w_high, 1)

            def gated_high_part(n, parity):
                act.wait_ge(s_gated, n + 1)
                act.activation(gated_high[:, parity, :], gated[:, parity, :], ACT.Copy).then_inc(s_g_high, 1)

            for b in range(NB):
                act.activation(src_high[:, b * QB:(b + 1) * QB], src[:, b * QB:(b + 1) * QB], ACT.Copy).then_inc(s_src_high, 1)
            weights_high(0, 64)
            gated_high_part(0, 0)

            def body(it, last):
                for k in range(2 * UNITS):
                    u, b, f = k // UNITS, k // F % NB, k % F
                    act.wait_ge(s_a, it * 2 * UNITS + (k + 1))
                    act.activation(silu[:, k % 4, :], a_ps[:, k % 2, :], ACT.Silu).then_inc(s_silu, 1)
                    ends = last and u == 1
                    if f == 1 and not (ends and b == NB - 1): gated_high_part(it * 2 * NB + (u * NB + b + 1), (b + 1) % 2)
                    if f == 2 and b == 1 and not ends: weights_high(1 - u, it * 64 + 64 * (u + 1))
            experts(act, body)

        @block.vector
        def _(dve):
            dve.sem_inc(s_hidden, AHEAD)
            dve.sem_inc(s_g_low, AHEAD)

            def weights_low(u, n):
                for w in range(2):
                    dve.wait_ge(s_w_high, n + (w + 1))
                    dve.tensor_tensor(w_low[:, u, w, :], w_sb[:, u, w, :], w_high[:, u, w, :].bitcast(F32), ALU.subtract).then_inc(s_w_low, 1)

            def gated_low_part(n, parity):
                dve.wait_ge(s_g_high, n + 1)
                dve.tensor_tensor(gated_low[:, parity, :], gated[:, parity, :], gated_high[:, parity, :].bitcast(F32), ALU.subtract).then_inc(s_g_low, 1)

            for b in range(NB):
                cols = slice(b * QB, (b + 1) * QB)
                dve.wait_ge(s_src_high, b + 1)
                dve.tensor_tensor(src_low[:, cols], src[:, cols], src_high[:, cols].bitcast(F32), ALU.subtract).then_inc(s_src_low, 1)
            weights_low(0, 0)
            gated_low_part(0, 0)

            def body(it, last):
                for k in range(2 * UNITS):
                    u, b, f = k // UNITS, k // F % NB, k % F
                    U = it * 2 * UNITS + k
                    dve.wait_ge(s_silu, U + (1 + AHEAD))
                    dve.wait_ge(s_b, U + 1)
                    dve.tensor_tensor(hidden[:, b % 2 * F + f, :], silu[:, k % 4, :], b_ps[:, k % 2, :], ALU.mult).then_inc(s_hidden, 1)
                    ends = last and u == 1
                    if f == 1 and not (ends and b == NB - 1): gated_low_part(it * 2 * NB + (u * NB + b + 1), (b + 1) % 2)
                    if f == 2 and b == 1 and not ends: weights_low(1 - u, it * 4 + 2 * (u + 1))
            experts(dve, body)
            dve.wait_ge(s_o, E * NB)
            for b in range(NB):
                cols = slice(b * QB, (b + 1) * QB)
                dve.scalar_tensor_tensor(out=x[:, cols], in0=o_ps[:, b, :], scalar=gain, in1=x[:, cols],
                                         op0=ALU.mult, op1=ALU.add).then_inc(s_x, 1)


VECTORS = ["L0_c", "L1_c", "qkv_b", "out_b", "g_attn", "b_attn", "g1", "b1", "g2", "b2", "b_inl", "ff_b1", "ff_b2",
           "ln1_w", "ln1_b", "ln2_w", "ln2_b", "q_b", "k_b", "moe_b1", "L1_b_attn", "L1_b_proj"]
WIDTHS = {"qkv_b": 3, "ff_b1": 4, "q_b": 8, "moe_b1": 8, "L1_b_attn": 3}


def vector_columns():
    at, n = {}, 0
    for name in VECTORS:
        at[name] = n
        n += WIDTHS.get(name, 1)
    return at, n


CONST_F32 = [("ident", P), ("averages", P), ("ones", P), ("spread_heads", P), ("counting", 16),
             ("eps", 1), ("one", 1)]
CONST_BF16 = [("ident_bf", P), ("ones_bf", P), ("mask_q", P), ("mask_k", P), ("pick_bf", 24 * P), ("pick_pair", 8 * P)]


class Constants:

    def __init__(self, consts, consts_bf, semaphores):
        self.semaphores = semaphores
        cut = {}
        for names, tensor in ((CONST_F32, consts), (CONST_BF16, consts_bf)):
            n = 0
            for name, w in names:
                cut[name] = tensor[:, n:n + w]
                n += w
        self.ident, self.averages, self.ones = cut["ident"], cut["averages"], cut["ones"]
        self.spread_heads = cut["spread_heads"]
        self.counting, self.eps, self.one = cut["counting"], cut["eps"], cut["one"]
        self.pick_pair = cut["pick_pair"].rearrange("p (k m) -> p k m", m=P)
        self.ident_bf, self.ones_bf, self.mask_q, self.mask_k = cut["ident_bf"], cut["ones_bf"], cut["mask_q"], cut["mask_k"]
        self.pick_bf = cut["pick_bf"].rearrange("p (k m) -> p k m", m=P)


def modulation(nc, c, modulations, vectors, at, weights):
    with ExitStack() as ctx:
        sem = c.semaphores.of("mod_")
        silu = ctx.enter_context(nc.sbuf_tensor("mod_silu", [P, 2], F32))
        sign = ctx.enter_context(nc.sbuf_tensor("mod_sign", [P, 2, 2], F32))
        size = ctx.enter_context(nc.sbuf_tensor("mod_size", [P, 2, 2], F32))
        mod_ps = ctx.enter_context(nc.psum_tensor("mod_ps", [P, 2, 6], F32))
        s_silu = sem("silu_ready"); s_mod = sem("product"); s_step = sem("step")
        block = ctx.enter_context(nc.Block())

        @block.scalar
        def _(act):
            act.activation(silu[:, :], vectors[:, at["L0_c"]:at["L1_c"] + 1], ACT.Silu).then_inc(s_silu, 1)

        @block.tensor
        def _(pe):
            pe.wait_ge(s_silu, 1)
            for layer in range(2):
                for i in range(6):
                    mm = pe.matmul(mod_ps[:, layer, i:i + 1], weights[:, layer, i * P:(i + 1) * P], silu[:, layer:layer + 1],
                                   start=True, stop=True)
            mm.then_inc(s_mod, 1)

        @block.vector
        def _(dve):
            dve.wait_ge(s_mod, 1)
            dve.tensor_copy(modulations[:, :, :], mod_ps[:, :, :]).then_inc(s_step, 1)
            dve.wait_ge(s_step, 1)
            gates = modulations[:, :, 2:6:3]
            dve.tensor_scalar(modulations[:, :, 1:5:3], mod_ps[:, :, 1:5:3], 1.0, None, ALU.add)
            dve.tensor_scalar(sign[:, :, :], gates, 0.0, 2.0, ALU.is_ge, ALU.mult).then_inc(s_step, 1)
            dve.wait_ge(s_step, 2)
            dve.scalar_tensor_tensor(out=size[:, :, :], in0=sign[:, :, :], scalar=-1.0, in1=gates, op0=ALU.add, op1=ALU.mult).then_inc(s_step, 1)
            dve.wait_ge(s_step, 3)
            dve.tensor_scalar(size[:, :, :], size[:, :, :], 0.25, None, ALU.max).then_inc(s_step, 1)
            dve.wait_ge(s_step, 4)
            dve.scalar_tensor_tensor(out=gates, in0=sign[:, :, :], scalar=-1.0, in1=size[:, :, :], op0=ALU.add, op1=ALU.mult)


def adaln_kernel(nc, ins, out):
    at, n_vec = vector_columns()
    with ExitStack() as ctx:
        sb = lambda n, s, d=F32: ctx.enter_context(nc.sbuf_tensor(n, s, d))
        dram = lambda n, s, d=F32: nc.dram_tensor(n, s, d, kind="Internal").ap()
        x = sb("x", [P, S])
        vectors = sb("vectors", [P, n_vec])
        consts = sb("consts", [P, sum(w for _, w in CONST_F32)])
        consts_bf = sb("consts_bf", [P, sum(w for _, w in CONST_BF16)], BF16)
        w_mod = sb("w_mod", [P, 2, 6 * D])
        w_qkv = sb("w_qkv", [P, 2, 3 * D])
        w_out = sb("w_out", [P, 2, D])
        w_ctx = sb("w_ctx", [P, D]); w_x = sb("w_x", [P, D])
        ff_w1 = sb("ff_w1", [P, 4 * P]); ff_w2 = sb("ff_w2", [P, 4, D])
        modulations = sb("modulations", [P, 2, 6]); gate_w1 = sb("gate_w1", [P, 8])
        s_load = ctx.enter_context(nc.semaphore("inputs_loaded"))
        s_later = ctx.enter_context(nc.semaphore("later_inputs_loaded"))
        s_store = ctx.enter_context(nc.semaphore("output_stored"))
        q_rows = dram("q_rows", [H, NROW, S], BF16); k_rows = dram("k_rows", [H, NROW, S], BF16)
        o_dram = dram("o_parts", [H, 4, HD + 1, S]); rden_dram = dram("inverse_sums", [H, S])
        band_dram = dram("band", [2 * NT, P, 2 * P]); gates_dram = dram("gate_rows", [8, S])

        c = Constants(consts, consts_bf, Semaphores(nc))

        def vec(name, k=0): return vectors[:, at[name] + k:at[name] + k + 1]
        def mod(layer, i): return modulations[:, layer, i:i + 1]

        def start_loads(sp, loads, signal):
            for dst, src in loads: sp.dma_start(dst, src).then_inc(signal, 16)

        first = [(vectors[:, :], ins["vectors"]), (w_mod[:, 0, :], ins["L0_wmod"]), (w_mod[:, 1, :], ins["L1_wmod"]),
                 (consts[:, :], ins["consts"]), (x[:, :], ins["x"])]
        later = [(w_qkv[:, 0, :], ins["L0_attn_qkv_w"]), (w_qkv[:, 1, :], ins["L1_attn_W_attn"]),
                 (consts_bf[:, :], ins["consts_bf"].bitcast(BF16)),
                 (w_out[:, 0, :], ins["L0_attn_out_w"]), (w_out[:, 1, :], ins["L1_attn_W_proj"]),
                 (w_ctx[:, :], ins["L0_attn_w_ctx"]), (w_x[:, :], ins["L0_attn_w_x"]), (ff_w1[:, :], ins["L0_attn_ff_w1"]),
                 (ff_w2[:, :, :], ins["L0_attn_ff_w2"].rearrange("(f p) d -> p f d", p=P)), (gate_w1[:, :], ins["L1_ffn_gate_kernel"])]
        with nc.Block() as block:
            @block.sync
            def _(sp):
                start_loads(sp, first, s_load)
                start_loads(sp, later, s_later)
                sp.wait_ge(s_load, 16 * len(first))

        def await_loads(signal, loads):
            with nc.Block() as block:
                @block.sync
                def _(sp):
                    sp.wait_ge(signal, 16 * len(loads))

        modulation(nc, c, modulations, vectors, at, w_mod)

        def dump(t):
            with nc.Block() as block:
                @block.sync
                def _(sp):
                    sp.dma_start(out, t).then_inc(s_store, 16)
                    sp.wait_ge(s_store, 16)

        def causal_attention(layer, src, q_bias, k_bias, v_bias, out_bias, ctx_out, gain, base, dst):
            with ExitStack() as own:
                strips = own.enter_context(nc.sbuf_tensor(f"strips{layer}", [P, 4, S], F32))
                sums = own.enter_context(nc.sbuf_tensor(f"sums{layer}", [P, 4, S // 8], F32))
                v_all = own.enter_context(nc.sbuf_tensor(f"v_all{layer}", [P, NT, D], F32))
                qkv(nc, f"qkv{layer}_", c, src, w_qkv[:, layer, :], q_bias, k_bias, v_all, q_rows, k_rows)
                consts_of = lambda name: (lambda n: ins[name].bitcast(BF16)[bass.ds(n, 1)].rearrange("o r s -> (o r) s")) if layer else (lambda n: ins[name].bitcast(BF16))
                attention(nc, f"att{layer}_", c, q_rows, k_rows, consts_of(f"q_const{layer}"), consts_of(f"k_const{layer}"),
                          v_all, c.ident_bf, c.mask_q, c.mask_k, o_dram, strips, sums)
                attention_out(nc, f"out{layer}_", c, o_dram, strips, sums, rden_dram, w_out[:, layer, :], v_bias, out_bias, ctx_out, gain, base, dst)

        with ExitStack() as own:
            t = lambda n: own.enter_context(nc.sbuf_tensor(n, [P, S], F32))
            h, normed, attended = t("h0"), t("normed0"), t("attended0")
            layer_norms(nc, "ln0_", c, [(x, h, mod(0, 1), mod(0, 0)), (h, normed, vec("g_attn"), vec("b_attn"))])
            await_loads(s_later, later)
            causal_attention(0, normed, vec("qkv_b", 0), vec("qkv_b", 1), vec("qkv_b", 2), vec("out_b"), attended, c.one, h, h)
            layer_norms(nc, "ln1_", c, [(h, normed, vec("g1"), vec("b1"))])
            liquid(nc, "liq_", c, attended, w_ctx, w_x, vec("b_inl"), normed, h, h)
            layer_norms(nc, "ln2_", c, [(h, normed, vec("g2"), vec("b2"))])
            gelu_ffn(nc, "ffn_", c, normed, ff_w1, lambda f: vec("ff_b1", f), ff_w2, vec("ff_b2"), h, mod(0, 2), x)

        c.semaphores.end_section()
        with ExitStack() as own:
            t = lambda n, s=[P, S], d=F32: own.enter_context(nc.sbuf_tensor(n, s, d))
            h, normed = t("h1"), t("normed1")
            rows = t("moa_rows", [32, S]); rows_bf = t("moa_rows_bf", [32, S], BF16); moe_rows = t("moe_rows", [48, S]); moe_rows_bf = t("moe_rows_bf", [48, S], BF16)
            moe_w1 = t("moe_w1", [P, 8, P]); moe_w2 = t("moe_w2", [P, 8, D]); moe_b2 = t("moe_b2", [48, D]); moe_gate = t("moe_gate", [P, 16])
            with ExitStack() as inner:
                u = lambda n, s: inner.enter_context(nc.sbuf_tensor(n, s, F32))
                gate_w = u("gate_w", [P, EA]); q_w = u("q_w", [P, EA, D]); kv_w = u("kv_w", [P, 2, D]); rel = u("rel", [P, 2 * P])
                o_w = u("o_w", [P, EA, D]); o_b = u("o_b", [32, D])
                token_gates = u("token_gates", [P, NT, 2]); v_bias = u("v_bias", [P, D])
                keys = u("keys", [P, 3, S]); values = u("values", [P, NT, D]); queries = u("queries", [P, 2, S])
                loads = []
                with nc.Block() as block:
                    s_w = c.semaphores.of("moa_")("weights_loaded")
                    s_z = c.semaphores.of("moa_")("o_b_zeroed")
                    @block.gpsimd
                    def _(pool):
                        pool.memset(o_b[:, :], 0.0).then_inc(s_z, 1)
                    @block.sync
                    def _(sp):
                        sp.wait_ge(s_z, 1)
                        loads[:] = [(gate_w[:, :], ins["L0_ffn_attn_gate_w"]), (q_w[:, :, :], ins["L0_ffn_q_w"].rearrange("e d h -> d e h")),
                                 (kv_w[:, 0, :], ins["L0_ffn_k_w"]), (kv_w[:, 1, :], ins["L0_ffn_v_w"]), (rel[:, :], ins["rel"]),
                                 (v_bias[:, :], ins["L0_ffn_v_b"].partition_broadcast(P)),
                                 (o_w[:, :, :], ins["L0_ffn_o_w"].rearrange("e h d -> h e d")), (o_b[0:EA, :], ins["L0_ffn_o_b"]),
                                 (moe_w1[:, :, :].rearrange("p e (t f) -> p (e t) f", t=2), ins["L0_ffn_ff_w1"].rearrange("e d f -> d e f")),
                                 (moe_w2[:, :, :], ins["L0_ffn_ff_w2"].rearrange("(e t) f d -> (t f) e d", t=2)),
                                 *((moe_b2[16 * k:16 * k + 16, :], ins["L0_ffn_ff_b2"]) for k in range(3)), (moe_gate[:, :], ins["L0_ffn_ff_gate_w"])]
                        start_loads(sp, loads, s_w)
                layer_norms(nc, "ln3_", c, [(x, h, mod(0, 4), mod(0, 3)), (h, normed, vec("ln1_w"), vec("ln1_b"))])
                await_loads(s_w, loads)
                top2_gates(nc, "g1_", c, normed, gate_w[:, :], EA, rows, rows_bf, token_gates=token_gates)
                moa_keys(nc, "keys_", c, normed, kv_w[:, 0, :], vec("k_b"), kv_w[:, 1, :], v_bias, rel, keys, values)
                scaled_q_bias = u("scaled_q_bias", [P, EA])
                with nc.Block() as block:
                    @block.vector
                    def _(dve):
                        dve.tensor_scalar(scaled_q_bias[:, :], vectors[:, at["q_b"]:at["q_b"] + EA], float(D) ** -0.5, None, ALU.mult)
                moa_queries(nc, "queries_", c, normed, q_w, lambda e: scaled_q_bias[:, e:e + 1], rows_bf, queries)
                with ExitStack() as deep:
                    near = deep.enter_context(nc.sbuf_tensor("near", [P, 2 * NT, WINDOW], F32))
                    moa_near_bias(nc, "near_", c, rel[:, :], queries, near, band_dram)
                    moa_attention(nc, "moa_", c, keys, values, queries, near, token_gates, queries)
                moa_out(nc, "mo_", c, queries, rows, rows_bf, o_w, o_b, h, h)
            layer_norms(nc, "ln4_", c, [(h, normed, vec("ln2_w"), vec("ln2_b"))])
            top2_gates(nc, "g2_", c, normed, moe_gate[:, :], 16, moe_rows, moe_rows_bf, in_parts=True)
            moe_ffn(nc, "moe_", c, normed, moe_rows, moe_rows_bf, moe_w1, lambda e: vec("moe_b1", e), moe_w2, moe_b2, h, mod(0, 5), x)

        c.semaphores.end_section()
        with ExitStack() as own:
            t = lambda n, s=[P, S], d=F32: own.enter_context(nc.sbuf_tensor(n, s, d))
            h, attended = t("h2"), t("attended1")
            layer_norms(nc, "ln5_", c, [(x, h, mod(1, 1), mod(1, 0))])
            causal_attention(1, h, vec("L1_b_attn", 0), vec("L1_b_attn", 1), vec("L1_b_attn", 2), vec("L1_b_proj"), attended, mod(1, 2), x, x)
            gates = t("expert_gates", [8, S])
            layer_norms(nc, "ln6_", c, [(x, h, mod(1, 4), mod(1, 3))])
            top2_gates(nc, "g3_", c, h, gate_w1[:, :], 8, gates)
            swiglu_experts(nc, "exp_", c, h, gates, gates_dram, ins["L1_ffn_w0"], ins["L1_ffn_w1"], ins["L1_ffn_wo"], mod(1, 5), x)
        c.semaphores.end_section()
        dump(x[:, :])


def host_constants():
    f = {name: np.zeros((P, w), np.float32) for name, w in CONST_F32}
    f["ident"][:] = np.eye(P)
    f["averages"][:] = 1.0 / P
    f["ones"][:] = 1.0
    for h in range(H): f["spread_heads"][h, h * HD:(h + 1) * HD] = 1.0
    f["counting"][:] = np.arange(16)
    f["eps"][:] = EPS
    f["one"][:] = 1.0
    b = {name: np.zeros((P, w), np.float32) for name, w in CONST_BF16}
    b["ident_bf"][:] = np.eye(P)
    b["ones_bf"][:] = 1.0
    i = np.arange(P)
    b["mask_q"][:] = np.where(i[None, :] > i[:, None], NEG, 0)
    b["mask_k"][:] = np.where(i[None, :] < i[:, None], NEG, 0)
    for e in range(8):
        for k in range(2): b["pick_pair"][2 * e + k:48:16, e * P + k * 64:e * P + (k + 1) * 64] = 1.0
    for r in range(24): b["pick_bf"][r, r * P:(r + 1) * P] = 1.0
    pos = np.arange(S)
    slopes = 2.0 ** -np.arange(1, H + 1)
    q1, k1 = np.zeros((2, H, CROWS, S), np.float32)
    high, low = pos // 256 * 256, pos % 256
    q1[:, 0:2] = 1.0
    k1[:, 0], k1[:, 1] = slopes[:, None] * high, slopes[:, None] * low
    q1[:, 2], q1[:, 3] = -slopes[:, None] * high, -slopes[:, None] * low
    k1[:, 2:4] = 1.0
    k1[:, MROW - NROW:MROW - NROW + 2] = 1.0
    q0, k0 = np.zeros((2, CROWS, S), np.float32)
    k0[MROW - NROW:MROW - NROW + 2] = 1.0
    bits = lambda a: (np.ascontiguousarray(a).view(np.uint32) >> 16).astype(np.uint16)
    return {"consts": np.concatenate([f[n] for n, _ in CONST_F32], 1),
            "consts_bf": bits(np.concatenate([b[n] for n, _ in CONST_BF16], 1)),
            "q_const0": bits(q0), "k_const0": bits(k0), "q_const1": bits(q1), "k_const1": bits(k1)}


AS_THEY_ARE = ["L0_wmod", "L1_wmod", "L0_attn_qkv_w", "L1_attn_W_attn", "L0_attn_out_w", "L1_attn_W_proj", "L0_attn_w_ctx",
               "L0_attn_w_x", "L0_attn_ff_w1", "L0_attn_ff_w2", "L0_ffn_attn_gate_w", "L0_ffn_q_w", "L0_ffn_k_w", "L0_ffn_v_w",
               "L0_ffn_v_b", "L0_ffn_o_w", "L0_ffn_o_b", "L0_ffn_ff_w1", "L0_ffn_ff_w2", "L0_ffn_ff_b2", "L0_ffn_ff_gate_w",
               "L1_ffn_gate_kernel", "L1_ffn_w0", "L1_ffn_w1", "L1_ffn_wo"]
SOURCES = {"L0_c": "L0_c", "L1_c": "L1_c", "q_b": "L0_ffn_q_b", "k_b": "L0_ffn_k_b",
           "moe_b1": "L0_ffn_ff_b1", "ln1_w": "L0_ffn_ln1_w", "ln1_b": "L0_ffn_ln1_b", "ln2_w": "L0_ffn_ln2_w",
           "ln2_b": "L0_ffn_ln2_b", "L1_b_attn": "L1_attn_b_attn", "L1_b_proj": "L1_attn_b_proj"}


def lay_out(inputs):
    a = {name: np.ascontiguousarray(inputs[name]) for name in AS_THEY_ARE}
    a["x"] = np.ascontiguousarray(np.asarray(inputs["L0_attn_x"])[0].T)
    columns = []
    for name in VECTORS:
        v = np.asarray(inputs[SOURCES.get(name, "L0_attn_" + name)])
        columns.append(v.reshape(WIDTHS.get(name, 1), P).T)
    a["vectors"] = np.ascontiguousarray(np.concatenate(columns, 1))
    rel = np.asarray(inputs["L0_ffn_rel_table"])
    a["rel"] = np.ascontiguousarray(rel[np.clip(np.arange(-P, P), -NEAR, NEAR) + NEAR].T)
    a.update(host_constants())
    return a


def kernel(**inputs):
    import concourse.bacc as bacc
    from concourse.bass_utils import run_bass_kernel_spmd

    nc = bacc.Bacc("TRN2", target_bir_lowering=False, num_devices=1)
    arrays = lay_out(inputs)
    ins = {n: nc.dram_tensor("in_" + n, a.shape, mybir.dt.from_np(a.dtype), kind="ExternalInput").ap() for n, a in arrays.items()}
    out = nc.dram_tensor("out_0_dram", (P, S), F32, kind="ExternalOutput").ap()
    adaln_kernel(nc, ins, out)
    r = run_bass_kernel_spmd(nc, [{"in_" + n: a for n, a in arrays.items()}], core_ids=[0])
    return np.ascontiguousarray(r.results[0]["out_0_dram"].T)[None]
```
